# Optimizing a Trainium2 kernel written in Bass

```python
import numpy as np
import jax
import jax.numpy as jnp

def _softmax(x, axis=-1):
    return jax.nn.softmax(x, axis=axis)

def _gelu(x):
    return jax.nn.gelu(x, approximate=True)

def _silu(x):
    return jax.nn.silu(x)

def _sigmoid(x):
    return jax.nn.sigmoid(x)

def _layernorm(x, axis=-1, eps=1e-05):
    m = jnp.mean(x, axis=axis, keepdims=True)
    v = jnp.var(x, axis=axis, keepdims=True)
    return (x - m) / jnp.sqrt(v + eps)

def _scatter_add(tgt, idx, src, axis=0):
    return tgt.at[idx].add(src)

def _segment_sum(src, seg, n):
    return jax.ops.segment_sum(src, seg, n)
kernel_name = 'mk_perceiver_d1_seqx_r8_755cec'

def setup_inputs(seed: int=0):
    np.random.seed(seed)
    _w = jnp.asarray

    def _rec_inputs():
        import jax
        import jax.numpy as jnp
        _rk = jax.random.key(seed)
        x = -0.0005207 + 1.001 * jax.random.normal(jax.random.fold_in(_rk, 1), (16, 64, 512), jnp.float32)
        _lenS = 64 - jax.random.randint(jax.random.fold_in(_rk, 7), (16,), 0, max(1, 64 // 4) + 1, jnp.int32)
        _lenS2 = 128 - jax.random.randint(jax.random.fold_in(_rk, 8), (16,), 0, max(1, 128 // 4) + 1, jnp.int32)
        _ctx_4096P = jax.random.normal(jax.random.fold_in(_rk, 11), (16, 16, 512), jnp.float32)
        _ctx_4096c = jax.random.dirichlet(jax.random.fold_in(_rk, 511), 0.3 * jnp.ones((16,), jnp.float32), (16, 128))
        _ctx_4096t = jnp.einsum('bsk,bkd->bsd', _ctx_4096c, _ctx_4096P)
        _ctx_4096t = _ctx_4096t * jax.lax.rsqrt(jnp.mean(jnp.square(_ctx_4096t)) + 1e-12) * 0.953939
        ctx_4096 = -0.00010331 + 0.999899 * (_ctx_4096t + 0.3 * jax.random.normal(jax.random.fold_in(_rk, 611), (16, 128, 512), jnp.float32))
        return (x, ctx_4096)
    x, ctx_4096 = _rec_inputs()

    def _L0_xattn_setup():
        import jax, jax.numpy as jnp
        import numpy as np
        import math
        HIDDEN = 512
        N_HEADS = 32
        HEAD_DIM = 128
        N_KV_HEADS = 4
        N_GROUPS = N_HEADS // N_KV_HEADS
        key = jax.random.key(seed)
        ks = jax.random.split(key, 6)
        B, NL, S = (8, 64, 512)
        latents = jax.random.normal(ks[0], (B, NL, HIDDEN), dtype=jnp.float32)
        context = jax.random.normal(ks[1], (B, S, HIDDEN), dtype=jnp.float32)
        scale = 1.0 / math.sqrt(HIDDEN)
        Wq = jax.random.normal(ks[2], (HIDDEN, N_HEADS * HEAD_DIM), dtype=jnp.float32) * scale
        Wk = jax.random.normal(ks[3], (HIDDEN, N_KV_HEADS * HEAD_DIM), dtype=jnp.float32) * scale
        Wv = jax.random.normal(ks[4], (HIDDEN, N_KV_HEADS * HEAD_DIM), dtype=jnp.float32) * scale
        Wo = jax.random.normal(ks[5], (N_HEADS * HEAD_DIM, HIDDEN), dtype=jnp.float32) * scale
        return {'latents': latents, 'context': context, 'Wq': Wq, 'Wk': Wk, 'Wv': Wv, 'Wo': Wo}
    _L0_xattn_all = _L0_xattn_setup()
    _L0_xattn_in = {k: v for k, v in _L0_xattn_all.items() if k in ('Wq', 'Wk', 'Wv', 'Wo')}
    del _L0_xattn_all

    def _L0_attn_setup():
        import jax, jax.numpy as jnp
        import numpy as np
        B, S, D = (2, 256, 512)
        H = 32
        HD = D // H
        THETA = 10000.0

        def _rope_cos_sin(seq_len, head_dim, theta=THETA):
            inv = 1.0 / theta ** (np.arange(0, head_dim, 2)[:head_dim // 2].astype(np.float32) / head_dim)
            t = np.arange(seq_len)
            f = np.outer(t, inv).astype(np.float32)
            return (jnp.asarray(np.cos(f)), jnp.asarray(np.sin(f)))

        def _apply_rotary(x, cos, sin):
            xr = x.astype(jnp.float32).reshape(*x.shape[:-1], HD // 2, 2)
            x0, x1 = (xr[..., 0], xr[..., 1])
            c = cos[None, :, None, :]
            s = sin[None, :, None, :]
            o0 = x0 * c - x1 * s
            o1 = x0 * s + x1 * c
            return jnp.stack((o0, o1), axis=-1).reshape(*x.shape[:-1], HD)
        key = jax.random.key(seed)
        ks = jax.random.split(key, 5)
        std = 0.02
        return {'x': jax.random.normal(ks[0], (B, S, D), dtype=jnp.float32), 'wq': jax.random.normal(ks[1], (D, D), dtype=jnp.float32) * std, 'wk': jax.random.normal(ks[2], (D, D), dtype=jnp.float32) * std, 'wv': jax.random.normal(ks[3], (D, D), dtype=jnp.float32) * std, 'wo': jax.random.normal(ks[4], (D, D), dtype=jnp.float32) * std}
    _L0_attn_all = _L0_attn_setup()
    _L0_attn_in = {k: v for k, v in _L0_attn_all.items() if k in ('wq', 'wk', 'wv', 'wo')}
    del _L0_attn_all

    def _L0_ffn_setup():
        import jax, jax.numpy as jnp
        import numpy as np
        K_TOP = 8
        key = jax.random.key(seed)
        k1, k2, k3 = jax.random.split(key, 3)
        B, S, H, E = (4, 512, 512, 64)
        hidden_states = jax.random.normal(k1, (B, S, H), dtype=jnp.float32)
        router_weight = jax.random.normal(k2, (E, H), dtype=jnp.float32)
        router_bias = jnp.zeros((E,), dtype=jnp.float32)
        expert_bias = jax.random.normal(k3, (E, H), dtype=jnp.float32) * 0.1
        return {'hidden_states': hidden_states, 'router_weight': router_weight, 'router_bias': router_bias, 'expert_bias': expert_bias}
    _L0_ffn_all = _L0_ffn_setup()
    _L0_ffn_in = {k: v for k, v in _L0_ffn_all.items() if k in ('router_weight', 'router_bias', 'expert_bias')}
    del _L0_ffn_all
    return {'x': x, 'ctx_4096': ctx_4096, 'L0_xattn_Wq': _L0_xattn_in['Wq'], 'L0_xattn_Wk': _L0_xattn_in['Wk'], 'L0_xattn_Wv': _L0_xattn_in['Wv'], 'L0_xattn_Wo': _L0_xattn_in['Wo'], 'L0_attn_wq': _L0_attn_in['wq'], 'L0_attn_wk': _L0_attn_in['wk'], 'L0_attn_wv': _L0_attn_in['wv'], 'L0_attn_wo': _L0_attn_in['wo'], 'L0_ffn_router_weight': _L0_ffn_in['router_weight'], 'L0_ffn_router_bias': _L0_ffn_in['router_bias'], 'L0_ffn_expert_bias': _L0_ffn_in['expert_bias']}

def reference(x, ctx_4096, L0_xattn_Wq, L0_xattn_Wk, L0_xattn_Wv, L0_xattn_Wo, L0_attn_wq, L0_attn_wk, L0_attn_wv, L0_attn_wo, L0_ffn_router_weight, L0_ffn_router_bias, L0_ffn_expert_bias):
    import jax
    import jax.numpy as jnp

    def _L0_xattn_ref(latents, context, Wq, Wk, Wv, Wo):
        import jax, jax.numpy as jnp
        import numpy as np
        import math
        HIDDEN = 512
        N_HEADS = 32
        HEAD_DIM = 128
        N_KV_HEADS = 4
        N_GROUPS = N_HEADS // N_KV_HEADS
        b, q_len, _ = latents.shape
        kv_len = q_len + context.shape[1]
        hidden_states = jnp.concatenate([context, latents], axis=1)
        q = (latents @ Wq).reshape(b, q_len, N_KV_HEADS, N_GROUPS, HEAD_DIM)
        k = (hidden_states @ Wk).reshape(b, kv_len, N_KV_HEADS, HEAD_DIM)
        v = (hidden_states @ Wv).reshape(b, kv_len, N_KV_HEADS, HEAD_DIM)
        scale = 1.0 / math.sqrt(HEAD_DIM)
        scores = jnp.einsum('bqhgd,bkhd->bhgqk', q, k) * scale
        attn = jax.nn.softmax(scores.astype(jnp.float32), axis=-1).astype(q.dtype)
        out = jnp.einsum('bhgqk,bkhd->bqhgd', attn, v)
        out = out.reshape(b, q_len, N_HEADS * HEAD_DIM)
        return out @ Wo

    def _L0_attn_ref(x, wq, wk, wv, wo):
        import jax, jax.numpy as jnp
        import numpy as np
        B, S, D = (2, 256, 512)
        H = 32
        HD = D // H
        THETA = 10000.0

        def _rope_cos_sin(seq_len, head_dim, theta=THETA):
            inv = 1.0 / theta ** (np.arange(0, head_dim, 2)[:head_dim // 2].astype(np.float32) / head_dim)
            t = np.arange(seq_len)
            f = np.outer(t, inv).astype(np.float32)
            return (jnp.asarray(np.cos(f)), jnp.asarray(np.sin(f)))

        def _apply_rotary(x, cos, sin):
            xr = x.astype(jnp.float32).reshape(*x.shape[:-1], HD // 2, 2)
            x0, x1 = (xr[..., 0], xr[..., 1])
            c = cos[None, :, None, :]
            s = sin[None, :, None, :]
            o0 = x0 * c - x1 * s
            o1 = x0 * s + x1 * c
            return jnp.stack((o0, o1), axis=-1).reshape(*x.shape[:-1], HD)
        b, s, d = x.shape
        q = (x @ wq).reshape(b, s, H, HD)
        k = (x @ wk).reshape(b, s, H, HD)
        v = (x @ wv).reshape(b, s, H, HD)
        cos, sin = _rope_cos_sin(s, HD)
        q = _apply_rotary(q, cos, sin)
        k = _apply_rotary(k, cos, sin)
        scale = 1.0 / jnp.sqrt(jnp.float32(HD))
        scores = jnp.einsum('bqhd,bkhd->bhqk', q, k) * scale
        causal = jnp.tril(jnp.ones((s, s), dtype=bool))
        scores = jnp.where(causal[None, None], scores, jnp.finfo(scores.dtype).min)
        probs = jax.nn.softmax(scores, axis=-1)
        out = jnp.einsum('bhqk,bkhd->bqhd', probs, v).reshape(b, s, d)
        return out @ wo

    def _L0_ffn_ref(hidden_states, router_weight, router_bias, expert_bias):
        import jax, jax.numpy as jnp
        import numpy as np
        K_TOP = 8
        B, S, H = hidden_states.shape
        E = router_weight.shape[0]
        T = B * S
        flat = hidden_states.reshape(T, H)
        logits = jnp.einsum('th,eh->te', flat, router_weight) + router_bias
        scores = jax.nn.softmax(logits, axis=-1)
        topk_w, topk_idx = jax.lax.top_k(scores, K_TOP)
        w_sum = topk_w.sum(axis=-1, keepdims=True)
        w_dense = jnp.zeros((T, E), dtype=scores.dtype).at[jnp.arange(T)[:, None], topk_idx].add(topk_w)
        bias_mix = jnp.einsum('te,eh->th', w_dense, expert_bias)
        out = flat * w_sum + bias_mix
        return out.reshape(B, S, H)
    x = x + _L0_xattn_ref(_layernorm(x, axis=-1), ctx_4096, L0_xattn_Wq, L0_xattn_Wk, L0_xattn_Wv, L0_xattn_Wo)
    x = x + _L0_attn_ref(_layernorm(x, axis=-1), L0_attn_wq, L0_attn_wk, L0_attn_wv, L0_attn_wo)
    x = x + _L0_ffn_ref(_layernorm(x, axis=-1), L0_ffn_router_weight, L0_ffn_router_bias, L0_ffn_expert_bias)
    return x

_drawn_inputs = setup_inputs


def setup_inputs(seed=0):
    import zlib

    import numpy as np

    out = dict(_drawn_inputs(seed))
    spreads = {'L0_ffn_router_bias': (0.0, 0.8)}
    factors = {'L0_attn_wq': 8.0, 'L0_attn_wk': 8.0}
    for name, (base, spread) in spreads.items():
        noise = np.random.default_rng([zlib.crc32(name.encode()), seed]).standard_normal(out[name].shape)
        drawn = base * np.exp(spread * noise) if base else spread * noise
        out[name] = jnp.asarray(drawn.astype(out[name].dtype))
    for name, factor in factors.items():
        out[name] = (out[name] * factor).astype(out[name].dtype)
    return out
```

```python
from contextlib import ExitStack

import concourse.bass as bass
from concourse import mybir
import numpy as np

F32 = mybir.dt.float32
F32R = mybir.dt.float32r
ALU = mybir.AluOpType
ACT = mybir.ActivationFunctionType
AX = mybir.AxisListType

P = 128
D = 512
KT = D // P
B, NL, NC = 16, 64, 128
NK = NL + NC
TT = B * NL // P
HK, G, HD = 4, 8, 128
XS = float(HD) ** -0.5
SD = 16
E = 64
KV = 2 * NK + 3 * HD
EPS = 1e-5
PASSES = ((0, 0), (0, 1), (1, 0))


def wait_pos(eng, sem, value):
    if isinstance(value, int) and value <= 0:
        return
    eng.wait_ge(sem, value)


def wait_apart(eng, sem, value):
    if not isinstance(value, int):
        value = eng.to_reg(value)
        eng.wait_ge(sem, 1)
    wait_pos(eng, sem, value)


def contexts(seq):
    return seq[:].rearrange("p k (c n) -> p k c n", c=3)[:, :, 0:3:2, :]


def latents(seq):
    return seq[:, :, NC:NC + P]


def stage_keys_values(nc, env):
    ctx = ExitStack()
    with ctx:
        def sb(name, shape, dt=F32):
            return ctx.enter_context(nc.sbuf_tensor(name, shape, dt))

        def ps(name):
            return ctx.enter_context(nc.psum_tensor(name, [P, 512], F32))

        def sem(name):
            return ctx.enter_context(nc.semaphore(name))

        x1, xnT, ident = env["x1"], env["xnT"], env["ident"]
        wk_f = sb("wk_f", [P, KT, D])
        wv_f = sb("wv_f", [P, KT, D])
        wk = [sb(f"wk_{n}", [P, KT, D], F32R) for n in "hl"]
        wv = [sb(f"wv_{n}", [P, KT, D], F32R) for n in "hl"]
        ctx_f = [sb(f"ctx_f{i}", [P, KT, 2, NC]) for i in range(2)]
        seq = [[sb(f"seq{i}_{n}", [P, KT, 2 * NK], F32R) for n in "hl"] for i in range(2)]
        stats = sb("a_stats", [P, 2, 6])
        mv = sb("a_mv", [P, 2, 2])
        var = sb("a_var", [P, 2, 1])
        rstd = sb("a_rstd", [P, 2, 1])
        minus_half = env["minus_half"]
        xn = sb("a_xn", [P, 2, D])
        kv = [sb(f"kv_out{i}", [P, HK, KV]) for i in range(2)]
        ps_t = ps("a_ps_t")
        ps_k = [ps(f"a_ps_k{i}") for i in range(2)]
        ps_v = [ps(f"a_ps_v{i}") for i in range(3)]

        ident_ready = sem("ident_ready")
        w_in = [sem("a_wk_in"), sem("a_wv_in")]
        x_in = [sem(f"a_x_in{i}") for i in range(2)]
        ctx_in = [sem(f"a_ctx_in{i}") for i in range(2)]
        kv_stored = [sem(f"a_kv_stored{i}") for i in range(2)]
        w_high = sem("a_w_high")
        w_low = sem("a_w_low")
        ln_steps = sem("a_ln_steps")
        var_ready = sem("a_var_ready")
        rstd_ready = sem("a_rstd_ready")
        xn_ready = sem("a_xn_ready")
        xnT_ps = sem("a_xnT_ps")
        ctx_high = sem("a_ctx_high")
        ctx_low = sem("a_ctx_low")
        lat_high = sem("a_lat_high")
        lat_low = sem("a_lat_low")
        lat_kept = sem("a_lat_kept")
        k_ps = sem("a_k_ps")
        v_ps = sem("a_v_ps")
        k_out = sem("a_k_out")
        v_out = sem("a_v_out")
        block = ctx.enter_context(nc.Block())

        @block.sync
        def _(sp):
            def load(t, i):
                wait_pos(sp, xn_ready, t - 1)
                sp.dma_start(x1[:, bass.ds(t, 1), :], env["x"][bass.ds(t, 1)].rearrange("t p d -> p t d"))\
                    .then_inc(x_in[i], 16)
                wait_pos(sp, ctx_low, t - 1)
                sp.dma_start(ctx_f[i][:], env["ctxT"][bass.ds(t, 1)].rearrange("t p c -> p (t c)")
                             .rearrange("p (k b n) -> p k b n", k=KT, b=2)).then_inc(ctx_in[i], 16)

            def store(t, i):
                wait_apart(sp, k_out, HK * (t + 1))
                sp.wait_ge(v_out, 3 * (t + 1))
                sp.dma_start(env["kv_dram"][bass.ds(t, 1)].rearrange("t p c -> p (t c)"),
                             kv[i][:].rearrange("p h c -> p (h c)")).then_inc(kv_stored[i], 16)

            load(0, 0)
            sp.dma_start(wv_f[:], env["wv"].rearrange("(k p) n -> p k n", p=P)).then_inc(w_in[1], 16)
            sp.dma_start(wk_f[:], env["wk"].rearrange("(k p) n -> p k n", p=P)).then_inc(w_in[0], 16)
            load(1, 1)
            with sp.Fori(0, TT // 2 - 1) as tb:
                for i in range(2):
                    load(2 * tb + 2 + i, i)
                    store(2 * tb + i, i)
            for i in range(2):
                store(TT - 2 + i, i)
            for i in range(2):
                sp.wait_ge(kv_stored[i], 16 * (TT // 2))

        @block.gpsimd
        def _(pool):
            pool.memset(ident[:], 0.0).then_inc(ident_ready, 1)
            pool.wait_ge(ident_ready, 1)
            pool.affine_select(out=ident[:], in_=ident[:], compare_op=ALU.not_equal, fill=1.0, base=0,
                               pattern=[[-1, P]], channel_multiplier=1).then_inc(ident_ready, 1)
            pool.memset(minus_half[:], -0.5).then_inc(ident_ready, 1)
            def inverse_deviation(t, i):
                wait_apart(pool, ln_steps, 2 * t + 2)
                pool.tensor_scalar(var[:, i, :], mv[:, i, 1:2], EPS, None, ALU.add).then_inc(var_ready, 1)
                pool.wait_ge(var_ready, t + 1)
                pool.tensor_tensor(rstd[:, i, :], var[:, i, :], minus_half[:], ALU.pow).then_inc(rstd_ready, 1)

            def keep_latents(t, i):
                pool.wait_ge(lat_low, t + 1)
                for n in range(2):
                    last = pool.tensor_copy(xnT[n][:, :, bass.ds(t * P, P)], latents(seq[i][n]).bitcast(F32))
                last.then_inc(lat_kept, 1)

            pool.wait_ge(ident_ready, 3)
            inverse_deviation(0, 0)
            inverse_deviation(1, 1)
            with pool.Fori(0, TT // 2 - 1) as tb:
                for i in range(2):
                    inverse_deviation(2 * tb + 2 + i, i)
                    keep_latents(2 * tb + i, i)
            keep_latents(TT - 2, 0)
            keep_latents(TT - 1, 1)

        @block.scalar
        def _(act):
            def split_ctx(tb, i):
                t = 2 * tb + i
                act.wait_ge(ctx_in[i], 16 * (tb + 1))
                wait_pos(act, v_ps, 3 * (t - 1))
                act.activation(contexts(seq[i][0]), ctx_f[i][:], ACT.Copy).then_inc(ctx_high, 1)

            def split_latents(tb, i):
                t = 2 * tb + i
                act.wait_ge(xnT_ps, t + 1)
                wait_pos(act, lat_kept, t - 1)
                act.activation(latents(seq[i][0]), ps_t[:].rearrange("p (k n) -> p k n", k=KT),
                               ACT.Copy).then_inc(lat_high, 1)

            def values_out(tb, i):
                t = 2 * tb + i
                wait_pos(act, kv_stored[i], 16 * tb)
                for c in range(3):
                    act.wait_ge(v_ps, 3 * t + c + 1)
                    act.activation(kv[i][:, :, 2 * NK + c * HD:2 * NK + (c + 1) * HD],
                                   ps_v[c][:].rearrange("p (h d) -> p h d", h=HK), ACT.Copy).then_inc(v_out, 1)

            split_ctx(0, 0)
            for n, (f, w) in enumerate(((wv_f, wv), (wk_f, wk))):
                act.wait_ge(w_in[1 - n], 16)
                act.activation(w[0][:], f[:], ACT.Copy).then_inc(w_high, 1)
            split_latents(0, 0)
            split_ctx(0, 1)

            def two_tiles(tb):
                for i in range(2):
                    values_out(tb, i)
                    split_latents(tb + i, 1 - i)
                    split_ctx(tb + 1, i)

            two_tiles(0)
            with act.Fori(1, TT // 2 - 1) as tb:
                two_tiles(tb)
            values_out(TT // 2 - 1, 0)
            split_latents(TT // 2 - 1, 1)
            values_out(TT // 2 - 1, 1)

        @block.vector
        def _(dve):
            def layernorm(tb, i):
                t = 2 * tb + i
                dve.wait_ge(x_in[i], 16 * (tb + 1))
                wait_pos(dve, xnT_ps, t - 1)
                xt = x1[:, bass.ds(t, 1), :].rearrange("p t d -> p (t d)")
                dve.bn_stats(stats[:, i, :], xt).then_inc(ln_steps, 1)
                wait_apart(dve, ln_steps, 2 * t + 1)
                dve.bn_aggr(mv[:, i, :], stats[:, i, :]).then_inc(ln_steps, 1)
                dve.wait_ge(rstd_ready, t + 1)
                dve.tensor_scalar(xn[:, i, :], xt, mv[:, i, 0:1], rstd[:, i, :], ALU.subtract, ALU.mult)\
                    .then_inc(xn_ready, 1)

            def split_ctx(tb, i):
                t = 2 * tb + i
                dve.wait_ge(ctx_high, t + 1)
                dve.tensor_tensor(contexts(seq[i][1]), ctx_f[i][:], contexts(seq[i][0]).bitcast(F32),
                                  ALU.subtract).then_inc(ctx_low, 1)

            def split_latents(tb, i):
                t = 2 * tb + i
                dve.wait_ge(lat_high, t + 1)
                dve.tensor_tensor(latents(seq[i][1]), ps_t[:].rearrange("p (k n) -> p k n", k=KT),
                                  latents(seq[i][0]).bitcast(F32), ALU.subtract).then_inc(lat_low, 1)

            def keys_out(tb, i):
                t = 2 * tb + i
                wait_pos(dve, kv_stored[i], 16 * tb)
                for h in range(HK):
                    dve.wait_ge(k_ps, HK * t + h + 1)
                    dve.tensor_copy(kv[i][:, h, 0:2 * NK], ps_k[h % 2][:, 0:2 * NK]).then_inc(k_out, 1)

            layernorm(0, 0)
            split_ctx(0, 0)
            for n, (f, w) in enumerate(((wv_f, wv), (wk_f, wk))):
                dve.wait_ge(w_high, n + 1)
                dve.tensor_tensor(w[1][:], f[:], w[0][:].bitcast(F32), ALU.subtract).then_inc(w_low, 1)
            split_latents(0, 0)
            layernorm(0, 1)
            split_ctx(0, 1)

            def two_tiles(tb):
                for i in range(2):
                    keys_out(tb, i)
                    split_latents(tb + i, 1 - i)
                    layernorm(tb + 1, i)
                    split_ctx(tb + 1, i)

            two_tiles(0)
            with dve.Fori(1, TT // 2 - 1) as tb:
                two_tiles(tb)
            keys_out(TT // 2 - 1, 0)
            split_latents(TT // 2 - 1, 1)
            keys_out(TT // 2 - 1, 1)

        @block.tensor
        def _(pe):
            def transposes(t, i):
                pe.wait_ge(xn_ready, t + 1)
                wait_pos(pe, lat_low, t)
                for k in range(KT):
                    last = pe.transpose(ps_t[:, k * P:(k + 1) * P], xn[:, i, k * P:(k + 1) * P], ident[:])
                last.then_inc(xnT_ps, 1)

            def value(t, i, c):
                wait_pos(pe, v_out, 3 * (t - 1) + c + 1)
                n = 0
                for a, b in PASSES:
                    for k in range(KT):
                        last = pe.matmul(ps_v[c][:], seq[i][a][:, k, (0, 2 * P, P)[c]:][:, 0:P], wv[b][:, k, :], start=(n == 0), stop=(n == 3 * KT - 1))
                        n += 1
                last.then_inc(v_ps, 1)

            def keys(t, i, h):
                wait_pos(pe, k_out, HK * t + h - 1)
                n = 0
                for a, b in PASSES:
                    for k in range(KT):
                        last = pe.matmul(ps_k[h % 2][:, 0:2 * NK], wk[a][:, k, h * HD:(h + 1) * HD],
                                         seq[i][b][:, k, :], start=(n == 0), stop=(n == 3 * KT - 1))
                        n += 1
                last.then_inc(k_ps, 1)

            def step(t, i, first=False, last=False):
                pe.wait_ge(ctx_low, t + 1)
                if first:
                    pe.wait_ge(w_low, 1)
                value(t, i, 0)
                if not last:
                    transposes(t + 1, 1 - i)
                value(t, i, 1)
                if first:
                    pe.wait_ge(w_low, 2)
                pe.wait_ge(lat_low, t + 1)
                for h in range(HK):
                    keys(t, i, h)
                value(t, i, 2)

            pe.wait_ge(ident_ready, 2)
            transposes(0, 0)
            step(0, 0, first=True)
            step(1, 1)
            with pe.Fori(1, TT // 2 - 1) as tb:
                for i in range(2):
                    step(2 * tb + i, i)
            step(TT - 2, 0)
            step(TT - 1, 1, last=True)


def stage_cross_attention(nc, env):
    ctx = ExitStack()
    with ctx:
        def sb(name, shape, dt=F32):
            return ctx.enter_context(nc.sbuf_tensor(name, shape, dt))

        def ps(name):
            return ctx.enter_context(nc.psum_tensor(name, [P, 512], F32))

        def sem(name):
            return ctx.enter_context(nc.semaphore(name))

        HALF = TT // 2
        HT = HALF * P
        STEPS = HK * B
        BODIES = STEPS // 4
        VO = 2 * NK
        WO_RING = G + 4

        x1, xnT, ident = env["x1"], env["xnT"], env["ident"]
        wq_f = sb("wq_f", [P, 2, KT, HD])
        wq = [sb(f"wq_{n}", [P, 2, KT, HD], F32R) for n in "hl"]
        wo_f = sb("wo_f", [P, 2, D])
        wo = [sb(f"wo_{n}", [P, WO_RING, D], F32R) for n in "hl"]
        kv_f = sb("kv_f", [P, 2, KV])
        kv = [sb(f"kv_{n}", [P, 2, KV], F32R) for n in "hl"]
        q_all = sb("q_all", [P, 2, G, HT])
        q = [sb(f"q_{n}", [P, 2, G, NL], F32R) for n in "hl"]
        probs = [sb(f"probs{i}", [P, NL + 4 * NK]) for i in range(2)]
        pT_ctx = [sb(f"pT_ctx_{n}", [P, 512], F32R) for n in "hl"]
        pT_lat = [sb(f"pT_lat_{n}", [P, 512], F32R) for n in "hl"]
        oT = [sb(f"oT_{n}", [P, 2, G, P], F32R) for n in "hl"]
        nmax = sb("nmax", [P, 2, 4])
        psum_p = sb("psum_p", [P, 2, 4])
        rsum = sb("rsum", [P, 2, 4])
        ps_q = [ps(f"ps_q{i}") for i in range(2)]
        ps_s = [ps(f"ps_s{i}") for i in range(2)]
        ps_tc, ps_tl, ps_o, ps_y = ps("ps_tc"), ps("ps_tl"), ps("ps_o"), ps("ps_y")

        wq_in = [sem(f"wq_in{i}") for i in range(2)]
        wo_in = [sem(f"wo_in{i}") for i in range(2)]
        kv_in = [sem(f"kv_in{i}") for i in range(2)]
        wq_high, wq_low = sem("wq_high"), sem("wq_low")
        wo_high, wo_low = sem("wo_high"), sem("wo_low")
        kv_high, kv_low = sem("kv_high"), sem("kv_low")
        q_high, q_low = sem("q_high"), sem("q_low")
        q_ps = sem("q_ps")
        q_out = sem("q_out")
        s_ps = sem("s_ps")
        pad_ready = sem("pad_ready")
        max_ready = sem("max_ready")
        exp_done = sem("exp_done")
        rsum_ready = sem("rsum_ready")
        probs_ready = sem("probs_ready")
        pT_ps = sem("pT_ps")
        pT_high, pT_low = sem("pT_high"), sem("pT_low")
        o_ps = sem("o_ps")
        oT_high, oT_low = sem("oT_high"), sem("oT_low")
        y_head = sem("y_head")
        x_added = sem("x_added")
        block = ctx.enter_context(nc.Block())

        @block.sync
        def _(sp):
            def load_wq(c, i):
                wait_pos(sp, wq_low, c - 1)
                row = (c // (2 * G)) * G + c % G
                sp.dma_start(wq_f[:, i], env["wq"][bass.ds(row, 1)].rearrange("r p (k d) -> p (r k) d", k=KT))\
                    .then_inc(wq_in[i], 16)

            def load_kv(pair, i):
                wait_pos(sp, kv_low, pair - 1)
                t, h = pair % TT, pair // TT
                sp.dma_start(kv_f[:, i, :], env["kv_dram"][bass.ds(t, 1), :, bass.ds(h * KV, KV)]
                             .rearrange("t p c -> p (t c)")).then_inc(kv_in[i], 16)

            load_wq(0, 0)
            load_wq(1, 1)
            load_kv(0, 0)
            load_kv(1, 1)
            for c in range(2, G + 2):
                load_wq(c, c % 2)

            def body(bi, more_wq=4, more_kv=2):
                for k in range(4):
                    if k < more_wq:
                        load_wq(4 * bi + k + G + 2, k % 2)
                    if k % 2 and k // 2 < more_kv:
                        load_kv(2 * bi + 2 + k // 2, k // 2)

            with sp.Fori(0, BODIES - 3) as bi:
                body(bi)
            body(BODIES - 3, more_wq=2)
            body(BODIES - 2, more_wq=0)

        @block.gpsimd
        def _(pool):
            def load_wo(w, i):
                wait_pos(pool, wo_low, w - 1)
                pool.dma_start(wo_f[:, i, :], env["wo"][bass.ds(w * HD, HD), :]).then_inc(wo_in[i], 16)

            def split_wo(w, i):
                pool.wait_ge(wo_in[i], 16 * (w // 2 + 1))
                old = w - WO_RING
                wait_apart(pool, y_head, (old // G * TT + TT - 1) * G + old % G + 1)
                place = bass.ds(w % WO_RING, 1)
                pool.tensor_copy(wo[0][:, place, :], wo_f[:, i:i + 1, :]).then_inc(wo_high, 1)
                wait_apart(pool, wo_high, w + 1)
                pool.tensor_tensor(wo[1][:, place, :], wo_f[:, i:i + 1, :], wo[0][:, place, :].bitcast(F32),
                                   ALU.subtract).then_inc(wo_low, 1)

            load_wo(0, 0)
            load_wo(1, 1)
            for w in range(WO_RING):
                split_wo(w, w % 2)
                load_wo(w + 2, w % 2)
            with pool.Fori(WO_RING // 2, HK * G // 2 - 1) as half:
                for i in range(2):
                    split_wo(2 * half + i, i)
                    load_wo(2 * half + i + 2, i)
            for i in range(2):
                split_wo(HK * G - 2 + i, i)

        def step_queries(bi, k):
            return q_all[:, bass.ds((bi // 2) % 2, 1), :, bass.ds((bi % 2) * 4 * NL + k * NL, NL)]\
                .rearrange("p a g t -> p (a g) t")

        def before(bi, k):
            return (bi, k - 1) if k else (bi - 1, 3)

        def after(bi, k):
            return (bi, k + 1) if k < 3 else (bi + 1, 0)

        @block.scalar
        def _(act):
            def split_wq(c, i, uses):
                act.wait_ge(wq_in[i], 16 * uses)
                wait_pos(act, q_ps, c - 1)
                act.activation(wq[0][:, i], wq_f[:, i], ACT.Copy).then_inc(wq_high, 1)

            def queries_out(c, i, parity, g):
                act.wait_ge(q_ps, c + 1)
                act.activation(q_all[:, bass.ds(parity, 1), bass.ds(g, 1), :].rearrange("p a g t -> p (a g t)"),
                               ps_q[i][:], ACT.Copy, scale=XS).then_inc(q_out, 1)

            def split_kv(pair, i, uses):
                act.wait_ge(kv_in[i], 16 * uses)
                wait_pos(act, o_ps, 2 * (pair - 1))
                act.activation(kv[0][:, i, :], kv_f[:, i, :], ACT.Copy).then_inc(kv_high, 1)

            def split_q(bi, k):
                n = 4 * bi + k
                wait_pos(act, s_ps, 2 * (n - 1))
                act.wait_ge(q_out, (bi // 2 + 1) * G)
                act.activation(q[0][:, k % 2], step_queries(bi, k), ACT.Copy).then_inc(q_high, 1)

            def softmax(bi, k, js):
                n, i = 4 * bi + k, k % 2
                wait_pos(act, pT_ps, 2 * (n - 1))
                for j in js:
                    if j % 2 == 0:
                        act.wait_ge(max_ready, 2 * n + j // 2 + 1)
                    act.activation(probs[i][:, NL + j * NK:NL + (j + 1) * NK],
                                   ps_s[j // 2][:, (j % 2) * NK:(j % 2 + 1) * NK], ACT.Exp,
                                   bias=nmax[:, i, j:j + 1], accum_out=psum_p[:, i, j:j + 1]).then_inc(exp_done, 1)

            def split_probs(bi, k):
                n, rows = 4 * bi + k, slice(k % 2 * NL, k % 2 * NL + NL)
                wait_pos(act, o_ps, n)
                act.wait_ge(pT_ps, 2 * n + 1)
                act.activation(pT_ctx[0][:], ps_tc[:], ACT.Copy).then_inc(pT_high, 1)
                act.wait_ge(pT_ps, 2 * n + 2)
                act.activation(pT_lat[0][rows, :], ps_tl[rows, :], ACT.Copy).then_inc(pT_high, 1)

            def split_out(bi, k):
                n, pair = 4 * bi + k, 2 * bi + k // 2
                act.wait_ge(o_ps, n + 1)
                wait_pos(act, y_head, (pair - 1) * G)
                act.activation(oT[0][:, k // 2, :, k % 2 * NL:(k % 2 + 1) * NL],
                               ps_o[:].rearrange("p (g t) -> p g t", g=G), ACT.Copy).then_inc(oT_high, 1)

            def body(bi, queries=4, wqs=4, first=False, last=False):
                for k in range(4):
                    n = 4 * bi + k
                    softmax(bi, k, (0, 1))
                    if not (first and k == 0):
                        split_out(*before(bi, k))
                    softmax(bi, k, (2, 3))
                    if k < wqs:
                        split_wq(n + G + 1, (k + 1) % 2, 2 * bi + (k + G + 1) // 2 + 1)
                    if k % 2 == 0 and not (last and k == 2):
                        split_kv(2 * bi + k // 2 + 1, (k // 2 + 1) % 2, bi + k // 2 + 1)
                    if k < queries:
                        queries_out(n + G, k % 2, (bi // 2 + 1) % 2, (bi % 2) * 4 + k)
                    if not (last and k == 3):
                        split_q(*after(bi, k))
                    split_probs(bi, k)

            for c in range(G):
                split_wq(c, c % 2, c // 2 + 1)
                if c:
                    queries_out(c - 1, (c - 1) % 2, 0, c - 1)
                if c == 2:
                    split_kv(0, 0, 1)
            split_wq(G, 0, G // 2 + 1)
            queries_out(G - 1, 1, 0, G - 1)
            split_q(0, 0)
            body(0, first=True)
            with act.Fori(1, BODIES - 3) as bi:
                body(bi)
            body(BODIES - 3, wqs=3)
            body(BODIES - 2, queries=0, wqs=0)
            body(BODIES - 1, queries=0, wqs=0, last=True)
            split_out(BODIES - 1, 3)

        @block.vector
        def _(dve):
            def low_wq(c, i):
                dve.wait_ge(wq_high, c + 1)
                dve.tensor_tensor(wq[1][:, i], wq_f[:, i], wq[0][:, i].bitcast(F32), ALU.subtract)\
                    .then_inc(wq_low, 1)

            def low_kv(pair, i):
                dve.wait_ge(kv_high, pair + 1)
                dve.tensor_tensor(kv[1][:, i, :], kv_f[:, i, :], kv[0][:, i, :].bitcast(F32), ALU.subtract)\
                    .then_inc(kv_low, 1)

            def low_q(bi, k):
                dve.wait_ge(q_high, 4 * bi + k + 1)
                dve.tensor_tensor(q[1][:, k % 2], step_queries(bi, k), q[0][:, k % 2].bitcast(F32), ALU.subtract)\
                    .then_inc(q_low, 1)

            def row_max(bi, k):
                n, i = 4 * bi + k, k % 2
                for j in range(2):
                    dve.wait_ge(s_ps, 2 * n + j + 1)
                    dve.tensor_reduce(nmax[:, i, 2 * j:2 * j + 2],
                                      ps_s[j][:, 0:2 * NK].rearrange("p (j n) -> p j n", j=2), AX.X, ALU.max,
                                      negate=True).then_inc(max_ready, 1)

            def normalise(bi, k):
                n, i = 4 * bi + k, k % 2
                dve.wait_ge(exp_done, 4 * (n + 1))
                dve.reciprocal(rsum[:, i, :], psum_p[:, i, :]).then_inc(rsum_ready, 1)
                dve.wait_ge(rsum_ready, n + 1)
                for j in range(4):
                    p = probs[i][:, NL + j * NK:NL + (j + 1) * NK]
                    last = dve.tensor_scalar(p, p, rsum[:, i, j:j + 1], None, ALU.mult)
                last.then_inc(probs_ready, 1)

            def low_probs(bi, k):
                n, rows = 4 * bi + k, slice(k % 2 * NL, k % 2 * NL + NL)
                dve.wait_ge(pT_high, 2 * n + 1)
                dve.tensor_tensor(pT_ctx[1][:], ps_tc[:], pT_ctx[0][:].bitcast(F32), ALU.subtract).then_inc(pT_low, 1)
                dve.wait_ge(pT_high, 2 * n + 2)
                dve.tensor_tensor(pT_lat[1][rows, :], ps_tl[rows, :], pT_lat[0][rows, :].bitcast(F32), ALU.subtract)\
                    .then_inc(pT_low, 1)

            def add_output(pair):
                dve.wait_ge(y_head, (pair + 1) * G)
                xt = x1[:, bass.ds(pair % TT, 1), :].rearrange("p t d -> p (t d)")
                dve.tensor_tensor(xt, ps_y[:], xt, ALU.add).then_inc(x_added, 1)

            def low_out(bi, k):
                dve.wait_ge(oT_high, 4 * bi + k + 1)
                cols = slice(k % 2 * NL, (k % 2 + 1) * NL)
                dve.tensor_tensor(oT[1][:, k // 2, :, cols], ps_o[:].rearrange("p (g t) -> p g t", g=G),
                                  oT[0][:, k // 2, :, cols].bitcast(F32), ALU.subtract).then_inc(oT_low, 1)

            def body(bi, wqs=4, first=False, last=False):
                for k in range(4):
                    row_max(bi, k)
                    if k % 2 == 0 and not first:
                        add_output(2 * bi + k // 2 - 2)
                    if not (first and k == 0):
                        low_out(*before(bi, k))
                    normalise(bi, k)
                    if k < wqs:
                        low_wq(4 * bi + k + G + 1, (k + 1) % 2)
                    if k % 2 == 0 and not (last and k == 2):
                        low_kv(2 * bi + k // 2 + 1, (k // 2 + 1) % 2)
                    if not (last and k == 3):
                        low_q(*after(bi, k))
                    low_probs(bi, k)

            dve.memset(probs[1][:, 0:NL], 0.0).then_inc(pad_ready, 1)
            for c in range(G):
                low_wq(c, c % 2)
                if c == 2:
                    low_kv(0, 0)
            low_wq(G, 0)
            low_q(0, 0)
            body(0, first=True)
            with dve.Fori(1, BODIES - 3) as bi:
                body(bi)
            body(BODIES - 3, wqs=3)
            body(BODIES - 2, wqs=0)
            body(BODIES - 1, wqs=0, last=True)
            low_out(BODIES - 1, 3)
            add_output(STEPS // 2 - 2)
            add_output(STEPS // 2 - 1)

        @block.tensor
        def _(pe):
            def product(out, pairs, **kw):
                for n, (lhsT, rhs) in enumerate(pairs):
                    last = pe.matmul(out, lhsT, rhs, start=(n == 0), stop=(n == len(pairs) - 1), **kw)
                return last

            def queries(c, i, half):
                pe.wait_ge(wq_low, c + 1)
                wait_pos(pe, q_out, c - 1)
                product(ps_q[i][:], [(wq[a][:, i, t, :], xnT[b][:, t, bass.ds(half * HT, HT)])
                                     for a, b in PASSES for t in range(KT)]).then_inc(q_ps, 1)

            def scores(bi, k):
                n, pair = 4 * bi + k, 2 * bi + k // 2
                keys = slice(k % 2 * NK, (k % 2 + 1) * NK)
                if k % 2 == 0:
                    pe.wait_ge(kv_low, pair + 1)
                pe.wait_ge(q_low, n + 1)
                for j in range(4):
                    if j % 2 == 0:
                        wait_pos(pe, exp_done, 4 * (n - 1) + j + 2)
                    last = product(ps_s[j // 2][:, (j % 2) * NK:(j % 2 + 1) * NK],
                                   [(q[a][:, k % 2, 2 * j:2 * j + 2, :].rearrange("p g t -> p (g t)"),
                                     kv[b][:, k // 2, keys]) for a, b in PASSES])
                    if j % 2:
                        last.then_inc(s_ps, 1)

            def transposes(bi, k):
                n, s = 4 * bi + k, k % 2
                pe.wait_ge(probs_ready, n + 1)
                wait_pos(pe, pT_low, 2 * n)
                for j in range(4):
                    start = NL + j * NK + (NL if s else 0)
                    last = pe.transpose(ps_tc[:, j * P:(j + 1) * P], probs[s][:, start:start + NC], ident[:])
                last.then_inc(pT_ps, 1)
                for j in range(4):
                    if s:
                        last = pe.transpose(ps_tl[:, j * P:(j + 1) * P], probs[s][:, j * NK:j * NK + P], ident[:])
                    else:
                        start = NL + j * NK + NC
                        last = pe.transpose(ps_tl[0:NL, j * P:(j + 1) * P], probs[s][:, start:start + NL], ident[:])
                last.then_inc(pT_ps, 1)

            def output_product(pair, i, heads):
                if 0 in heads:
                    pe.wait_ge(oT_low, 2 * (pair + 1))
                    wait_pos(pe, x_added, pair)
                for g in heads:
                    w = pair // TT * G + g
                    pe.wait_ge(wo_low, w + 1)
                    for n, (a, b) in enumerate(PASSES):
                        last = pe.matmul(ps_y[:], oT[a][:, i, g, :], wo[b][:, bass.ds(w % WO_RING, 1), :]
                                         .rearrange("p w d -> p (w d)"), start=(g == 0 and n == 0),
                                         stop=(g == G - 1 and n == 2))
                    last.then_inc(y_head, 1)

            def outputs(bi, k):
                n, i, s = 4 * bi + k, k // 2, k % 2
                lat = slice(s * NL, (s + 1) * NL)
                wait_pos(pe, oT_low, n)
                pe.wait_ge(pT_low, 2 * n + 1)
                for m, (a, b) in enumerate(PASSES):
                    pe.matmul(ps_o[:], kv[a][:, i, VO + s * HD:VO + (s + 1) * HD], pT_ctx[b][:], start=(m == 0),
                              stop=False)
                pe.wait_ge(pT_low, 2 * n + 2)
                for m, (a, b) in enumerate(PASSES):
                    last = pe.matmul(ps_o[:], kv[a][lat, i, VO + 2 * HD:VO + 3 * HD], pT_lat[b][lat, :], start=False,
                                     stop=(m == 2))
                last.then_inc(o_ps, 1)

            def body(bi, next_queries=True, first=False, last=False):
                for k in range(4):
                    pair, i = 2 * bi + k // 2 - 1, (k // 2 + 1) % 2
                    if next_queries:
                        queries(4 * bi + k + G, k % 2, (bi // 2 + 1) % 2)
                    if not (first and k < 2):
                        output_product(pair, i, range(k % 2 * 4, k % 2 * 4 + 3))
                    transposes(bi, k)
                    if not (first and k < 2):
                        output_product(pair, i, range(k % 2 * 4 + 3, k % 2 * 4 + 4))
                    if not (last and k == 3):
                        scores(*after(bi, k))
                    outputs(bi, k)

            for c in range(G):
                queries(c, c % 2, 0)
            pe.wait_ge(pad_ready, 1)
            scores(0, 0)
            body(0, first=True)
            with pe.Fori(1, BODIES - 2) as bi:
                body(bi)
            body(BODIES - 2, next_queries=False)
            body(BODIES - 1, next_queries=False, last=True)
            output_product(STEPS // 2 - 1, 1, range(G))


def stage_self_attention(nc, env):
    ctx = ExitStack()
    with ctx:
        def sb(name, shape, dt=F32):
            return ctx.enter_context(nc.sbuf_tensor(name, shape, dt))

        def ps(name):
            return ctx.enter_context(nc.psum_tensor(name, [P, 512], F32))

        def sem(name):
            return ctx.enter_context(nc.semaphore(name))

        x1, ident, minus_half = env["x1"], env["ident"], env["minus_half"]
        names = ("k", "q", "v", "o")
        w_f = {n: sb(f"c_w{n}_f", [P, KT, D]) for n in names}
        w = {n: [sb(f"c_w{n}_{p}", [P, KT, D], F32R) for p in "hl"] for n in names}
        ident_r = sb("ident_r", [P, P], F32R)
        cmask_f, cmask = sb("c_mask_f", [P, D]), sb("c_mask", [P, D], F32R)
        bmask = sb("c_bmask", [P, 4])
        cos, sin = sb("c_cos", [P, SD]), sb("c_sin", [P, SD])
        stats, mv = sb("c_stats", [P, 6]), sb("c_mv", [P, 2])
        var, rstd = sb("c_var", [P, 1]), sb("c_rstd", [P, 1])
        xn = sb("c_xn", [P, D])
        xT = [sb(f"c_xT_{p}", [P, KT, P], F32R) for p in "hl"]
        rot_a = {n: sb(f"rot_a_{n}", [P, D]) for n in "kq"}
        rot_b = {n: sb(f"rot_b_{n}", [P, D]) for n in "kq"}
        kT = [sb(f"c_kT_{p}", [P, 4, P], F32R) for p in "hl"]
        qz = [[sb(f"qz{i}_{p}", [P, 4, 2, P], F32R) for p in "hl"] for i in range(2)]
        kblk = [[sb(f"kblk{s}_{p}", [P, 4, 4, NL], F32R) for p in "hl"] for s in range(2)]
        v_f, v_swap = sb("v_f", [P, D]), sb("v_swap", [P, D])
        vz = [[sb(f"vz{i}_{p}", [P, 2, D], F32R) for p in "hl"] for i in range(2)]
        probs = [sb(f"c_probs{i}", [P, D]) for i in range(2)]
        nmax, psum_p, rsum = (sb(n, [P, 2, 8]) for n in ("c_nmax", "c_psum", "c_rsum"))
        pT = [sb(f"c_pT_{p}", [P, 4, P], F32R) for p in "hl"]
        oT = [sb(f"c_oT_{p}", [P, 2, 4, P], F32R) for p in "hl"]
        ps_t = ps("c_ps_t")
        ps_p = [ps(f"c_ps_p{i}") for i in range(2)]
        ps_s = [ps(f"c_ps_s{i}") for i in range(2)]
        ps_pt = ps("c_ps_pt")
        ps_o = [ps(f"c_ps_o{i}") for i in range(2)]

        w_in = {n: sem(f"c_w{n}_in") for n in names}
        table_in = [sem(f"c_table_in{i}") for i in range(5)]
        w_high, w_low = sem("c_w_high"), sem("c_w_low")
        tables = sem("c_tables")
        zeroed = sem("c_zeroed")
        stats_ready = sem("c_stats_ready")
        var_ready, rstd_ready = sem("c_var_ready"), sem("c_rstd_ready")
        xn_ready = sem("c_xn_ready")
        xT_ps, xT_high, xT_low = sem("c_xT_ps"), sem("c_xT_high"), sem("c_xT_low")
        kp_ps, qp_ps, vp_ps = sem("kp_ps"), sem("qp_ps"), sem("vp_ps")
        k_turned, q_turned = sem("k_turned"), sem("q_turned")
        k_rot, q_rot = sem("k_rot"), sem("q_rot")
        kT_ps, kT_high, kT_low = sem("c_kT_ps"), sem("c_kT_high"), sem("c_kT_low")
        qT_ps, qz_high, qz_low = sem("c_qT_ps"), sem("c_qz_high"), sem("c_qz_low")
        kblk_ready = sem("kblk_ready")
        v_out = sem("v_out_c")
        v_swapped = sem("v_swapped")
        vz_high, vz_low = sem("vz_high"), sem("vz_low")
        vz_even = sem("vz_even")
        s_ps, max_ready, sub_done = sem("c_s_ps"), sem("c_max_ready"), sem("c_sub_done")
        exp_done, sum_ready, rsum_ready = sem("c_exp_done"), sem("c_sum_ready"), sem("c_rsum_ready")
        probs_ready = sem("c_probs_ready")
        pT_ps, pT_high, pT_low = sem("c_pT_ps"), sem("c_pT_high"), sem("c_pT_low")
        o_ps, oT_high, oT_low = sem("c_o_ps"), sem("c_oT_high"), sem("c_oT_low")
        y_ps, x_added = sem("c_y_ps"), sem("c_x_added")
        block = ctx.enter_context(nc.Block())

        def tile(t):
            return x1[:, bass.ds(t, 1), :].rearrange("p t d -> p (t d)")

        def is_last(t):
            return isinstance(t, int) and t == TT - 1

        def has_two_after(t):
            return not isinstance(t, int) or t < TT - 2

        def run(eng, slot):
            def two_tiles(tb):
                for i in range(2):
                    for o in range(4):
                        slot(2 * tb + i, i, o)
            two_tiles(0)
            with eng.Fori(1, TT // 2 - 1) as tb:
                two_tiles(tb)
            two_tiles(TT // 2 - 1)

        def before(t, i, o):
            return (t, i, o - 1) if o else (t - 1, 1 - i, 3)

        def value_block(i, j, h):
            rows = slice(h * NL, (h + 1) * NL)
            src = (v_f if j == h else v_swap)[rows, :]

            def heads(a):
                return a.rearrange("p (g h d) -> p g h d", h=2, d=SD)[:, :, h, :]
            return [heads(vz[i][p][rows, j, :]) for p in range(2)], heads(src)

        def own_columns(a):
            return a[:].rearrange("p o j (c n) -> p o (j c) n", c=2)[:, :, 0:4:3, :]

        def batches(a):
            return a[:].rearrange("p (o j n) -> p o j n", o=4, j=2)

        def output_block(o, q):
            rows = slice(32 * q, 32 * q + 32)
            return rows, ps_o[o % 2][rows, :].rearrange("p (j q n) -> p j q n", j=2, q=4)[:, :, q, :]

        @block.sync
        def _(sp):
            for n in names:
                sp.dma_start(w_f[n][:], env["c_w" + n].rearrange("(k p) n -> p k n", p=P)).then_inc(w_in[n], 16)
            for i, (dst, src) in enumerate(((cos, "cos"), (sin, "sin"), (bmask, "bmask"), (cmask_f, "cmask"))):
                sp.dma_start(dst[:], env[src]).then_inc(table_in[i], 16)

            def swap(t):
                sp.wait_ge(v_out, t + 1)
                wait_pos(sp, vz_low, t)
                for h in range(2):
                    sp.dma_start(v_swap[h * NL:(h + 1) * NL, :], v_f[(1 - h) * NL:(2 - h) * NL, :])\
                        .then_inc(v_swapped, 16)
            swap(0)
            with sp.Fori(1, TT) as t:
                swap(t)

        @block.gpsimd
        def _(pool):
            def inverse_deviation(t):
                wait_apart(pool, stats_ready, 2 * t + 2)
                pool.tensor_scalar(var[:], mv[:, 1:2], EPS, None, ALU.add).then_inc(var_ready, 1)
                pool.wait_ge(var_ready, t + 1)
                pool.tensor_tensor(rstd[:], var[:], minus_half[:], ALU.pow).then_inc(rstd_ready, 1)

            def rotate(t, n, turned, rot):
                pool.wait_ge(turned, t + 1)
                pool.tensor_tensor(rot_a[n][:], rot_a[n][:], rot_b[n][:], ALU.add).then_inc(rot, 1)

            def spread_keys(t, s):
                pool.wait_ge(kT_low, t + 1)
                wait_pos(pool, s_ps, 2 * (2 * t + s - 1))
                for p in range(2):
                    k = kT[p][:, 2 * s:2 * s + 2, :].rearrange("p a (j n) -> p (a j) n", j=2).bitcast(F32)
                    last = pool.tensor_tensor(kblk[s][p][:], k.unsqueeze(2).broadcast_to([P, 4, 4, NL]),
                                              bmask[:].unsqueeze(1).unsqueeze(3).broadcast_to([P, 4, 4, NL]), ALU.mult)
                last.then_inc(kblk_ready, 1)

            def low_values(t, i):
                pool.wait_ge(vz_high, t + 1)
                for h in range(2):
                    if h:
                        pool.wait_ge(kblk_ready, 2 * t + 2)
                        pool.wait_ge(vz_even, t + 1)
                    for j in range(2):
                        dst, src = value_block(i, j, h)
                        last = pool.tensor_tensor(dst[1], src, dst[0].bitcast(F32), ALU.subtract)
                    last.then_inc(vz_low if h else vz_even, 1)
                pool.wait_ge(vz_low, t + 1)

            for i in range(2):
                for p in range(2):
                    pool.memset(qz[i][p][:].bitcast(F32), 0.0)
                    last = pool.memset(vz[i][p][:].bitcast(F32), 0.0)
            last.then_inc(zeroed, 1)
            inverse_deviation(0)
            inverse_deviation(1)
            pool.wait_ge(table_in[2], 16)
            rotate(0, "k", k_turned, k_rot)
            rotate(0, "q", q_turned, q_rot)
            spread_keys(0, 0)
            spread_keys(0, 1)
            low_values(0, 0)

            def slot(t, i, o):
                if is_last(t):
                    return
                if o == 0:
                    rotate(t + 1, "k", k_turned, k_rot)
                    if has_two_after(t):
                        inverse_deviation(t + 2)
                if o == 1:
                    rotate(t + 1, "q", q_turned, q_rot)
                    spread_keys(t + 1, 0)
                if o == 2:
                    spread_keys(t + 1, 1)
                if o == 3:
                    low_values(t + 1, 1 - i)
            run(pool, slot)

        @block.scalar
        def _(act):
            def copy(out, in_):
                return act.activation(out, in_, ACT.Copy)

            def split_w(n):
                act.wait_ge(w_in[n], 16)
                copy(w[n][0][:], w_f[n][:]).then_inc(w_high, 1)

            def high_x(t):
                act.wait_ge(xT_ps, t + 1)
                wait_pos(act, vp_ps, t)
                copy(xT[0][:].rearrange("p k n -> p (k n)"), ps_t[:]).then_inc(xT_high, 1)

            def high_k(t):
                act.wait_ge(kT_ps, t + 1)
                wait_pos(act, kblk_ready, 2 * t)
                copy(kT[0][:].rearrange("p k n -> p (k n)"), ps_t[:]).then_inc(kT_high, 1)

            def high_q(t, i):
                act.wait_ge(qT_ps, t + 1)
                wait_pos(act, s_ps, 4 * (t - 1))
                copy(own_columns(qz[i][0]), batches(ps_t)).then_inc(qz_high, 1)

            def values_out(t):
                act.wait_ge(vp_ps, t + 1)
                wait_pos(act, vz_low, t)
                copy(v_f[:], ps_p[0][:]).then_inc(v_out, 1)

            def high_values(t, i):
                act.wait_ge(v_swapped, 32 * (t + 1))
                wait_pos(act, o_ps, 4 * (t - 1))
                for j in range(2):
                    for h in range(2):
                        dst, src = value_block(i, j, h)
                        last = copy(dst[0], src)
                last.then_inc(vz_high, 1)

            def exponential(m, b):
                act.wait_ge(sub_done, m + 1)
                act.activation(probs[b][:], probs[b][:], ACT.Exp, scale=float(SD) ** -0.5).then_inc(exp_done, 1)

            def high_probs(m):
                act.wait_ge(pT_ps, m + 1)
                wait_pos(act, o_ps, m)
                copy(pT[0][:].rearrange("p k n -> p (k n)"), ps_pt[:]).then_inc(pT_high, 1)

            def high_out(t, i, o):
                m = 4 * t + o
                act.wait_ge(o_ps, m + 1)
                if o == 0:
                    wait_pos(act, y_ps, t - 1)
                for q in range(4):
                    rows, src = output_block(o, q)
                    last = copy(oT[0][rows, i, o, :].rearrange("p (j n) -> p j n", j=2), src)
                last.then_inc(oT_high, 1)

            split_w("k")
            split_w("q")
            high_x(0)
            act.wait_ge(table_in[3], 16)
            copy(cmask[:], cmask_f[:])
            copy(ident_r[:], ident[:]).then_inc(tables, 1)
            split_w("v")
            act.wait_ge(zeroed, 1)
            high_k(0)
            high_q(0, 0)
            split_w("o")
            values_out(0)
            high_x(1)
            exponential(0, 0)
            exponential(1, 1)
            high_values(0, 0)

            def slot(t, i, o):
                m = 4 * t + o
                more = not is_last(t)
                high_probs(m)
                if o == 2 and more:
                    values_out(t + 1)
                if o == 3 and more:
                    high_values(t + 1, 1 - i)
                if not (isinstance(m, int) and m == 0):
                    high_out(*before(t, i, o))
                if o == 1 and more:
                    high_q(t + 1, 1 - i)
                if o == 2 and has_two_after(t):
                    high_x(t + 2)
                if more or o < 2:
                    exponential(m + 2, o % 2)
                if o == 0 and more:
                    high_k(t + 1)
            run(act, slot)
            high_out(TT - 1, 1, 3)

        @block.vector
        def _(dve):
            def sub(out, a, b):
                return dve.tensor_tensor(out, a, b.bitcast(F32), ALU.subtract)

            def low_w(n):
                dve.wait_ge(w_high, names.index(n) + 1)
                sub(w[n][1][:], w_f[n][:], w[n][0][:]).then_inc(w_low, 1)

            def statistics(t):
                wait_pos(dve, xn_ready, t)
                dve.bn_stats(stats[:], tile(t)).then_inc(stats_ready, 1)
                wait_apart(dve, stats_ready, 2 * t + 1)
                dve.bn_aggr(mv[:], stats[:]).then_inc(stats_ready, 1)

            def normalised(t):
                dve.wait_ge(rstd_ready, t + 1)
                wait_pos(dve, xT_ps, t)
                dve.tensor_scalar(xn[:], tile(t), mv[:, 0:1], rstd[:], ALU.subtract, ALU.mult).then_inc(xn_ready, 1)

            def flat(a):
                return a[:].rearrange("p k n -> p (k n)")

            def low_x(t):
                dve.wait_ge(xT_high, t + 1)
                sub(flat(xT[1]), ps_t[:], flat(xT[0])).then_inc(xT_low, 1)

            def turn(t, n, proj, bank, turned, rot_T):
                dve.wait_ge(proj, t + 1)
                wait_pos(dve, rot_T, t)
                heads = "p (h d) -> p h d"
                dve.tensor_tensor(rot_a[n][:].rearrange(heads, d=SD), bank[:].rearrange(heads, d=SD),
                                  cos[:].unsqueeze(1).broadcast_to([P, D // SD, SD]), ALU.mult)
                pairs = "p (h c e) -> p h c e"
                for e in range(2):
                    last = dve.tensor_tensor(
                        rot_b[n][:].rearrange(pairs, c=SD // 2, e=2)[:, :, :, e],
                        bank[:].rearrange(pairs, c=SD // 2, e=2)[:, :, :, 1 - e],
                        sin[:].rearrange("p (c e) -> p c e", e=2)[:, :, e].unsqueeze(1)
                        .broadcast_to([P, D // SD, SD // 2]), ALU.mult)
                last.then_inc(turned, 1)

            def low_k(t):
                dve.wait_ge(kT_high, t + 1)
                sub(flat(kT[1]), ps_t[:], flat(kT[0])).then_inc(kT_low, 1)

            def low_q(t, i):
                dve.wait_ge(qz_high, t + 1)
                sub(own_columns(qz[i][1]), batches(ps_t), own_columns(qz[i][0])).then_inc(qz_low, 1)

            def per_head(a, b):
                return a[:, b, :].unsqueeze(2).broadcast_to([P, 8, NL])

            def heads(a):
                return a[:].rearrange("p (h n) -> p h n", h=8)

            def subtract_max(m, b):
                dve.wait_ge(s_ps, m + 1)
                dve.tensor_reduce(nmax[:, b, :], heads(ps_s[b]), AX.X, ALU.max, negate=True).then_inc(max_ready, 1)
                dve.wait_ge(max_ready, m + 1)
                wait_pos(dve, pT_ps, m - 1)
                dve.tensor_tensor(heads(probs[b]), heads(ps_s[b]), per_head(nmax, b), ALU.add).then_inc(sub_done, 1)

            def divide_by_sum(m, b):
                dve.wait_ge(exp_done, m + 1)
                dve.tensor_reduce(psum_p[:, b, :], heads(probs[b]), AX.X, ALU.add).then_inc(sum_ready, 1)
                dve.wait_ge(sum_ready, m + 1)
                dve.reciprocal(rsum[:, b, :], psum_p[:, b, :]).then_inc(rsum_ready, 1)
                dve.wait_ge(rsum_ready, m + 1)
                dve.tensor_tensor(heads(probs[b]), heads(probs[b]), per_head(rsum, b), ALU.mult)\
                    .then_inc(probs_ready, 1)

            def low_probs(m):
                dve.wait_ge(pT_high, m + 1)
                sub(flat(pT[1]), ps_pt[:], flat(pT[0])).then_inc(pT_low, 1)

            def low_out(t, i, o):
                m = 4 * t + o
                dve.wait_ge(oT_high, m + 1)
                for q in range(4):
                    rows, src = output_block(o, q)
                    dst = [oT[p][rows, i, o, :].rearrange("p (j n) -> p j n", j=2) for p in range(2)]
                    last = sub(dst[1], src, dst[0])
                last.then_inc(oT_low, 1)

            def add_output(t):
                dve.wait_ge(y_ps, t + 1)
                dve.tensor_tensor(tile(t), ps_p[1][:], tile(t), ALU.add).then_inc(x_added, 1)

            statistics(0)
            normalised(0)
            statistics(1)
            low_w("k")
            low_x(0)
            low_w("q")
            normalised(1)
            for i in range(2):
                dve.wait_ge(table_in[i], 16)
            turn(0, "k", kp_ps, ps_p[0], k_turned, kT_ps)
            low_w("v")
            turn(0, "q", qp_ps, ps_p[1], q_turned, qT_ps)
            dve.wait_ge(zeroed, 1)
            low_k(0)
            low_q(0, 0)
            low_w("o")
            low_x(1)
            subtract_max(0, 0)
            subtract_max(1, 1)
            divide_by_sum(0, 0)
            turn(1, "k", kp_ps, ps_p[0], k_turned, kT_ps)

            def slot(t, i, o):
                m = 4 * t + o
                more = not is_last(t)
                if o == 1 and more:
                    low_k(t + 1)
                if more or o < 3:
                    divide_by_sum(m + 1, (o + 1) % 2)
                low_probs(m)
                if not (isinstance(m, int) and m == 0):
                    low_out(*before(t, i, o))
                if o == 3 and not (isinstance(t, int) and t == 0):
                    add_output(t - 1)
                if more or o < 2:
                    subtract_max(m + 2, o % 2)
                if o == 0 and has_two_after(t):
                    statistics(t + 2)
                if o == 0 and more:
                    turn(t + 1, "q", qp_ps, ps_p[1], q_turned, qT_ps)
                if o == 1 and more:
                    low_q(t + 1, 1 - i)
                if o == 1 and has_two_after(t):
                    normalised(t + 2)
                if o == 2 and has_two_after(t):
                    low_x(t + 2)
                if o == 3 and has_two_after(t):
                    turn(t + 2, "k", kp_ps, ps_p[0], k_turned, kT_ps)
            run(dve, slot)
            low_out(TT - 1, 1, 3)
            add_output(TT - 1)

        @block.tensor
        def _(pe):
            def turn_tile(src, done):
                for k in range(KT):
                    last = pe.transpose(ps_t[:, k * P:(k + 1) * P], src[:, k * P:(k + 1) * P], ident[:])
                last.then_inc(done, 1)

            def project(n, bank, done):
                ops = [(a, b, k) for a, b in PASSES for k in range(KT)]
                for c, (a, b, k) in enumerate(ops):
                    last = pe.matmul(bank[:], xT[a][:, k, :], w[n][b][:, k, :], start=(c == 0),
                                     stop=(c == len(ops) - 1))
                last.then_inc(done, 1)

            def x_turned(t):
                pe.wait_ge(xn_ready, t + 1)
                wait_pos(pe, qz_low, t)
                turn_tile(xn, xT_ps)

            def k_project(t):
                pe.wait_ge(xT_low, t + 1)
                wait_pos(pe, v_out, t)
                project("k", ps_p[0], kp_ps)

            def q_project(t):
                wait_pos(pe, x_added, t - 2)
                project("q", ps_p[1], qp_ps)

            def v_project(t):
                pe.wait_ge(k_turned, t + 1)
                project("v", ps_p[0], vp_ps)

            def k_turn(t):
                pe.wait_ge(k_rot, t + 1)
                pe.wait_ge(xT_low, t + 1)
                turn_tile(rot_a["k"], kT_ps)

            def q_turn(t):
                pe.wait_ge(q_rot, t + 1)
                pe.wait_ge(kT_low, t + 1)
                turn_tile(rot_a["q"], qT_ps)

            def scores(t, i, o):
                m, s, b = 4 * t + o, o // 2, o % 2
                rows = slice(b * NL, (b + 1) * NL)
                if o % 2 == 0:
                    pe.wait_ge(kblk_ready, 2 * t + s + 1)
                if o == 0:
                    pe.wait_ge(qz_low, t + 1)
                wait_pos(pe, sub_done, m - 1)
                pe.matmul(ps_s[b][:], ident_r[:], cmask[:], start=True, stop=False, skip_group_check=True)
                ops = [(x, j, p, r) for x in range(2) for j in range(2) for p, r in PASSES]
                for c, (x, j, p, r) in enumerate(ops):
                    last = pe.matmul(ps_s[b][:, x * 256:(x + 1) * 256], qz[i][p][rows, 2 * s + x, j, :],
                                     kblk[s][r][rows, 2 * x + j, :, :].rearrange("p h n -> p (h n)"), start=False,
                                     stop=(c == len(ops) - 1), skip_group_check=True)
                last.then_inc(s_ps, 1)

            def probs_turned(m, b):
                pe.wait_ge(probs_ready, m + 1)
                wait_pos(pe, pT_low, m)
                for q in range(4):
                    last = pe.transpose(ps_pt[:, q * P:(q + 1) * P], probs[b][:, q * P:(q + 1) * P], ident[:])
                last.then_inc(pT_ps, 1)

            def outputs(t, i, o):
                m = 4 * t + o
                pe.wait_ge(pT_low, m + 1)
                if o == 0:
                    pe.wait_ge(vz_low, t + 1)
                wait_pos(pe, oT_low, m - 1)
                for j in range(2):
                    for c, (a, b) in enumerate(PASSES):
                        last = pe.matmul(ps_o[o % 2][:, j * 256:(j + 1) * 256], vz[i][a][:, j, o * P:(o + 1) * P],
                                         pT[b][:, :, j * NL:(j + 1) * NL], start=(c == 0), stop=(c == 2))
                last.then_inc(o_ps, 1)

            def output_product(t, i):
                pe.wait_ge(oT_low, 4 * (t + 1))
                if isinstance(t, int) and t + 3 > TT:
                    pe.wait_ge(x_added, t)
                else:
                    pe.wait_ge(q_turned, t + 3)
                for c, (a, b, k) in enumerate([(a, b, k) for a, b in PASSES for k in range(4)]):
                    last = pe.matmul(ps_p[1][:], oT[a][:, i, k, :], w["o"][b][:, k, :], start=(c == 0), stop=(c == 11))
                last.then_inc(y_ps, 1)

            x_turned(0)
            pe.wait_ge(w_low, 1)
            k_project(0)
            pe.wait_ge(w_low, 2)
            q_project(0)
            k_turn(0)
            pe.wait_ge(w_low, 3)
            v_project(0)
            q_turn(0)
            x_turned(1)
            pe.wait_ge(tables, 1)
            scores(0, 0, 0)
            scores(0, 0, 1)
            k_project(1)
            pe.wait_ge(w_low, 4)

            def slot(t, i, o):
                more = not is_last(t)
                probs_turned(4 * t + o, o % 2)
                if o < 2:
                    scores(t, i, o + 2)
                elif more:
                    scores(t + 1, 1 - i, o - 2)
                if o == 0 and more:
                    q_project(t + 1)
                    k_turn(t + 1)
                if o == 1 and more:
                    q_turn(t + 1)
                    v_project(t + 1)
                if o == 2:
                    if has_two_after(t):
                        x_turned(t + 2)
                    if not (isinstance(t, int) and t == 0):
                        output_product(t - 1, 1 - i)
                if o == 3 and has_two_after(t):
                    k_project(t + 2)
                outputs(t, i, o)
            run(pe, slot)
            output_product(TT - 1, 1)


def stage_experts(nc, env):
    ctx = ExitStack()
    with ctx:
        def sb(name, shape, dt=F32):
            return ctx.enter_context(nc.sbuf_tensor(name, shape, dt))

        def ps(name):
            return ctx.enter_context(nc.psum_tensor(name, [P, 512], F32))

        def sem(name):
            return ctx.enter_context(nc.semaphore(name))

        x1, ident, minus_half = env["x1"], env["ident"], env["minus_half"]
        rw_f = sb("rw_f", [P, KT, E])
        rw = [sb(f"rw_{p}", [P, KT, E], F32R) for p in "hl"]
        eb_f = sb("eb_f", [E, D])
        eb = [sb(f"eb_{p}", [E, D], F32R) for p in "hl"]
        rbias = sb("rbias", [P, E])
        stats, mv = sb("d_stats", [P, 6]), sb("d_mv", [P, 2])
        var, rstd = sb("d_var", [P, 1]), sb("d_rstd", [P, 1])
        xn = sb("d_xn", [P, 2, D])
        xT = [sb(f"d_xT_{p}", [P, KT, P], F32R) for p in "hl"]
        logits, probs, rest, chosen = (sb(n, [P, E]) for n in ("logits", "d_probs", "rest", "chosen"))
        nmax, psum_p, rsum, wsum = (sb(n, [P, 1]) for n in ("d_nmax", "d_psum", "d_rsum", "wsum"))
        top = sb("top", [P, 8])
        wT = [sb(f"wT_{p}", [E, P], F32R) for p in "hl"]
        y = sb("y", [P, 2, D])
        ps_t, ps_l, ps_w, ps_y = ps("d_ps_t"), ps("d_ps_l"), ps("d_ps_w"), ps("d_ps_y")

        w_in = [sem(f"d_w_in{i}") for i in range(3)]
        stored = [sem(f"stored{i}") for i in range(2)]
        w_high, w_low = sem("d_w_high"), sem("d_w_low")
        stats_ready = sem("d_stats_ready")
        var_ready, rstd_ready = sem("d_var_ready"), sem("d_rstd_ready")
        xn_ready = sem("d_xn_ready")
        xT_ps, xT_high, xT_low = sem("d_xT_ps"), sem("d_xT_high"), sem("d_xT_low")
        l_ps = sem("l_ps")
        steps = sem("d_steps")
        exp_done = sem("d_exp_done")
        chosen_ready = sem("chosen_ready")
        wT_ps, wT_high, wT_low = sem("wT_ps"), sem("wT_high"), sem("wT_low")
        y_ps, y_part, y_ready = sem("d_y_ps"), sem("y_part"), sem("y_ready")
        block = ctx.enter_context(nc.Block())

        def tile(t):
            return x1[:, bass.ds(t, 1), :].rearrange("p t d -> p (t d)")

        def run(eng, slot):
            def two_tiles(tb):
                for i in range(2):
                    slot(2 * tb + i, i)
            two_tiles(0)
            with eng.Fori(1, TT // 2 - 1) as tb:
                two_tiles(tb)
            two_tiles(TT // 2 - 1)

        def exists(t):
            return not isinstance(t, int) or t < TT

        @block.sync
        def _(sp):
            sp.dma_start(rw_f[:], env["router_wT"].rearrange("(k p) e -> p k e", p=P)).then_inc(w_in[0], 16)
            sp.dma_start(eb_f[:], env["expert_bias"]).then_inc(w_in[1], 16)
            sp.dma_start(rbias[:], env["router_bias"].unsqueeze(0).broadcast_to([P, E])).then_inc(w_in[2], 16)

            def store(t, i):
                sp.wait_ge(y_ready, t + 1)
                sp.dma_start(env["out"][bass.ds(t, 1)].rearrange("t p d -> p (t d)"), y[:, i, :])\
                    .then_inc(stored[i], 16)
            run(sp, store)
            for i in range(2):
                sp.wait_ge(stored[i], 16 * (TT // 2))

        @block.gpsimd
        def _(pool):
            def inverse_deviation(t):
                wait_apart(pool, stats_ready, 2 * t + 2)
                pool.tensor_scalar(var[:], mv[:, 1:2], EPS, None, ALU.add).then_inc(var_ready, 1)
                pool.wait_ge(var_ready, t + 1)
                pool.tensor_tensor(rstd[:], var[:], minus_half[:], ALU.pow).then_inc(rstd_ready, 1)
            inverse_deviation(0)
            with pool.Fori(1, TT) as t:
                inverse_deviation(t)

        @block.scalar
        def _(act):
            def copy(out, in_):
                return act.activation(out, in_, ACT.Copy)

            def high_x(t):
                act.wait_ge(xT_ps, t + 1)
                wait_pos(act, l_ps, t)
                copy(xT[0][:].rearrange("p k n -> p (k n)"), ps_t[:]).then_inc(xT_high, 1)

            act.wait_ge(w_in[0], 16)
            copy(rw[0][:], rw_f[:]).then_inc(w_high, 1)
            act.wait_ge(w_in[1], 16)
            copy(eb[0][:], eb_f[:]).then_inc(w_high, 1)
            high_x(0)

            def slot(t, i):
                act.wait_ge(steps, 7 * t + 2)
                act.activation(probs[:], logits[:], ACT.Exp, bias=nmax[:], accum_out=psum_p[:]).then_inc(exp_done, 1)
                if exists(t + 1):
                    high_x(t + 1)
                act.wait_ge(wT_ps, t + 1)
                wait_pos(act, y_ps, t)
                copy(wT[0][:], ps_w[0:E, 0:P]).then_inc(wT_high, 1)
            run(act, slot)

        @block.vector
        def _(dve):
            def sub(out, a, b):
                return dve.tensor_tensor(out, a, b.bitcast(F32), ALU.subtract)

            def statistics(t):
                wait_pos(dve, xn_ready, t)
                dve.bn_stats(stats[:], tile(t)).then_inc(stats_ready, 1)
                wait_apart(dve, stats_ready, 2 * t + 1)
                dve.bn_aggr(mv[:], stats[:]).then_inc(stats_ready, 1)

            def normalised(t, i):
                dve.wait_ge(rstd_ready, t + 1)
                wait_pos(dve, y_part, t - 1)
                dve.tensor_scalar(xn[:, i, :], tile(t), mv[:, 0:1], rstd[:], ALU.subtract, ALU.mult)\
                    .then_inc(xn_ready, 1)

            def low_x(t):
                dve.wait_ge(xT_high, t + 1)
                sub(xT[1][:].rearrange("p k n -> p (k n)"), ps_t[:], xT[0][:].rearrange("p k n -> p (k n)"))\
                    .then_inc(xT_low, 1)

            statistics(0)
            normalised(0, 0)
            statistics(1)
            dve.wait_ge(w_high, 1)
            sub(rw[1][:], rw_f[:], rw[0][:]).then_inc(w_low, 1)
            low_x(0)
            normalised(1, 1)
            dve.wait_ge(w_high, 2)
            sub(eb[1][:], eb_f[:], eb[0][:]).then_inc(w_low, 1)
            dve.wait_ge(w_in[2], 16)

            def slot(t, i):
                def step(n, instruction):
                    instruction.then_inc(steps, 1)
                    wait_apart(dve, steps, 7 * t + n)

                dve.wait_ge(l_ps, t + 1)
                wait_pos(dve, exp_done, t)
                step(1, dve.tensor_tensor(logits[:], ps_l[:, 0:E], rbias[:], ALU.add))
                dve.tensor_reduce(nmax[:], logits[:], AX.X, ALU.max, negate=True).then_inc(steps, 1)
                if exists(t + 2):
                    statistics(t + 2)
                dve.wait_ge(exp_done, t + 1)
                step(3, dve.reciprocal(rsum[:], psum_p[:]))
                step(4, dve.tensor_scalar(probs[:], probs[:], rsum[:], None, ALU.mult))
                step(5, dve.max(top[:], probs[:]))
                step(6, dve.match_replace(rest[:], top[:], probs[:], 0.0))
                wait_pos(dve, wT_ps, t)
                dve.tensor_tensor(chosen[:], probs[:], rest[:], ALU.subtract).then_inc(chosen_ready, 1)
                step(7, dve.tensor_reduce(wsum[:], top[:], AX.X, ALU.add))
                if exists(t + 1):
                    low_x(t + 1)
                wait_pos(dve, stored[i], 16 * (t // 2))
                dve.scalar_tensor_tensor(y[:, i, :], xn[:, i, :], wsum[:], tile(t), ALU.mult, ALU.add)\
                    .then_inc(y_part, 1)
                dve.wait_ge(wT_high, t + 1)
                sub(wT[1][:], ps_w[0:E, 0:P], wT[0][:]).then_inc(wT_low, 1)
                if exists(t + 2):
                    normalised(t + 2, i)
                dve.wait_ge(y_ps, t + 1)
                dve.wait_ge(y_part, t + 1)
                dve.tensor_tensor(y[:, i, :], y[:, i, :], ps_y[:], ALU.add).then_inc(y_ready, 1)
            run(dve, slot)

        @block.tensor
        def _(pe):
            def x_turned(t, i):
                pe.wait_ge(xn_ready, t + 1)
                wait_pos(pe, xT_low, t)
                for k in range(KT):
                    last = pe.transpose(ps_t[:, k * P:(k + 1) * P], xn[:, i, k * P:(k + 1) * P], ident[:])
                last.then_inc(xT_ps, 1)

            def router(t):
                pe.wait_ge(xT_low, t + 1)
                wait_pos(pe, steps, 7 * (t - 1) + 1)
                for c, (a, b, k) in enumerate([(a, b, k) for a, b in PASSES for k in range(KT)]):
                    last = pe.matmul(ps_l[:, 0:E], xT[a][:, k, :], rw[b][:, k, :], start=(c == 0), stop=(c == 11))
                last.then_inc(l_ps, 1)

            x_turned(0, 0)
            pe.wait_ge(w_low, 1)
            router(0)
            pe.wait_ge(w_low, 2)

            def slot(t, i):
                if exists(t + 1):
                    x_turned(t + 1, 1 - i)
                wait_apart(pe, chosen_ready, t + 1)
                wait_pos(pe, wT_low, t)
                pe.transpose(ps_w[0:E, 0:P], chosen[:], ident[:]).then_inc(wT_ps, 1)
                if exists(t + 1):
                    router(t + 1)
                pe.wait_ge(wT_low, t + 1)
                wait_pos(pe, y_ready, t)
                for c, (a, b) in enumerate(PASSES):
                    last = pe.matmul(ps_y[:], wT[a][:], eb[b][:], start=(c == 0), stop=(c == 2))
                last.then_inc(y_ps, 1)
            run(pe, slot)


def build(nc, **env):
    with ExitStack() as ctx:
        def sb(name, shape, dt=F32):
            return ctx.enter_context(nc.sbuf_tensor(name, shape, dt))
        env["ident"] = sb("ident", [P, P])
        env["minus_half"] = sb("minus_half", [P, 1])
        env["x1"] = sb("x1", [P, TT, D])
        with ExitStack() as latents_kept:
            env["xnT"] = [latents_kept.enter_context(nc.sbuf_tensor(f"xnT_{n}", [P, KT, TT * P], F32R)) for n in "hl"]
            stage_keys_values(nc, env)
            stage_cross_attention(nc, env)
        stage_self_attention(nc, env)
        stage_experts(nc, env)


def kernel(**inputs):
    import concourse.bacc as bacc
    from concourse.bass_utils import run_bass_kernel_spmd

    a = {n: np.asarray(v) for n, v in inputs.items()}
    order = np.arange(D).reshape(2, 2, 2, 4, SD).transpose(0, 2, 1, 3, 4).reshape(-1)
    half = np.arange(P) % NL
    angle = np.outer(half, 1.0 / 10000.0 ** (np.arange(0, SD, 2).astype(np.float32) / SD)).astype(np.float32)
    arrays = dict(
        x=a["x"].reshape(TT, P, D),
        ctxT=a["ctx_4096"].reshape(TT, 2, NC, KT, P).transpose(0, 4, 3, 1, 2).reshape(TT, P, KT * 2 * NC),
        wq=a["L0_xattn_Wq"].reshape(KT, P, HK * G, HD).transpose(2, 1, 0, 3).reshape(HK * G, P, KT * HD),
        wk=a["L0_xattn_Wk"], wv=a["L0_xattn_Wv"], wo=a["L0_xattn_Wo"],
        c_wq=a["L0_attn_wq"], c_wk=a["L0_attn_wk"], c_wv=a["L0_attn_wv"][:, order], c_wo=a["L0_attn_wo"][order],
        router_wT=a["L0_ffn_router_weight"].T, router_bias=a["L0_ffn_router_bias"],
        expert_bias=a["L0_ffn_expert_bias"],
        cos=np.repeat(np.cos(angle), 2, axis=1),
        sin=np.repeat(np.sin(angle), 2, axis=1) * np.tile(np.array([-1, 1], np.float32), SD // 2),
        bmask=(half[:, None] // SD == np.arange(4)).astype(np.float32),
        cmask=np.tile(np.where(half[:, None] >= np.arange(NL), 0, -1e30).astype(np.float32), (1, 8)),
    )
    arrays = {n: np.ascontiguousarray(v) for n, v in arrays.items()}
    nc = bacc.Bacc("TRN2", target_bir_lowering=False, num_devices=1)
    env = {n: nc.dram_tensor(f"in_{n}", v.shape, mybir.dt.from_np(v.dtype), kind="ExternalInput").ap()
           for n, v in arrays.items()}
    env["kv_dram"] = nc.dram_tensor("kv_dram", (TT, P, HK * KV), F32, kind="Internal").ap()
    env["out"] = nc.dram_tensor("out", (TT, P, D), F32, kind="ExternalOutput").ap()
    build(nc, **env)
    r = run_bass_kernel_spmd(nc, [{f"in_{n}": v for n, v in arrays.items()}], core_ids=[0])
    return r.results[0]["out"].reshape(B, NL, D)
```

```python
from contextlib import ExitStack

import concourse.bass as bass
from concourse import mybir
import numpy as np

F32 = mybir.dt.float32
F32R = mybir.dt.float32r
ALU = mybir.AluOpType
ACT = mybir.ActivationFunctionType
AX = mybir.AxisListType

P = 128
D = 512
KT = D // P
B, NL, NC = 16, 64, 128
NK = NL + NC
TT = B * NL // P
HK, G, HD = 4, 8, 128
XS = float(HD) ** -0.5
SD = 16
E = 64
KV = 2 * NK + 3 * HD
EPS = 1e-5
PASSES = ((0, 0), (0, 1), (1, 0))


def wait_pos(eng, sem, value):
    if isinstance(value, int) and value <= 0:
        return
    eng.wait_ge(sem, value)


def wait_apart(eng, sem, value):
    if not isinstance(value, int):
        value = eng.to_reg(value)
        eng.wait_ge(sem, 1)
    wait_pos(eng, sem, value)


def contexts(seq):
    return seq[:].rearrange("p k (c n) -> p k c n", c=3)[:, :, 0:3:2, :]


def latents(seq):
    return seq[:, :, NC:NC + P]


def load_wq(sp, env, c, i):
    wait_pos(sp, env["wq_low"], c - 1)
    row = (c // (2 * G)) * G + c % G
    sp.dma_start(env["wq_f"][:, i], env["wq"][bass.ds(row, 1)].rearrange("r p (k d) -> p (r k) d", k=KT))\
        .then_inc(env["wq_in"][i], 16)


def high_wq(act, env, c, i, uses):
    act.wait_ge(env["wq_in"][i], 16 * uses)
    wait_pos(act, env["q_ps"], c - 1)
    act.activation(env["wq_split"][0][:, i], env["wq_f"][:, i], ACT.Copy).then_inc(env["wq_high"], 1)


def low_wq(dve, env, c, i):
    dve.wait_ge(env["wq_high"], c + 1)
    dve.tensor_tensor(env["wq_split"][1][:, i], env["wq_f"][:, i], env["wq_split"][0][:, i].bitcast(F32),
                      ALU.subtract).then_inc(env["wq_low"], 1)


def stage_keys_values(nc, env):
    ctx = ExitStack()
    with ctx:
        def sb(name, shape, dt=F32):
            return ctx.enter_context(nc.sbuf_tensor(name, shape, dt))

        def ps(name):
            return ctx.enter_context(nc.psum_tensor(name, [P, 512], F32))

        def sem(name):
            return ctx.enter_context(nc.semaphore(name))

        x1, xnT, ident = env["x1"], env["xnT"], env["ident"]
        wk_f = sb("wk_f", [P, KT, D])
        wv_f = sb("wv_f", [P, KT, D])
        wk = [sb(f"wk_{n}", [P, KT, D], F32R) for n in "hl"]
        wv = [sb(f"wv_{n}", [P, KT, D], F32R) for n in "hl"]
        ctx_f = [sb(f"ctx_f{i}", [P, KT, 2, NC]) for i in range(2)]
        seq = [[sb(f"seq{i}_{n}", [P, KT, 2 * NK], F32R) for n in "hl"] for i in range(2)]
        stats = sb("a_stats", [P, 2, 6])
        mv = sb("a_mv", [P, 2, 2])
        var = sb("a_var", [P, 2, 1])
        rstd = sb("a_rstd", [P, 2, 1])
        minus_half = env["minus_half"]
        xn = sb("a_xn", [P, 2, D])
        kv = [sb(f"kv_out{i}", [P, HK, KV]) for i in range(2)]
        first, second, all_k = slice(0, KT // 2), slice(KT // 2, KT), slice(0, KT)
        weight_parts = ((wv_f[:, first], first, env["wv"]), (wv_f[:, second], second, env["wv"]),
                        (wk_f[:], all_k, env["wk"]))
        split_parts = [[w[:, rows] for w in ws] for ws, rows in ((wv, first), (wv, second), (wk, all_k))]
        ps_t = ps("a_ps_t")
        ps_k = [ps(f"a_ps_k{i}") for i in range(2)]
        ps_v = [ps(f"a_ps_v{i}") for i in range(3)]

        ident_ready = sem("ident_ready")
        w_in = [sem(f"a_w_in{i}") for i in range(3)]
        x_in = [sem(f"a_x_in{i}") for i in range(2)]
        ctx_in = [sem(f"a_ctx_in{i}") for i in range(2)]
        kv_stored = env["kv_stored"]
        w_high = sem("a_w_high")
        w_low = sem("a_w_low")
        ln_steps = sem("a_ln_steps")
        var_ready = sem("a_var_ready")
        rstd_ready = sem("a_rstd_ready")
        xn_ready = sem("a_xn_ready")
        xnT_ps = sem("a_xnT_ps")
        ctx_high = sem("a_ctx_high")
        ctx_low = sem("a_ctx_low")
        lat_high = sem("a_lat_high")
        lat_low = sem("a_lat_low")
        lat_kept = sem("a_lat_kept")
        k_ps = sem("a_k_ps")
        v_ps = sem("a_v_ps")
        k_out = sem("a_k_out")
        v_out = sem("a_v_out")
        block = ctx.enter_context(nc.Block())

        @block.sync
        def _(sp):
            def load(t, i):
                wait_pos(sp, xn_ready, t - 1)
                sp.dma_start(x1[:, bass.ds(t, 1), :], env["x"][bass.ds(t, 1)].rearrange("t p d -> p t d"))\
                    .then_inc(x_in[i], 16)
                wait_pos(sp, ctx_low, t - 1)
                sp.dma_start(ctx_f[i][:], env["ctxT"][bass.ds(t, 1)].rearrange("t p c -> p (t c)")
                             .rearrange("p (k b n) -> p k b n", k=KT, b=2)).then_inc(ctx_in[i], 16)

            def store(t, i):
                wait_apart(sp, k_out, HK * (t + 1))
                sp.wait_ge(v_out, 3 * (t + 1))
                sp.dma_start(env["kv_dram"][bass.ds(t, 1)].rearrange("t p c -> p (t c)"),
                             kv[i][:].rearrange("p h c -> p (h c)")).then_inc(kv_stored[i], 16)

            load(0, 0)
            for n, (f, rows, w) in enumerate(weight_parts):
                sp.dma_start(f, w.rearrange("(k p) n -> p k n", p=P)[:, rows, :]).then_inc(w_in[n], 16)
            load(1, 1)
            with sp.Fori(0, TT // 2 - 1) as tb:
                for i in range(2):
                    load(2 * tb + 2 + i, i)
                    store(2 * tb + i, i)
            load_wq(sp, env, 0, 0)
            load_wq(sp, env, 1, 1)
            for i in range(2):
                store(TT - 2 + i, i)
            load_wq(sp, env, 2, 0)
            load_wq(sp, env, 3, 1)

        @block.gpsimd
        def _(pool):
            pool.memset(ident[:], 0.0).then_inc(ident_ready, 1)
            pool.wait_ge(ident_ready, 1)
            pool.affine_select(out=ident[:], in_=ident[:], compare_op=ALU.not_equal, fill=1.0, base=0,
                               pattern=[[-1, P]], channel_multiplier=1).then_inc(ident_ready, 1)
            pool.memset(minus_half[:], -0.5).then_inc(ident_ready, 1)
            def inverse_deviation(t, i):
                wait_apart(pool, ln_steps, 2 * t + 2)
                pool.tensor_scalar(var[:, i, :], mv[:, i, 1:2], EPS, None, ALU.add).then_inc(var_ready, 1)
                pool.wait_ge(var_ready, t + 1)
                pool.tensor_tensor(rstd[:, i, :], var[:, i, :], minus_half[:], ALU.pow).then_inc(rstd_ready, 1)

            def keep_latents(t, i):
                pool.wait_ge(lat_low, t + 1)
                for n in range(2):
                    last = pool.tensor_copy(xnT[n][:, :, bass.ds(t * P, P)], latents(seq[i][n]).bitcast(F32))
                last.then_inc(lat_kept, 1)

            pool.wait_ge(ident_ready, 3)
            inverse_deviation(0, 0)
            inverse_deviation(1, 1)
            with pool.Fori(0, TT // 2 - 1) as tb:
                for i in range(2):
                    inverse_deviation(2 * tb + 2 + i, i)
                    keep_latents(2 * tb + i, i)
            keep_latents(TT - 2, 0)
            keep_latents(TT - 1, 1)

        @block.scalar
        def _(act):
            def split_ctx(tb, i):
                t = 2 * tb + i
                act.wait_ge(ctx_in[i], 16 * (tb + 1))
                wait_pos(act, v_ps, 3 * (t - 1))
                act.activation(contexts(seq[i][0]), ctx_f[i][:], ACT.Copy).then_inc(ctx_high, 1)

            def split_latents(tb, i):
                t = 2 * tb + i
                act.wait_ge(xnT_ps, t + 1)
                wait_pos(act, lat_kept, t - 1)
                act.activation(latents(seq[i][0]), ps_t[:].rearrange("p (k n) -> p k n", k=KT),
                               ACT.Copy).then_inc(lat_high, 1)

            def values_out(tb, i, cs):
                t = 2 * tb + i
                wait_pos(act, kv_stored[i], 16 * tb)
                for c in cs:
                    act.wait_ge(v_ps, 3 * t + c + 1)
                    act.activation(kv[i][:, :, 2 * NK + c * HD:2 * NK + (c + 1) * HD],
                                   ps_v[c][:].rearrange("p (h d) -> p h d", h=HK), ACT.Copy).then_inc(v_out, 1)

            split_ctx(0, 0)
            for n, (f, _, _) in enumerate(weight_parts):
                act.wait_ge(w_in[n], 16)
                act.activation(split_parts[n][0], f, ACT.Copy).then_inc(w_high, 1)
            split_latents(0, 0)
            split_ctx(0, 1)

            def two_tiles(tb):
                for i in range(2):
                    values_out(tb, i, (0,))
                    split_latents(tb + i, 1 - i)
                    values_out(tb, i, (1, 2))
                    split_ctx(tb + 1, i)

            two_tiles(0)
            with act.Fori(1, TT // 2 - 1) as tb:
                two_tiles(tb)
            values_out(TT // 2 - 1, 0, (0,))
            split_latents(TT // 2 - 1, 1)
            values_out(TT // 2 - 1, 0, (1, 2))
            for c in range(2):
                high_wq(act, env, c, c, 1)
            values_out(TT // 2 - 1, 1, (0, 1, 2))

        @block.vector
        def _(dve):
            def layernorm(tb, i):
                t = 2 * tb + i
                dve.wait_ge(x_in[i], 16 * (tb + 1))
                wait_pos(dve, xnT_ps, t - 1)
                xt = x1[:, bass.ds(t, 1), :].rearrange("p t d -> p (t d)")
                dve.bn_stats(stats[:, i, :], xt).then_inc(ln_steps, 1)
                wait_apart(dve, ln_steps, 2 * t + 1)
                dve.bn_aggr(mv[:, i, :], stats[:, i, :]).then_inc(ln_steps, 1)
                dve.wait_ge(rstd_ready, t + 1)
                dve.tensor_scalar(xn[:, i, :], xt, mv[:, i, 0:1], rstd[:, i, :], ALU.subtract, ALU.mult)\
                    .then_inc(xn_ready, 1)

            def split_ctx(tb, i):
                t = 2 * tb + i
                dve.wait_ge(ctx_high, t + 1)
                dve.tensor_tensor(contexts(seq[i][1]), ctx_f[i][:], contexts(seq[i][0]).bitcast(F32),
                                  ALU.subtract).then_inc(ctx_low, 1)

            def split_latents(tb, i):
                t = 2 * tb + i
                dve.wait_ge(lat_high, t + 1)
                dve.tensor_tensor(latents(seq[i][1]), ps_t[:].rearrange("p (k n) -> p k n", k=KT),
                                  latents(seq[i][0]).bitcast(F32), ALU.subtract).then_inc(lat_low, 1)

            def keys_out(tb, i):
                t = 2 * tb + i
                wait_pos(dve, kv_stored[i], 16 * tb)
                for h in range(HK):
                    dve.wait_ge(k_ps, HK * t + h + 1)
                    dve.tensor_copy(kv[i][:, h, 0:2 * NK], ps_k[h % 2][:, 0:2 * NK]).then_inc(k_out, 1)

            layernorm(0, 0)
            split_ctx(0, 0)
            for n, (f, _, _) in enumerate(weight_parts):
                high, low = split_parts[n]
                dve.wait_ge(w_high, n + 1)
                dve.tensor_tensor(low, f, high.bitcast(F32), ALU.subtract).then_inc(w_low, 1)
            split_latents(0, 0)
            layernorm(0, 1)
            split_ctx(0, 1)

            def two_tiles(tb):
                for i in range(2):
                    split_latents(tb + i, 1 - i)
                    keys_out(tb, i)
                    layernorm(tb + 1, i)
                    split_ctx(tb + 1, i)

            two_tiles(0)
            with dve.Fori(1, TT // 2 - 1) as tb:
                two_tiles(tb)
            split_latents(TT // 2 - 1, 1)
            keys_out(TT // 2 - 1, 0)
            for c in range(2):
                low_wq(dve, env, c, c)
            keys_out(TT // 2 - 1, 1)

        @block.tensor
        def _(pe):
            def transposes(t, i):
                pe.wait_ge(xn_ready, t + 1)
                wait_pos(pe, lat_low, t)
                for k in range(KT):
                    last = pe.transpose(ps_t[:, k * P:(k + 1) * P], xn[:, i, k * P:(k + 1) * P], ident[:])
                last.then_inc(xnT_ps, 1)

            def value(t, i, c, first=False):
                wait_pos(pe, v_out, 3 * (t - 1) + c + 1)
                n = 0
                for a, b in PASSES:
                    if first and b == 1:
                        pe.wait_ge(w_low, 2)
                    for k in range(KT):
                        last = pe.matmul(ps_v[c][:], seq[i][a][:, k, (0, 2 * P, P)[c]:][:, 0:P], wv[b][:, k, :], start=(n == 0), stop=(n == 3 * KT - 1))
                        n += 1
                last.then_inc(v_ps, 1)

            def keys(t, i, h):
                wait_pos(pe, k_out, HK * t + h - 1)
                n = 0
                for a, b in PASSES:
                    for k in range(KT):
                        last = pe.matmul(ps_k[h % 2][:, 0:2 * NK], wk[a][:, k, h * HD:(h + 1) * HD],
                                         seq[i][b][:, k, :], start=(n == 0), stop=(n == 3 * KT - 1))
                        n += 1
                last.then_inc(k_ps, 1)

            def step(t, i, first=False, last=False):
                pe.wait_ge(ctx_low, t + 1)
                if first:
                    pe.wait_ge(w_high, 2)
                value(t, i, 0, first)
                if not (first or last):
                    transposes(t + 1, 1 - i)
                value(t, i, 1)
                if first:
                    transposes(t + 1, 1 - i)
                if first:
                    pe.wait_ge(w_low, 3)
                pe.wait_ge(lat_low, t + 1)
                for h in range(HK):
                    keys(t, i, h)
                value(t, i, 2)

            pe.wait_ge(ident_ready, 2)
            transposes(0, 0)
            step(0, 0, first=True)
            step(1, 1)
            with pe.Fori(1, TT // 2 - 1) as tb:
                for i in range(2):
                    step(2 * tb + i, i)
            step(TT - 2, 0)
            step(TT - 1, 1, last=True)


def stage_cross_attention(nc, env):
    ctx = ExitStack()
    with ctx:
        def sb(name, shape, dt=F32):
            return ctx.enter_context(nc.sbuf_tensor(name, shape, dt))

        def ps(name):
            return ctx.enter_context(nc.psum_tensor(name, [P, 512], F32))

        def sem(name):
            return ctx.enter_context(nc.semaphore(name))

        HALF = TT // 2
        HT = HALF * P
        STEPS = HK * B
        BODIES = STEPS // 4
        VO = 2 * NK
        WO_RING = G + 4

        x1, xnT, ident = env["x1"], env["xnT"], env["ident"]
        wq = env["wq_split"]
        wo_f = sb("wo_f", [P, 2, D])
        wo = [sb(f"wo_{n}", [P, WO_RING, D], F32R) for n in "hl"]
        kv_f = sb("kv_f", [P, 2, KV])
        kv = [sb(f"kv_{n}", [P, 2, KV], F32R) for n in "hl"]
        q_all = sb("q_all", [P, 2, G, HT])
        q = [sb(f"q_{n}", [P, 2, G, NL], F32R) for n in "hl"]
        probs = [sb(f"probs{i}", [P, NL + 4 * NK]) for i in range(2)]
        pT_ctx = [sb(f"pT_ctx_{n}", [P, 512], F32R) for n in "hl"]
        pT_lat = [sb(f"pT_lat_{n}", [P, 512], F32R) for n in "hl"]
        oT = [sb(f"oT_{n}", [P, 2, G, P], F32R) for n in "hl"]
        nmax = sb("nmax", [P, 2, 4])
        psum_p = sb("psum_p", [P, 2, 4])
        rsum = sb("rsum", [P, 2, 4])
        ps_q = [ps(f"ps_q{i}") for i in range(2)]
        ps_s = [ps(f"ps_s{i}") for i in range(2)]
        ps_tc, ps_tl, ps_o, ps_y = ps("ps_tc"), ps("ps_tl"), ps("ps_o"), ps("ps_y")

        wo_in = [sem(f"wo_in{i}") for i in range(2)]
        kv_in = [sem(f"kv_in{i}") for i in range(2)]
        wq_low, q_ps = env["wq_low"], env["q_ps"]
        wo_high, wo_low = sem("wo_high"), sem("wo_low")
        kv_high, kv_low = sem("kv_high"), sem("kv_low")
        q_high, q_low = sem("q_high"), sem("q_low")
        q_out = sem("q_out")
        s_ps = sem("s_ps")
        pad_ready = sem("pad_ready")
        max_ready = sem("max_ready")
        exp_done = sem("exp_done")
        rsum_ready = sem("rsum_ready")
        probs_ready = sem("probs_ready")
        pT_ps = sem("pT_ps")
        pT_high, pT_low = sem("pT_high"), sem("pT_low")
        o_ps = sem("o_ps")
        oT_high, oT_low = sem("oT_high"), sem("oT_low")
        y_head = sem("y_head")
        x_added = sem("x_added")
        block = ctx.enter_context(nc.Block())

        @block.sync
        def _(sp):
            def load_kv(pair, i):
                wait_pos(sp, kv_low, pair - 1)
                t, h = pair % TT, pair // TT
                sp.dma_start(kv_f[:, i, :], env["kv_dram"][bass.ds(t, 1), :, bass.ds(h * KV, KV)]
                             .rearrange("t p c -> p (t c)")).then_inc(kv_in[i], 16)

            for i in range(2):
                sp.wait_ge(env["kv_stored"][i], 16 * (TT // 2))
                load_kv(i, i)
            for c in range(4, G + 2):
                load_wq(sp, env, c, c % 2)

            def body(bi, more_wq=4, more_kv=2):
                for k in range(4):
                    if k < more_wq:
                        load_wq(sp, env, 4 * bi + k + G + 2, k % 2)
                    if k % 2 and k // 2 < more_kv:
                        load_kv(2 * bi + 2 + k // 2, k // 2)

            with sp.Fori(0, BODIES - 3) as bi:
                body(bi)
            body(BODIES - 3, more_wq=2)
            body(BODIES - 2, more_wq=0)

        @block.gpsimd
        def _(pool):
            def load_wo(w, i):
                wait_pos(pool, wo_low, w - 1)
                pool.dma_start(wo_f[:, i, :], env["wo"][bass.ds(w * HD, HD), :]).then_inc(wo_in[i], 16)

            def split_wo(w, i):
                pool.wait_ge(wo_in[i], 16 * (w // 2 + 1))
                old = w - WO_RING
                wait_apart(pool, y_head, (old // G * TT + TT - 1) * G + old % G + 1)
                place = bass.ds(w % WO_RING, 1)
                pool.tensor_copy(wo[0][:, place, :], wo_f[:, i:i + 1, :]).then_inc(wo_high, 1)
                wait_apart(pool, wo_high, w + 1)
                pool.tensor_tensor(wo[1][:, place, :], wo_f[:, i:i + 1, :], wo[0][:, place, :].bitcast(F32),
                                   ALU.subtract).then_inc(wo_low, 1)

            load_wo(0, 0)
            load_wo(1, 1)
            for w in range(WO_RING):
                split_wo(w, w % 2)
                load_wo(w + 2, w % 2)
            with pool.Fori(WO_RING // 2, HK * G // 2 - 1) as half:
                for i in range(2):
                    split_wo(2 * half + i, i)
                    load_wo(2 * half + i + 2, i)
            for i in range(2):
                split_wo(HK * G - 2 + i, i)

        def step_queries(bi, k):
            return q_all[:, bass.ds((bi // 2) % 2, 1), :, bass.ds((bi % 2) * 4 * NL + k * NL, NL)]\
                .rearrange("p a g t -> p (a g) t")

        def before(bi, k):
            return (bi, k - 1) if k else (bi - 1, 3)

        def after(bi, k):
            return (bi, k + 1) if k < 3 else (bi + 1, 0)

        @block.scalar
        def _(act):
            def queries_out(c, i, parity, g):
                act.wait_ge(q_ps, c + 1)
                act.activation(q_all[:, bass.ds(parity, 1), bass.ds(g, 1), :].rearrange("p a g t -> p (a g t)"),
                               ps_q[i][:], ACT.Copy, scale=XS).then_inc(q_out, 1)

            def split_kv(pair, i, uses):
                act.wait_ge(kv_in[i], 16 * uses)
                wait_pos(act, o_ps, 2 * (pair - 1))
                act.activation(kv[0][:, i, :], kv_f[:, i, :], ACT.Copy).then_inc(kv_high, 1)

            def split_q(bi, k):
                n = 4 * bi + k
                wait_pos(act, s_ps, 2 * (n - 1))
                act.wait_ge(q_out, (bi // 2 + 1) * G)
                act.activation(q[0][:, k % 2], step_queries(bi, k), ACT.Copy).then_inc(q_high, 1)

            def softmax(bi, k, js):
                n, i = 4 * bi + k, k % 2
                wait_pos(act, pT_ps, 2 * (n - 1))
                for j in js:
                    if j % 2 == 0:
                        act.wait_ge(max_ready, 2 * n + j // 2 + 1)
                    act.activation(probs[i][:, NL + j * NK:NL + (j + 1) * NK],
                                   ps_s[j // 2][:, (j % 2) * NK:(j % 2 + 1) * NK], ACT.Exp,
                                   bias=nmax[:, i, j:j + 1], accum_out=psum_p[:, i, j:j + 1]).then_inc(exp_done, 1)

            def split_probs(bi, k):
                n, rows = 4 * bi + k, slice(k % 2 * NL, k % 2 * NL + NL)
                wait_pos(act, o_ps, n)
                act.wait_ge(pT_ps, 2 * n + 1)
                act.activation(pT_ctx[0][:], ps_tc[:], ACT.Copy).then_inc(pT_high, 1)
                act.wait_ge(pT_ps, 2 * n + 2)
                act.activation(pT_lat[0][rows, :], ps_tl[rows, :], ACT.Copy).then_inc(pT_high, 1)

            def split_out(bi, k):
                n, pair = 4 * bi + k, 2 * bi + k // 2
                act.wait_ge(o_ps, n + 1)
                wait_pos(act, y_head, (pair - 1) * G)
                act.activation(oT[0][:, k // 2, :, k % 2 * NL:(k % 2 + 1) * NL],
                               ps_o[:].rearrange("p (g t) -> p g t", g=G), ACT.Copy).then_inc(oT_high, 1)

            def body(bi, queries=4, wqs=4, first=False, last=False):
                for k in range(4):
                    n = 4 * bi + k
                    softmax(bi, k, (0, 1))
                    if not (first and k == 0):
                        split_out(*before(bi, k))
                    softmax(bi, k, (2, 3))
                    if k < wqs:
                        high_wq(act, env, n + G + 1, (k + 1) % 2, 2 * bi + (k + G + 1) // 2 + 1)
                    if k % 2 == 0 and not (last and k == 2):
                        split_kv(2 * bi + k // 2 + 1, (k // 2 + 1) % 2, bi + k // 2 + 1)
                    if k < queries:
                        queries_out(n + G, k % 2, (bi // 2 + 1) % 2, (bi % 2) * 4 + k)
                    if not (last and k == 3):
                        split_q(*after(bi, k))
                    split_probs(bi, k)

            for c in range(G):
                if c >= 2:
                    high_wq(act, env, c, c % 2, c // 2 + 1)
                if c:
                    queries_out(c - 1, (c - 1) % 2, 0, c - 1)
                if c == 5:
                    split_kv(0, 0, 1)
            high_wq(act, env, G, 0, G // 2 + 1)
            queries_out(G - 1, 1, 0, G - 1)
            split_q(0, 0)
            body(0, first=True)
            with act.Fori(1, BODIES - 3) as bi:
                body(bi)
            body(BODIES - 3, wqs=3)
            body(BODIES - 2, queries=0, wqs=0)
            body(BODIES - 1, queries=0, wqs=0, last=True)
            split_out(BODIES - 1, 3)

        @block.vector
        def _(dve):
            def low_kv(pair, i):
                dve.wait_ge(kv_high, pair + 1)
                dve.tensor_tensor(kv[1][:, i, :], kv_f[:, i, :], kv[0][:, i, :].bitcast(F32), ALU.subtract)\
                    .then_inc(kv_low, 1)

            def low_q(bi, k):
                dve.wait_ge(q_high, 4 * bi + k + 1)
                dve.tensor_tensor(q[1][:, k % 2], step_queries(bi, k), q[0][:, k % 2].bitcast(F32), ALU.subtract)\
                    .then_inc(q_low, 1)

            def row_max(bi, k):
                n, i = 4 * bi + k, k % 2
                for j in range(2):
                    dve.wait_ge(s_ps, 2 * n + j + 1)
                    dve.tensor_reduce(nmax[:, i, 2 * j:2 * j + 2],
                                      ps_s[j][:, 0:2 * NK].rearrange("p (j n) -> p j n", j=2), AX.X, ALU.max,
                                      negate=True).then_inc(max_ready, 1)

            def normalise(bi, k):
                n, i = 4 * bi + k, k % 2
                dve.wait_ge(exp_done, 4 * (n + 1))
                dve.reciprocal(rsum[:, i, :], psum_p[:, i, :]).then_inc(rsum_ready, 1)
                dve.wait_ge(rsum_ready, n + 1)
                for j in range(4):
                    p = probs[i][:, NL + j * NK:NL + (j + 1) * NK]
                    last = dve.tensor_scalar(p, p, rsum[:, i, j:j + 1], None, ALU.mult)
                last.then_inc(probs_ready, 1)

            def low_probs(bi, k):
                n, rows = 4 * bi + k, slice(k % 2 * NL, k % 2 * NL + NL)
                dve.wait_ge(pT_high, 2 * n + 1)
                dve.tensor_tensor(pT_ctx[1][:], ps_tc[:], pT_ctx[0][:].bitcast(F32), ALU.subtract).then_inc(pT_low, 1)
                dve.wait_ge(pT_high, 2 * n + 2)
                dve.tensor_tensor(pT_lat[1][rows, :], ps_tl[rows, :], pT_lat[0][rows, :].bitcast(F32), ALU.subtract)\
                    .then_inc(pT_low, 1)

            def add_output(pair):
                dve.wait_ge(y_head, (pair + 1) * G)
                xt = x1[:, bass.ds(pair % TT, 1), :].rearrange("p t d -> p (t d)")
                dve.tensor_tensor(xt, ps_y[:], xt, ALU.add).then_inc(x_added, 1)

            def low_out(bi, k):
                dve.wait_ge(oT_high, 4 * bi + k + 1)
                cols = slice(k % 2 * NL, (k % 2 + 1) * NL)
                dve.tensor_tensor(oT[1][:, k // 2, :, cols], ps_o[:].rearrange("p (g t) -> p g t", g=G),
                                  oT[0][:, k // 2, :, cols].bitcast(F32), ALU.subtract).then_inc(oT_low, 1)

            def body(bi, wqs=4, first=False, last=False):
                for k in range(4):
                    row_max(bi, k)
                    if k % 2 == 0 and not first:
                        add_output(2 * bi + k // 2 - 2)
                    if not (first and k == 0):
                        low_out(*before(bi, k))
                    normalise(bi, k)
                    if k < wqs:
                        low_wq(dve, env, 4 * bi + k + G + 1, (k + 1) % 2)
                    if k % 2 == 0 and not (last and k == 2):
                        low_kv(2 * bi + k // 2 + 1, (k // 2 + 1) % 2)
                    if not (last and k == 3):
                        low_q(*after(bi, k))
                    low_probs(bi, k)

            dve.memset(probs[1][:, 0:NL], 0.0).then_inc(pad_ready, 1)
            for c in range(G):
                if c >= 2:
                    low_wq(dve, env, c, c % 2)
                if c == 5:
                    low_kv(0, 0)
            low_wq(dve, env, G, 0)
            low_q(0, 0)
            body(0, first=True)
            with dve.Fori(1, BODIES - 3) as bi:
                body(bi)
            body(BODIES - 3, wqs=3)
            body(BODIES - 2, wqs=0)
            body(BODIES - 1, wqs=0, last=True)
            low_out(BODIES - 1, 3)
            add_output(STEPS // 2 - 2)
            add_output(STEPS // 2 - 1)

        @block.tensor
        def _(pe):
            def product(out, pairs, **kw):
                for n, (lhsT, rhs) in enumerate(pairs):
                    last = pe.matmul(out, lhsT, rhs, start=(n == 0), stop=(n == len(pairs) - 1), **kw)
                return last

            def queries(c, i, half):
                pe.wait_ge(wq_low, c + 1)
                wait_pos(pe, q_out, c - 1)
                product(ps_q[i][:], [(wq[a][:, i, t, :], xnT[b][:, t, bass.ds(half * HT, HT)])
                                     for a, b in PASSES for t in range(KT)]).then_inc(q_ps, 1)

            def scores(bi, k):
                n, pair = 4 * bi + k, 2 * bi + k // 2
                keys = slice(k % 2 * NK, (k % 2 + 1) * NK)
                if k % 2 == 0:
                    pe.wait_ge(kv_low, pair + 1)
                pe.wait_ge(q_low, n + 1)
                for j in range(4):
                    if j % 2 == 0:
                        wait_pos(pe, exp_done, 4 * (n - 1) + j + 2)
                    last = product(ps_s[j // 2][:, (j % 2) * NK:(j % 2 + 1) * NK],
                                   [(q[a][:, k % 2, 2 * j:2 * j + 2, :].rearrange("p g t -> p (g t)"),
                                     kv[b][:, k // 2, keys]) for a, b in PASSES])
                    if j % 2:
                        last.then_inc(s_ps, 1)

            def transposes(bi, k):
                n, s = 4 * bi + k, k % 2
                pe.wait_ge(probs_ready, n + 1)
                wait_pos(pe, pT_low, 2 * n)
                for j in range(4):
                    start = NL + j * NK + (NL if s else 0)
                    last = pe.transpose(ps_tc[:, j * P:(j + 1) * P], probs[s][:, start:start + NC], ident[:])
                last.then_inc(pT_ps, 1)
                for j in range(4):
                    if s:
                        last = pe.transpose(ps_tl[:, j * P:(j + 1) * P], probs[s][:, j * NK:j * NK + P], ident[:])
                    else:
                        start = NL + j * NK + NC
                        last = pe.transpose(ps_tl[0:NL, j * P:(j + 1) * P], probs[s][:, start:start + NL], ident[:])
                last.then_inc(pT_ps, 1)

            def output_product(pair, i, heads):
                if 0 in heads:
                    pe.wait_ge(oT_low, 2 * (pair + 1))
                    wait_pos(pe, x_added, pair)
                for g in heads:
                    w = pair // TT * G + g
                    pe.wait_ge(wo_low, w + 1)
                    for n, (a, b) in enumerate(PASSES):
                        last = pe.matmul(ps_y[:], oT[a][:, i, g, :], wo[b][:, bass.ds(w % WO_RING, 1), :]
                                         .rearrange("p w d -> p (w d)"), start=(g == 0 and n == 0),
                                         stop=(g == G - 1 and n == 2))
                    last.then_inc(y_head, 1)

            def outputs(bi, k):
                n, i, s = 4 * bi + k, k // 2, k % 2
                lat = slice(s * NL, (s + 1) * NL)
                wait_pos(pe, oT_low, n)
                pe.wait_ge(pT_low, 2 * n + 1)
                for m, (a, b) in enumerate(PASSES):
                    pe.matmul(ps_o[:], kv[a][:, i, VO + s * HD:VO + (s + 1) * HD], pT_ctx[b][:], start=(m == 0),
                              stop=False)
                pe.wait_ge(pT_low, 2 * n + 2)
                for m, (a, b) in enumerate(PASSES):
                    last = pe.matmul(ps_o[:], kv[a][lat, i, VO + 2 * HD:VO + 3 * HD], pT_lat[b][lat, :], start=False,
                                     stop=(m == 2))
                last.then_inc(o_ps, 1)

            def body(bi, next_queries=True, first=False, last=False):
                for k in range(4):
                    pair, i = 2 * bi + k // 2 - 1, (k // 2 + 1) % 2
                    if next_queries:
                        queries(4 * bi + k + G, k % 2, (bi // 2 + 1) % 2)
                    if not (first and k < 2):
                        output_product(pair, i, range(k % 2 * 4, k % 2 * 4 + 3))
                    transposes(bi, k)
                    if not (first and k < 2):
                        output_product(pair, i, range(k % 2 * 4 + 3, k % 2 * 4 + 4))
                    if not (last and k == 3):
                        scores(*after(bi, k))
                    outputs(bi, k)

            for c in range(G):
                queries(c, c % 2, 0)
            pe.wait_ge(pad_ready, 1)
            scores(0, 0)
            body(0, first=True)
            with pe.Fori(1, BODIES - 2) as bi:
                body(bi)
            body(BODIES - 2, next_queries=False)
            body(BODIES - 1, next_queries=False, last=True)
            output_product(STEPS // 2 - 1, 1, range(G))


def stage_self_attention_and_experts(nc, env):
    ctx = ExitStack()
    with ctx:
        def sb(name, shape, dt=F32):
            return ctx.enter_context(nc.sbuf_tensor(name, shape, dt))

        def ps(name):
            return ctx.enter_context(nc.psum_tensor(name, [P, 512], F32))

        def sem(name):
            return ctx.enter_context(nc.semaphore(name))

        x1, ident, minus_half = env["x1"], env["ident"], env["minus_half"]
        names = ("k", "q", "v", "o")
        SCALE = float(SD) ** -0.5
        w_f = [sb(f"c_w_f{i}", [P, KT, D]) for i in range(2)]
        w = {n: [sb(f"c_w{n}_{p}", [P, KT, D], F32R) for p in "hl"] for n in names}
        ident_r = sb("ident_r", [P, P], F32R)
        cmask_f, cmask = sb("c_mask_f", [P, D]), sb("c_mask", [P, D], F32R)
        bmask = sb("c_bmask", [P, 4])
        cos, sin = sb("c_cos", [P, SD]), sb("c_sin", [P, SD])
        stats, mv = sb("c_stats", [P, 6]), sb("c_mv", [P, 2])
        var, rstd = sb("c_var", [P, 1]), sb("c_rstd", [P, 1])
        xn = sb("c_xn", [P, D])
        xT = [sb(f"c_xT_{p}", [P, KT, P], F32R) for p in "hl"]
        rot_a = {n: sb(f"rot_a_{n}", [P, D]) for n in "kq"}
        rot_b = {n: sb(f"rot_b_{n}", [P, D]) for n in "kq"}
        kT = [sb(f"c_kT_{p}", [P, 4, P], F32R) for p in "hl"]
        qz = [[sb(f"qz{i}_{p}", [P, 4, 2, P], F32R) for p in "hl"] for i in range(2)]
        kblk = [[sb(f"kblk{s}_{p}", [P, 4, 4, NL], F32R) for p in "hl"] for s in range(2)]
        v_f, v_swap = sb("v_f", [P, D]), sb("v_swap", [P, D])
        vz = [[sb(f"vz{i}_{p}", [P, 2, D], F32R) for p in "hl"] for i in range(2)]
        probs = [sb(f"c_probs{i}", [P, D]) for i in range(2)]
        nmax, psum_p, rsum = (sb(n, [P, 2, 8]) for n in ("c_nmax", "c_psum", "c_rsum"))
        pT = [sb(f"c_pT_{p}", [P, 4, P], F32R) for p in "hl"]
        oT = [sb(f"c_oT_{p}", [P, 2, 4, P], F32R) for p in "hl"]
        ps_t = ps("c_ps_t")
        ps_p = [ps(f"c_ps_p{i}") for i in range(2)]
        ps_s = [ps(f"c_ps_s{i}") for i in range(2)]
        ps_pt = ps("c_ps_pt")
        ps_o = ps("c_ps_o")

        rw = [sb(f"rw_{p}", [P, KT, E], F32R) for p in "hl"]
        eb = [sb(f"eb_{p}", [E, D], F32R) for p in "hl"]
        rbias = sb("rbias", [P, E])
        d_stats, d_mv = sb("d_stats", [P, 6]), sb("d_mv", [P, 2])
        d_var, d_rstd = sb("d_var", [P, 1]), sb("d_rstd", [P, 1])
        d_xn = sb("d_xn", [P, D])
        d_xT = [sb(f"d_xT_{p}", [P, KT, P], F32R) for p in "hl"]
        logits, d_probs, rest, chosen = (sb(n, [P, E]) for n in ("logits", "d_probs", "rest", "chosen"))
        d_nmax, d_psum, d_rsum, wsum = (sb(n, [P, 1]) for n in ("d_nmax", "d_psum", "d_rsum", "wsum"))
        top = sb("top", [P, 8])
        wT = [sb(f"wT_{p}", [E, P], F32R) for p in "hl"]
        y = sb("y", [P, D])
        ps_d = ps("ps_d")

        w_in = [sem(f"c_w_in{i}") for i in range(6)]
        table_in = [sem(f"c_table_in{i}") for i in range(5)]
        w_high, w_low = sem("c_w_high"), sem("c_w_low")
        tables = sem("c_tables")
        zeroed = sem("c_zeroed")
        stats_ready = sem("c_stats_ready")
        var_ready, rstd_ready = sem("c_var_ready"), sem("c_rstd_ready")
        xn_ready = sem("c_xn_ready")
        xT_ps, xT_high, xT_low = sem("c_xT_ps"), sem("c_xT_high"), sem("c_xT_low")
        kp_ps, qp_ps, vp_ps = sem("kp_ps"), sem("qp_ps"), sem("vp_ps")
        k_turned, q_turned = sem("k_turned"), sem("q_turned")
        k_rot, q_rot = sem("k_rot"), sem("q_rot")
        kT_ps, kT_high, kT_low = sem("c_kT_ps"), sem("c_kT_high"), sem("c_kT_low")
        qT_ps, qz_high, qz_low = sem("c_qT_ps"), sem("c_qz_high"), sem("c_qz_low")
        kblk_ready = sem("kblk_ready")
        v_out = sem("v_out_c")
        v_swapped = sem("v_swapped")
        vz_high, vz_low = sem("vz_high"), sem("vz_low")
        vz_even = sem("vz_even")
        s_ps, max_ready = sem("c_s_ps"), sem("c_max_ready")
        exp_done, rsum_ready = sem("c_exp_done"), sem("c_rsum_ready")
        probs_ready = sem("c_probs_ready")
        pT_ps, pT_high, pT_low = sem("c_pT_ps"), sem("c_pT_high"), sem("c_pT_low")
        o_ps, oT_high, oT_low = sem("c_o_ps"), sem("c_oT_high"), sem("c_oT_low")
        y_ps, x_added = sem("c_y_ps"), sem("c_x_added")
        d_stored = sem("d_stored")
        d_stats_ready = sem("d_stats_ready")
        d_var_ready, d_rstd_ready = sem("d_var_ready"), sem("d_rstd_ready")
        d_xn_ready = sem("d_xn_ready")
        d_xT_ps, d_xT_high, d_xT_low = sem("d_xT_ps"), sem("d_xT_high"), sem("d_xT_low")
        l_ps = sem("l_ps")
        steps = sem("d_steps")
        d_exp_done = sem("d_exp_done")
        chosen_ready = sem("chosen_ready")
        wT_ps, wT_high, wT_low = sem("wT_ps"), sem("wT_high"), sem("wT_low")
        d_y_ps, y_part, y_ready = sem("d_y_ps"), sem("y_part"), sem("y_ready")
        block = ctx.enter_context(nc.Block())

        def tile(t):
            return x1[:, bass.ds(t, 1), :].rearrange("p t d -> p (t d)")

        def is_last(t):
            return isinstance(t, int) and t == TT - 1

        def has_two_after(t):
            return not isinstance(t, int) or t < TT - 2

        def run(eng, slot):
            def two_tiles(tb):
                for i in range(2):
                    for o in range(4):
                        slot(2 * tb + i, i, o)
            two_tiles(0)
            with eng.Fori(1, TT // 2 - 1) as tb:
                two_tiles(tb)
            two_tiles(TT // 2 - 1)

        def has_experts(t):
            return not isinstance(t, int) or t >= 2

        def before(t, i, o):
            return (t, i, o - 1) if o else (t - 1, 1 - i, 3)

        def value_block(i, j, h):
            rows = slice(h * NL, (h + 1) * NL)
            src = (v_f if j == h else v_swap)[rows, :]

            def heads(a):
                return a.rearrange("p (g h d) -> p g h d", h=2, d=SD)[:, :, h, :]
            return [heads(vz[i][p][rows, j, :]) for p in range(2)], heads(src)

        def own_columns(a):
            return a[:].rearrange("p o j (c n) -> p o (j c) n", c=2)[:, :, 0:4:3, :]

        def batches(a):
            return a[:].rearrange("p (o j n) -> p o j n", o=4, j=2)

        def output_block(o, q):
            rows = slice(32 * q, 32 * q + 32)
            return rows, ps_o[rows, :].rearrange("p (j q n) -> p j q n", j=2, q=4)[:, :, q, :]

        @block.sync
        def _(sp):
            for n, name in enumerate(names):
                wait_pos(sp, w_low, n - 1)
                sp.dma_start(w_f[n % 2][:], env["c_w" + name].rearrange("(k p) n -> p k n", p=P)).then_inc(w_in[n], 16)
                if n == 1:
                    for i, (dst, src) in enumerate(((cos, "cos"), (sin, "sin"), (bmask, "bmask"), (cmask_f, "cmask"))):
                        sp.dma_start(dst[:], env[src]).then_inc(table_in[i], 16)
            sp.dma_start(rbias[:], env["router_bias"].unsqueeze(0).broadcast_to([P, E])).then_inc(table_in[4], 16)

            def swap(t):
                sp.wait_ge(v_out, t + 1)
                wait_pos(sp, vz_low, t)
                for h in range(2):
                    sp.dma_start(v_swap[h * NL:(h + 1) * NL, :], v_f[(1 - h) * NL:(2 - h) * NL, :])\
                        .then_inc(v_swapped, 16)
            def store(t):
                sp.wait_ge(y_ready, t + 1)
                sp.dma_start(env["out"][bass.ds(t, 1)].rearrange("t p d -> p (t d)"), y[:]).then_inc(d_stored, 16)

            swap(0)
            sp.wait_ge(w_low, 3)
            sp.dma_start(w_f[0][:, :, 0:E], env["router_wT"].rearrange("(k p) e -> p k e", p=P)).then_inc(w_in[4], 16)
            sp.wait_ge(w_low, 4)
            sp.dma_start(w_f[1][0:E, 0, :], env["expert_bias"]).then_inc(w_in[5], 16)
            swap(1)
            swap(2)
            with sp.Fori(3, TT) as t:
                swap(t)
                store(t - 3)
            for t in range(TT - 3, TT):
                store(t)
            sp.wait_ge(d_stored, 16 * TT)

        @block.gpsimd
        def _(pool):
            def inverse_deviation(t):
                wait_apart(pool, stats_ready, 2 * t + 2)
                pool.tensor_scalar(var[:], mv[:, 1:2], EPS, None, ALU.add).then_inc(var_ready, 1)
                pool.wait_ge(var_ready, t + 1)
                pool.tensor_tensor(rstd[:], var[:], minus_half[:], ALU.pow).then_inc(rstd_ready, 1)

            def d_inverse_deviation(t):
                wait_apart(pool, d_stats_ready, 2 * t + 2)
                pool.tensor_scalar(d_var[:], d_mv[:, 1:2], EPS, None, ALU.add).then_inc(d_var_ready, 1)
                pool.wait_ge(d_var_ready, t + 1)
                pool.tensor_tensor(d_rstd[:], d_var[:], minus_half[:], ALU.pow).then_inc(d_rstd_ready, 1)

            def rotate(t, n, turned, rot):
                pool.wait_ge(turned, t + 1)
                pool.tensor_tensor(rot_a[n][:], rot_a[n][:], rot_b[n][:], ALU.add).then_inc(rot, 1)

            def spread_keys(t, s):
                pool.wait_ge(kT_low, t + 1)
                wait_pos(pool, s_ps, 2 * (2 * t + s - 1))
                for p in range(2):
                    k = kT[p][:, 2 * s:2 * s + 2, :].rearrange("p a (j n) -> p (a j) n", j=2).bitcast(F32)
                    last = pool.tensor_tensor(kblk[s][p][:], k.unsqueeze(2).broadcast_to([P, 4, 4, NL]),
                                              bmask[:].unsqueeze(1).unsqueeze(3).broadcast_to([P, 4, 4, NL]), ALU.mult)
                last.then_inc(kblk_ready, 1)

            def low_values(t, i):
                pool.wait_ge(vz_high, t + 1)
                for h in range(2):
                    if h:
                        pool.wait_ge(kblk_ready, 2 * t + 2)
                        pool.wait_ge(vz_even, t + 1)
                    for j in range(2):
                        dst, src = value_block(i, j, h)
                        last = pool.tensor_tensor(dst[1], src, dst[0].bitcast(F32), ALU.subtract)
                    last.then_inc(vz_low if h else vz_even, 1)
                pool.wait_ge(vz_low, t + 1)

            for i in range(2):
                for p in range(2):
                    pool.memset(qz[i][p][:].bitcast(F32), 0.0)
                    last = pool.memset(vz[i][p][:].bitcast(F32), 0.0)
            last.then_inc(zeroed, 1)
            inverse_deviation(0)
            inverse_deviation(1)
            pool.wait_ge(table_in[2], 16)
            rotate(0, "k", k_turned, k_rot)
            rotate(0, "q", q_turned, q_rot)
            spread_keys(0, 0)
            spread_keys(0, 1)
            low_values(0, 0)

            def slot(t, i, o):
                if o == 0 and has_experts(t):
                    d_inverse_deviation(t - 2)
                if is_last(t):
                    return
                if o == 0:
                    rotate(t + 1, "k", k_turned, k_rot)
                    if has_two_after(t):
                        inverse_deviation(t + 2)
                if o == 1:
                    rotate(t + 1, "q", q_turned, q_rot)
                    spread_keys(t + 1, 0)
                if o == 2:
                    spread_keys(t + 1, 1)
                if o == 3:
                    low_values(t + 1, 1 - i)
            run(pool, slot)
            for t in range(TT - 2, TT):
                d_inverse_deviation(t)

        @block.scalar
        def _(act):
            def copy(out, in_):
                return act.activation(out, in_, ACT.Copy)

            def split_w(n):
                act.wait_ge(w_in[n], 16)
                copy(w[names[n]][0][:], w_f[n % 2][:]).then_inc(w_high, 1)

            def high_x(t):
                act.wait_ge(xT_ps, t + 1)
                wait_pos(act, vp_ps, t)
                copy(xT[0][:].rearrange("p k n -> p (k n)"), ps_t[:]).then_inc(xT_high, 1)

            def high_k(t):
                act.wait_ge(kT_ps, t + 1)
                wait_pos(act, kblk_ready, 2 * t)
                copy(kT[0][:].rearrange("p k n -> p (k n)"), ps_t[:]).then_inc(kT_high, 1)

            def high_q(t, i):
                act.wait_ge(qT_ps, t + 1)
                wait_pos(act, s_ps, 4 * (t - 1))
                act.activation(own_columns(qz[i][0]), batches(ps_t), ACT.Copy, scale=SCALE).then_inc(qz_high, 1)

            def values_out(t):
                act.wait_ge(vp_ps, t + 1)
                wait_pos(act, vz_low, t)
                copy(v_f[:], ps_p[0][:]).then_inc(v_out, 1)

            def high_values(t, i):
                act.wait_ge(v_swapped, 32 * (t + 1))
                wait_pos(act, o_ps, 4 * (t - 1))
                for j in range(2):
                    for h in range(2):
                        dst, src = value_block(i, j, h)
                        last = copy(dst[0], src)
                last.then_inc(vz_high, 1)

            def exponential(m, b):
                act.wait_ge(max_ready, m + 1)
                wait_pos(act, pT_ps, m - 1)
                for h in range(8):
                    head = slice(h * NL, (h + 1) * NL)
                    last = act.activation(probs[b][:, head], ps_s[b][:, head], ACT.Exp, bias=nmax[:, b, h:h + 1],
                                          accum_out=psum_p[:, b, h:h + 1])
                last.then_inc(exp_done, 1)

            def high_probs(m):
                act.wait_ge(pT_ps, m + 1)
                wait_pos(act, o_ps, m)
                copy(pT[0][:].rearrange("p k n -> p (k n)"), ps_pt[:]).then_inc(pT_high, 1)

            def high_out(t, i, o):
                m = 4 * t + o
                act.wait_ge(o_ps, m + 1)
                if o == 0:
                    wait_pos(act, y_ps, t - 1)
                for q in range(4):
                    rows, src = output_block(o, q)
                    last = copy(oT[0][rows, i, o, :].rearrange("p (j n) -> p j n", j=2), src)
                last.then_inc(oT_high, 1)

            def d_high_x(t):
                act.wait_ge(d_xT_ps, t + 1)
                wait_pos(act, l_ps, t)
                copy(d_xT[0][:].rearrange("p k n -> p (k n)"), ps_d[:]).then_inc(d_xT_high, 1)

            def d_exponential(t):
                act.wait_ge(steps, 7 * t + 2)
                act.activation(d_probs[:], logits[:], ACT.Exp, bias=d_nmax[:], accum_out=d_psum[:])\
                    .then_inc(d_exp_done, 1)

            def d_high_w(t):
                act.wait_ge(wT_ps, t + 1)
                wait_pos(act, d_y_ps, t)
                copy(wT[0][:], ps_d[0:E, 0:P]).then_inc(wT_high, 1)

            split_w(0)
            split_w(1)
            high_x(0)
            act.wait_ge(table_in[3], 16)
            copy(cmask[:], cmask_f[:])
            copy(ident_r[:], ident[:]).then_inc(tables, 1)
            split_w(2)
            act.wait_ge(zeroed, 1)
            high_k(0)
            high_q(0, 0)
            split_w(3)
            values_out(0)
            high_x(1)
            exponential(0, 0)
            exponential(1, 1)
            high_values(0, 0)
            act.wait_ge(w_in[4], 16)
            copy(rw[0][:], w_f[0][:, :, 0:E]).then_inc(w_high, 1)
            act.wait_ge(w_in[5], 16)
            copy(eb[0][:], w_f[1][0:E, 0, :]).then_inc(w_high, 1)

            def slot(t, i, o):
                m = 4 * t + o
                more = not is_last(t)
                high_probs(m)
                if o == 1 and has_experts(t):
                    d_high_x(t - 2)
                if o == 3 and has_experts(t):
                    d_high_w(t - 2)
                if o == 2 and more:
                    values_out(t + 1)
                if o == 3 and more:
                    high_values(t + 1, 1 - i)
                if not (isinstance(m, int) and m == 0):
                    high_out(*before(t, i, o))
                if o == 1 and more:
                    high_q(t + 1, 1 - i)
                if o == 2 and has_two_after(t):
                    high_x(t + 2)
                if o == 2 and has_experts(t):
                    d_exponential(t - 2)
                if more or o < 2:
                    exponential(m + 2, o % 2)
                if o == 0 and more:
                    high_k(t + 1)
            run(act, slot)
            high_out(TT - 1, 1, 3)
            for t in range(TT - 2, TT):
                d_high_x(t)
                d_exponential(t)
                d_high_w(t)

        @block.vector
        def _(dve):
            def sub(out, a, b):
                return dve.tensor_tensor(out, a, b.bitcast(F32), ALU.subtract)

            def low_w(n):
                dve.wait_ge(w_high, n + 1)
                sub(w[names[n]][1][:], w_f[n % 2][:], w[names[n]][0][:]).then_inc(w_low, 1)

            def statistics(t):
                wait_pos(dve, xn_ready, t)
                dve.bn_stats(stats[:], tile(t)).then_inc(stats_ready, 1)
                wait_apart(dve, stats_ready, 2 * t + 1)
                dve.bn_aggr(mv[:], stats[:]).then_inc(stats_ready, 1)

            def normalised(t):
                dve.wait_ge(rstd_ready, t + 1)
                wait_pos(dve, xT_ps, t)
                dve.tensor_scalar(xn[:], tile(t), mv[:, 0:1], rstd[:], ALU.subtract, ALU.mult).then_inc(xn_ready, 1)

            def flat(a):
                return a[:].rearrange("p k n -> p (k n)")

            def low_x(t):
                dve.wait_ge(xT_high, t + 1)
                sub(flat(xT[1]), ps_t[:], flat(xT[0])).then_inc(xT_low, 1)

            def turn(t, n, proj, bank, turned, rot_T):
                dve.wait_ge(proj, t + 1)
                wait_pos(dve, rot_T, t)
                heads = "p (h d) -> p h d"
                dve.tensor_tensor(rot_a[n][:].rearrange(heads, d=SD), bank[:].rearrange(heads, d=SD),
                                  cos[:].unsqueeze(1).broadcast_to([P, D // SD, SD]), ALU.mult)
                pairs = "p (h c e) -> p h c e"
                for e in range(2):
                    last = dve.tensor_tensor(
                        rot_b[n][:].rearrange(pairs, c=SD // 2, e=2)[:, :, :, e],
                        bank[:].rearrange(pairs, c=SD // 2, e=2)[:, :, :, 1 - e],
                        sin[:].rearrange("p (c e) -> p c e", e=2)[:, :, e].unsqueeze(1)
                        .broadcast_to([P, D // SD, SD // 2]), ALU.mult)
                last.then_inc(turned, 1)

            def low_k(t):
                dve.wait_ge(kT_high, t + 1)
                sub(flat(kT[1]), ps_t[:], flat(kT[0])).then_inc(kT_low, 1)

            def low_q(t, i):
                dve.wait_ge(qz_high, t + 1)
                for o in range(4):
                    last = dve.scalar_tensor_tensor(own_columns(qz[i][1])[:, o], batches(ps_t)[:, o], SCALE,
                                                    own_columns(qz[i][0])[:, o].bitcast(F32), ALU.mult, ALU.subtract)
                last.then_inc(qz_low, 1)

            def per_head(a, b):
                return a[:, b, :].unsqueeze(2).broadcast_to([P, 8, NL])

            def heads(a):
                return a[:].rearrange("p (h n) -> p h n", h=8)

            def row_max(m, b):
                dve.wait_ge(s_ps, m + 1)
                dve.tensor_reduce(nmax[:, b, :], heads(ps_s[b]), AX.X, ALU.max, negate=True).then_inc(max_ready, 1)

            def divide_by_sum(m, b):
                dve.wait_ge(exp_done, m + 1)
                dve.reciprocal(rsum[:, b, :], psum_p[:, b, :]).then_inc(rsum_ready, 1)
                dve.wait_ge(rsum_ready, m + 1)
                dve.tensor_tensor(heads(probs[b]), heads(probs[b]), per_head(rsum, b), ALU.mult)\
                    .then_inc(probs_ready, 1)

            def low_probs(m):
                dve.wait_ge(pT_high, m + 1)
                sub(flat(pT[1]), ps_pt[:], flat(pT[0])).then_inc(pT_low, 1)

            def low_out(t, i, o):
                m = 4 * t + o
                dve.wait_ge(oT_high, m + 1)
                for q in range(4):
                    rows, src = output_block(o, q)
                    dst = [oT[p][rows, i, o, :].rearrange("p (j n) -> p j n", j=2) for p in range(2)]
                    last = sub(dst[1], src, dst[0])
                last.then_inc(oT_low, 1)

            def add_output(t):
                dve.wait_ge(y_ps, t + 1)
                dve.tensor_tensor(tile(t), ps_p[1][:], tile(t), ALU.add).then_inc(x_added, 1)

            def d_statistics(t):
                wait_apart(dve, x_added, t + 1)
                dve.bn_stats(d_stats[:], tile(t)).then_inc(d_stats_ready, 1)
                wait_apart(dve, d_stats_ready, 2 * t + 1)
                dve.bn_aggr(d_mv[:], d_stats[:]).then_inc(d_stats_ready, 1)

            def d_normalised(t):
                dve.wait_ge(d_rstd_ready, t + 1)
                dve.tensor_scalar(d_xn[:], tile(t), d_mv[:, 0:1], d_rstd[:], ALU.subtract, ALU.mult)\
                    .then_inc(d_xn_ready, 1)

            def d_low_x(t):
                dve.wait_ge(d_xT_high, t + 1)
                sub(flat(d_xT[1]), ps_d[:], flat(d_xT[0])).then_inc(d_xT_low, 1)

            def d_logits(t):
                dve.wait_ge(l_ps, t + 1)
                dve.tensor_tensor(logits[:], ps_d[:, 0:E], rbias[:], ALU.add).then_inc(steps, 1)
                dve.wait_ge(steps, 7 * t + 1)
                dve.tensor_reduce(d_nmax[:], logits[:], AX.X, ALU.max, negate=True).then_inc(steps, 1)

            def d_choose(t):
                def step(n, instruction):
                    instruction.then_inc(steps, 1)
                    wait_apart(dve, steps, 7 * t + n)

                dve.wait_ge(d_exp_done, t + 1)
                step(3, dve.reciprocal(d_rsum[:], d_psum[:]))
                step(4, dve.tensor_scalar(d_probs[:], d_probs[:], d_rsum[:], None, ALU.mult))
                step(5, dve.max(top[:], d_probs[:]))
                step(6, dve.match_replace(rest[:], top[:], d_probs[:], 0.0))
                dve.tensor_tensor(chosen[:], d_probs[:], rest[:], ALU.subtract).then_inc(chosen_ready, 1)
                step(7, dve.tensor_reduce(wsum[:], top[:], AX.X, ALU.add))
                wait_pos(dve, d_stored, 16 * t)
                dve.scalar_tensor_tensor(y[:], d_xn[:], wsum[:], tile(t), ALU.mult, ALU.add).then_inc(y_part, 1)

            def d_low_w(t):
                dve.wait_ge(wT_high, t + 1)
                sub(wT[1][:], ps_d[0:E, 0:P], wT[0][:]).then_inc(wT_low, 1)

            def d_add(t):
                dve.wait_ge(d_y_ps, t + 1)
                dve.wait_ge(y_part, t + 1)
                dve.tensor_tensor(y[:], y[:], ps_d[:], ALU.add).then_inc(y_ready, 1)

            statistics(0)
            normalised(0)
            statistics(1)
            low_w(0)
            low_x(0)
            low_w(1)
            normalised(1)
            for i in range(2):
                dve.wait_ge(table_in[i], 16)
            turn(0, "k", kp_ps, ps_p[0], k_turned, kT_ps)
            low_w(2)
            turn(0, "q", qp_ps, ps_p[1], q_turned, qT_ps)
            dve.wait_ge(zeroed, 1)
            low_k(0)
            low_q(0, 0)
            low_w(3)
            low_x(1)
            row_max(0, 0)
            row_max(1, 1)
            divide_by_sum(0, 0)
            dve.wait_ge(w_high, 5)
            sub(rw[1][:], w_f[0][:, :, 0:E], rw[0][:]).then_inc(w_low, 1)
            dve.wait_ge(w_high, 6)
            sub(eb[1][:], w_f[1][0:E, 0, :], eb[0][:]).then_inc(w_low, 1)
            dve.wait_ge(table_in[4], 16)
            turn(1, "k", kp_ps, ps_p[0], k_turned, kT_ps)

            def slot(t, i, o):
                m = 4 * t + o
                more = not is_last(t)
                if o == 1 and more:
                    low_k(t + 1)
                if more or o < 3:
                    divide_by_sum(m + 1, (o + 1) % 2)
                low_probs(m)
                if has_experts(t):
                    if o == 0:
                        d_normalised(t - 2)
                    if o == 1:
                        d_low_x(t - 2)
                    if o == 2:
                        d_logits(t - 2)
                    if o == 3:
                        d_low_w(t - 2)
                if not (isinstance(m, int) and m == 0):
                    low_out(*before(t, i, o))
                if o == 3 and not (isinstance(t, int) and t == 0):
                    add_output(t - 1)
                if more or o < 2:
                    row_max(m + 2, o % 2)
                if o == 0 and has_two_after(t):
                    statistics(t + 2)
                if o == 0 and more:
                    turn(t + 1, "q", qp_ps, ps_p[1], q_turned, qT_ps)
                if o == 1 and more:
                    low_q(t + 1, 1 - i)
                if o == 1 and has_two_after(t):
                    normalised(t + 2)
                if o == 2 and has_two_after(t):
                    low_x(t + 2)
                if o == 2 and has_experts(t):
                    d_choose(t - 2)
                if o == 3 and has_experts(t):
                    d_add(t - 2)
                if o == 3 and not (isinstance(t, int) and t == 0):
                    d_statistics(t - 1)
                if o == 3 and has_two_after(t):
                    turn(t + 2, "k", kp_ps, ps_p[0], k_turned, kT_ps)
            run(dve, slot)
            low_out(TT - 1, 1, 3)
            for t in range(TT - 2, TT):
                if t == TT - 1:
                    add_output(t)
                    d_statistics(t)
                d_normalised(t)
                d_low_x(t)
                d_logits(t)
                d_choose(t)
                d_low_w(t)
                d_add(t)

        @block.tensor
        def _(pe):
            def turn_tile(src, done):
                for k in range(KT):
                    last = pe.transpose(ps_t[:, k * P:(k + 1) * P], src[:, k * P:(k + 1) * P], ident[:])
                last.then_inc(done, 1)

            def project(n, bank, done):
                ops = [(a, b, k) for a, b in PASSES for k in range(KT)]
                for c, (a, b, k) in enumerate(ops):
                    last = pe.matmul(bank[:], xT[a][:, k, :], w[n][b][:, k, :], start=(c == 0),
                                     stop=(c == len(ops) - 1))
                last.then_inc(done, 1)

            def x_turned(t):
                pe.wait_ge(xn_ready, t + 1)
                wait_pos(pe, qz_low, t)
                turn_tile(xn, xT_ps)

            def k_project(t):
                pe.wait_ge(xT_low, t + 1)
                wait_pos(pe, v_out, t)
                project("k", ps_p[0], kp_ps)

            def q_project(t):
                wait_pos(pe, x_added, t - 2)
                project("q", ps_p[1], qp_ps)

            def v_project(t):
                pe.wait_ge(k_turned, t + 1)
                project("v", ps_p[0], vp_ps)

            def k_turn(t):
                pe.wait_ge(k_rot, t + 1)
                pe.wait_ge(xT_low, t + 1)
                turn_tile(rot_a["k"], kT_ps)

            def q_turn(t):
                pe.wait_ge(q_rot, t + 1)
                pe.wait_ge(kT_low, t + 1)
                turn_tile(rot_a["q"], qT_ps)

            def scores(t, i, o):
                m, s, b = 4 * t + o, o // 2, o % 2
                rows = slice(b * NL, (b + 1) * NL)
                if o % 2 == 0:
                    pe.wait_ge(kblk_ready, 2 * t + s + 1)
                if o == 0:
                    pe.wait_ge(qz_low, t + 1)
                wait_pos(pe, exp_done, m - 1)
                pe.matmul(ps_s[b][:], ident_r[:], cmask[:], start=True, stop=False, skip_group_check=True)
                ops = [(x, j, p, r) for x in range(2) for j in range(2) for p, r in PASSES]
                for c, (x, j, p, r) in enumerate(ops):
                    last = pe.matmul(ps_s[b][:, x * 256:(x + 1) * 256], qz[i][p][rows, 2 * s + x, j, :],
                                     kblk[s][r][rows, 2 * x + j, :, :].rearrange("p h n -> p (h n)"), start=False,
                                     stop=(c == len(ops) - 1), skip_group_check=True)
                last.then_inc(s_ps, 1)

            def probs_turned(m, b):
                pe.wait_ge(probs_ready, m + 1)
                wait_pos(pe, pT_low, m)
                for q in range(4):
                    last = pe.transpose(ps_pt[:, q * P:(q + 1) * P], probs[b][:, q * P:(q + 1) * P], ident[:])
                last.then_inc(pT_ps, 1)

            def outputs(t, i, o):
                m = 4 * t + o
                pe.wait_ge(pT_low, m + 1)
                if o == 0:
                    pe.wait_ge(vz_low, t + 1)
                wait_pos(pe, oT_low, m)
                for j in range(2):
                    for c, (a, b) in enumerate(PASSES):
                        last = pe.matmul(ps_o[:, j * 256:(j + 1) * 256], vz[i][a][:, j, o * P:(o + 1) * P],
                                         pT[b][:, :, j * NL:(j + 1) * NL], start=(c == 0), stop=(c == 2))
                last.then_inc(o_ps, 1)

            def output_product(t, i):
                pe.wait_ge(oT_low, 4 * (t + 1))
                if isinstance(t, int) and t + 3 > TT:
                    pe.wait_ge(x_added, t)
                else:
                    pe.wait_ge(q_turned, t + 3)
                for c, (a, b, k) in enumerate([(a, b, k) for a, b in PASSES for k in range(4)]):
                    last = pe.matmul(ps_p[1][:], oT[a][:, i, k, :], w["o"][b][:, k, :], start=(c == 0), stop=(c == 11))
                last.then_inc(y_ps, 1)

            def d_x_turned(t):
                pe.wait_ge(d_xn_ready, t + 1)
                wait_pos(pe, y_ready, t)
                for k in range(KT):
                    last = pe.transpose(ps_d[:, k * P:(k + 1) * P], d_xn[:, k * P:(k + 1) * P], ident[:])
                last.then_inc(d_xT_ps, 1)

            def router(t):
                pe.wait_ge(d_xT_low, t + 1)
                for c, (a, b, k) in enumerate([(a, b, k) for a, b in PASSES for k in range(KT)]):
                    last = pe.matmul(ps_d[:, 0:E], d_xT[a][:, k, :], rw[b][:, k, :], start=(c == 0), stop=(c == 11))
                last.then_inc(l_ps, 1)

            def d_w_turned(t):
                wait_apart(pe, chosen_ready, t + 1)
                pe.transpose(ps_d[0:E, 0:P], chosen[:], ident[:]).then_inc(wT_ps, 1)

            def d_output(t):
                pe.wait_ge(wT_low, t + 1)
                for c, (a, b) in enumerate(PASSES):
                    last = pe.matmul(ps_d[:], wT[a][:], eb[b][:], start=(c == 0), stop=(c == 2))
                last.then_inc(d_y_ps, 1)

            x_turned(0)
            pe.wait_ge(w_low, 1)
            k_project(0)
            pe.wait_ge(w_low, 2)
            q_project(0)
            k_turn(0)
            pe.wait_ge(w_low, 3)
            v_project(0)
            q_turn(0)
            x_turned(1)
            pe.wait_ge(tables, 1)
            scores(0, 0, 0)
            scores(0, 0, 1)
            k_project(1)
            pe.wait_ge(w_low, 6)

            def slot(t, i, o):
                more = not is_last(t)
                probs_turned(4 * t + o, o % 2)
                if o == 3 and has_experts(t):
                    d_w_turned(t - 2)
                if o < 2:
                    scores(t, i, o + 2)
                elif more:
                    scores(t + 1, 1 - i, o - 2)
                if o == 0 and more:
                    q_project(t + 1)
                    k_turn(t + 1)
                if o == 1 and more:
                    q_turn(t + 1)
                    v_project(t + 1)
                if o == 2:
                    if has_two_after(t):
                        x_turned(t + 2)
                    if not (isinstance(t, int) and t == 0):
                        output_product(t - 1, 1 - i)
                if o == 3 and has_experts(t):
                    d_output(t - 2)
                if o == 3 and has_two_after(t):
                    k_project(t + 2)
                if o == 0 and has_experts(t):
                    d_x_turned(t - 2)
                if o == 1 and has_experts(t):
                    router(t - 2)
                outputs(t, i, o)
            run(pe, slot)
            output_product(TT - 1, 1)
            for t in range(TT - 2, TT):
                d_x_turned(t)
                router(t)
                d_w_turned(t)
                d_output(t)


def build(nc, **env):
    with ExitStack() as ctx:
        def sb(name, shape, dt=F32):
            return ctx.enter_context(nc.sbuf_tensor(name, shape, dt))

        def sem(name):
            return ctx.enter_context(nc.semaphore(name))

        env["ident"] = sb("ident", [P, P])
        env["minus_half"] = sb("minus_half", [P, 1])
        env["x1"] = sb("x1", [P, TT, D])
        env["kv_stored"] = [sem(f"kv_stored{i}") for i in range(2)]
        env["wq_in"] = [sem(f"wq_in{i}") for i in range(2)]
        env["wq_high"], env["wq_low"] = sem("wq_high"), sem("wq_low")
        env["q_ps"] = sem("q_ps")
        with ExitStack() as latents_kept:
            env["xnT"] = [latents_kept.enter_context(nc.sbuf_tensor(f"xnT_{n}", [P, KT, TT * P], F32R)) for n in "hl"]
            env["wq_f"] = latents_kept.enter_context(nc.sbuf_tensor("wq_f", [P, 2, KT, HD], F32))
            env["wq_split"] = [latents_kept.enter_context(nc.sbuf_tensor(f"wq_{n}", [P, 2, KT, HD], F32R))
                               for n in "hl"]
            stage_keys_values(nc, env)
            stage_cross_attention(nc, env)
        stage_self_attention_and_experts(nc, env)


def kernel(**inputs):
    import concourse.bacc as bacc
    from concourse.bass_utils import run_bass_kernel_spmd

    a = {n: np.asarray(v) for n, v in inputs.items()}
    order = np.arange(D).reshape(2, 2, 2, 4, SD).transpose(0, 2, 1, 3, 4).reshape(-1)
    half = np.arange(P) % NL
    angle = np.outer(half, 1.0 / 10000.0 ** (np.arange(0, SD, 2).astype(np.float32) / SD)).astype(np.float32)
    arrays = dict(
        x=a["x"].reshape(TT, P, D),
        ctxT=a["ctx_4096"].reshape(TT, 2, NC, KT, P).transpose(0, 4, 3, 1, 2).reshape(TT, P, KT * 2 * NC),
        wq=a["L0_xattn_Wq"].reshape(KT, P, HK * G, HD).transpose(2, 1, 0, 3).reshape(HK * G, P, KT * HD),
        wk=a["L0_xattn_Wk"], wv=a["L0_xattn_Wv"], wo=a["L0_xattn_Wo"],
        c_wq=a["L0_attn_wq"], c_wk=a["L0_attn_wk"], c_wv=a["L0_attn_wv"][:, order], c_wo=a["L0_attn_wo"][order],
        router_wT=a["L0_ffn_router_weight"].T, router_bias=a["L0_ffn_router_bias"],
        expert_bias=a["L0_ffn_expert_bias"],
        cos=np.repeat(np.cos(angle), 2, axis=1),
        sin=np.repeat(np.sin(angle), 2, axis=1) * np.tile(np.array([-1, 1], np.float32), SD // 2),
        bmask=(half[:, None] // SD == np.arange(4)).astype(np.float32),
        cmask=np.tile(np.where(half[:, None] >= np.arange(NL), 0, -1e30).astype(np.float32), (1, 8)),
    )
    arrays = {n: np.ascontiguousarray(v) for n, v in arrays.items()}
    nc = bacc.Bacc("TRN2", target_bir_lowering=False, num_devices=1)
    env = {n: nc.dram_tensor(f"in_{n}", v.shape, mybir.dt.from_np(v.dtype), kind="ExternalInput").ap()
           for n, v in arrays.items()}
    env["kv_dram"] = nc.dram_tensor("kv_dram", (TT, P, HK * KV), F32, kind="Internal").ap()
    env["out"] = nc.dram_tensor("out", (TT, P, D), F32, kind="ExternalOutput").ap()
    build(nc, **env)
    r = run_bass_kernel_spmd(nc, [{f"in_{n}": v for n, v in arrays.items()}], core_ids=[0])
    return r.results[0]["out"].reshape(B, NL, D)
```

```python
from contextlib import ExitStack

import concourse.bass as bass
from concourse import mybir
import numpy as np

F32 = mybir.dt.float32
F32R = mybir.dt.float32r
ALU = mybir.AluOpType
ACT = mybir.ActivationFunctionType
AX = mybir.AxisListType

P = 128
D = 512
KT = D // P
B, NL, NC = 16, 64, 128
NK = NL + NC
TT = B * NL // P
HK, G, HD = 4, 8, 128
XS = float(HD) ** -0.5
SD = 16
E = 64
KV = 2 * NK + 3 * HD
EPS = 1e-5
PASSES = ((0, 0), (0, 1), (1, 0))


def wait_pos(eng, sem, value):
    if isinstance(value, int) and value <= 0:
        return
    eng.wait_ge(sem, value)


def wait_apart(eng, sem, value):
    if not isinstance(value, int):
        value = eng.to_reg(value)
        eng.wait_ge(sem, 1)
    wait_pos(eng, sem, value)


def contexts(seq):
    return seq[:].rearrange("p k (c n) -> p k c n", c=3)[:, :, 0:3:2, :]


def latents(seq):
    return seq[:, :, NC:NC + P]


def load_wq(sp, env, c, i):
    wait_pos(sp, env["wq_low"], c - 1)
    row = (c // (2 * G)) * G + c % G
    sp.dma_start(env["wq_f"][:, i], env["wq"][bass.ds(row, 1)].rearrange("r p (k d) -> p (r k) d", k=KT))\
        .then_inc(env["wq_in"][i], 16)


def high_wq(act, env, c, i, uses):
    act.wait_ge(env["wq_in"][i], 16 * uses)
    wait_pos(act, env["q_ps"], c - 1)
    act.activation(env["wq_split"][0][:, i], env["wq_f"][:, i], ACT.Copy).then_inc(env["wq_high"], 1)


def low_wq(dve, env, c, i):
    dve.wait_ge(env["wq_high"], c + 1)
    dve.tensor_tensor(env["wq_split"][1][:, i], env["wq_f"][:, i], env["wq_split"][0][:, i].bitcast(F32),
                      ALU.subtract).then_inc(env["wq_low"], 1)


def next_stage_views(env):
    xnT, q_all, wq_f, wq_split = env["xnT"], env["q_all"], env["wq_f"], env["wq_split"]
    env["c_w_f"] = [q_all[:, 0, i * KT:(i + 1) * KT, :] for i in range(2)]
    env["c_w"] = {name: [xnT[n][:, :, i * D:(i + 1) * D] for i in range(2)] for n, name in enumerate("kq")}
    env["c_rows"] = [q_all[:, 1, i, :] for i in range(G)]
    env["c_xn"], env["d_xn"] = (wq_f[:, i].rearrange("p k n -> p (k n)") for i in range(2))
    env["c_xT"], env["d_xT"] = ([w[:, i] for w in wq_split] for i in range(2))


def c_load_w(sp, env, n):
    sp.dma_start(env["c_w_f"][n % 2], env["c_w" + "kqvo"[n]].rearrange("(k p) n -> p k n", p=P))\
        .then_inc(env["c_w_in"][n], 16)


def c_high_slice(act, env, n, k):
    act.wait_ge(env["c_w_in"][n], 16)
    act.activation(env["c_w"]["kq"[n]][0][:, k, :], env["c_w_f"][n][:, k, :], ACT.Copy).then_inc(env["c_w_high"], 1)


def c_low_slice(dve, env, n, k):
    high, low = (w[:, k, :] for w in env["c_w"]["kq"[n]])
    dve.wait_ge(env["c_w_high"], KT * n + k + 1)
    dve.tensor_tensor(low, env["c_w_f"][n][:, k, :], high.bitcast(F32), ALU.subtract).then_inc(env["c_w_low"], 1)


def c_weights_split(n):
    return KT * min(n + 1, 2) + max(n - 1, 0)


def c_tile(env, t):
    return env["x1"][:, bass.ds(t, 1), :].rearrange("p t d -> p (t d)")


def c_statistics(dve, env, t):
    wait_pos(dve, env["c_xn_ready"], t)
    dve.bn_stats(env["c_stats"][:], c_tile(env, t)).then_inc(env["c_stats_ready"], 1)
    wait_apart(dve, env["c_stats_ready"], 2 * t + 1)
    dve.bn_aggr(env["c_mv"][:], env["c_stats"][:]).then_inc(env["c_stats_ready"], 1)


def c_inverse_deviation(pool, env, t):
    wait_apart(pool, env["c_stats_ready"], 2 * t + 2)
    pool.tensor_scalar(env["c_var"][:], env["c_mv"][:, 1:2], EPS, None, ALU.add).then_inc(env["c_var_ready"], 1)
    pool.wait_ge(env["c_var_ready"], t + 1)
    pool.tensor_tensor(env["c_rstd"][:], env["c_var"][:], env["minus_half"][:], ALU.pow)\
        .then_inc(env["c_rstd_ready"], 1)


def c_normalised(dve, env, t):
    dve.wait_ge(env["c_rstd_ready"], t + 1)
    wait_pos(dve, env["c_xT_ps"], t)
    dve.tensor_scalar(env["c_xn"], c_tile(env, t), env["c_mv"][:, 0:1], env["c_rstd"][:], ALU.subtract, ALU.mult)\
        .then_inc(env["c_xn_ready"], 1)


def c_x_turned(pe, env, t, bank):
    pe.wait_ge(env["c_xn_ready"], t + 1)
    for k in range(KT):
        last = pe.transpose(bank[:, k * P:(k + 1) * P], env["c_xn"][:, k * P:(k + 1) * P], env["ident"][:])
    last.then_inc(env["c_xT_ps"], 1)


def c_high_x(act, env, t, bank):
    act.wait_ge(env["c_xT_ps"], t + 1)
    wait_pos(act, env["vp_ps"], t)
    act.activation(env["c_xT"][0].rearrange("p k n -> p (k n)"), bank[:], ACT.Copy).then_inc(env["c_xT_high"], 1)


def c_low_x(dve, env, t, bank):
    high, low = (a.rearrange("p k n -> p (k n)") for a in env["c_xT"])
    dve.wait_ge(env["c_xT_high"], t + 1)
    dve.tensor_tensor(low, bank[:], high.bitcast(F32), ALU.subtract).then_inc(env["c_xT_low"], 1)


def stage_keys_values(nc, env):
    ctx = ExitStack()
    with ctx:
        def sb(name, shape, dt=F32):
            return ctx.enter_context(nc.sbuf_tensor(name, shape, dt))

        def ps(name):
            return ctx.enter_context(nc.psum_tensor(name, [P, 512], F32))

        def sem(name):
            return ctx.enter_context(nc.semaphore(name))

        x1, xnT, ident = env["x1"], env["xnT"], env["ident"]
        wk_f = sb("wk_f", [P, KT, D])
        wv_f = sb("wv_f", [P, KT, D])
        wk = [sb(f"wk_{n}", [P, KT, D], F32R) for n in "hl"]
        wv = [sb(f"wv_{n}", [P, KT, D], F32R) for n in "hl"]
        ctx_f = [sb(f"ctx_f{i}", [P, KT, 2, NC]) for i in range(2)]
        seq = [[sb(f"seq{i}_{n}", [P, KT, 2 * NK], F32R) for n in "hl"] for i in range(2)]
        stats = sb("a_stats", [P, 2, 6])
        mv = sb("a_mv", [P, 2, 2])
        var = sb("a_var", [P, 2, 1])
        rstd = sb("a_rstd", [P, 2, 1])
        minus_half = env["minus_half"]
        xn = sb("a_xn", [P, 2, D])
        kv = [sb(f"kv_out{i}", [P, HK, KV]) for i in range(2)]
        first, second, all_k = slice(0, KT // 2), slice(KT // 2, KT), slice(0, KT)
        weight_parts = ((wv_f[:, first], first, env["wv"]), (wv_f[:, second], second, env["wv"]),
                        (wk_f[:], all_k, env["wk"]))
        split_parts = [[w[:, rows] for w in ws] for ws, rows in ((wv, first), (wv, second), (wk, all_k))]
        ps_t = ps("a_ps_t")
        ps_k = [ps(f"a_ps_k{i}") for i in range(2)]
        ps_v = [ps(f"a_ps_v{i}") for i in range(3)]

        ident_ready = sem("ident_ready")
        w_in = [sem(f"a_w_in{i}") for i in range(3)]
        x_in = [sem(f"a_x_in{i}") for i in range(2)]
        ctx_in = [sem(f"a_ctx_in{i}") for i in range(2)]
        kv_stored = env["kv_stored"]
        w_high = sem("a_w_high")
        w_low = sem("a_w_low")
        ln_steps = sem("a_ln_steps")
        var_ready = sem("a_var_ready")
        rstd_ready = sem("a_rstd_ready")
        xn_ready = sem("a_xn_ready")
        xnT_ps = sem("a_xnT_ps")
        ctx_high = sem("a_ctx_high")
        ctx_low = sem("a_ctx_low")
        lat_high = sem("a_lat_high")
        lat_low = sem("a_lat_low")
        lat_kept = sem("a_lat_kept")
        k_ps = sem("a_k_ps")
        v_ps = sem("a_v_ps")
        k_out = sem("a_k_out")
        v_out = sem("a_v_out")
        block = ctx.enter_context(nc.Block())

        @block.sync
        def _(sp):
            def load(t, i):
                wait_pos(sp, xn_ready, t - 1)
                sp.dma_start(x1[:, bass.ds(t, 1), :], env["x"][bass.ds(t, 1)].rearrange("t p d -> p t d"))\
                    .then_inc(x_in[i], 16)
                wait_pos(sp, ctx_low, t - 1)
                sp.dma_start(ctx_f[i][:], env["ctxT"][bass.ds(t, 1)].rearrange("t p c -> p (t c)")
                             .rearrange("p (k b n) -> p k b n", k=KT, b=2)).then_inc(ctx_in[i], 16)

            def store(t, i):
                wait_apart(sp, k_out, HK * (t + 1))
                sp.wait_ge(v_out, 3 * (t + 1))
                sp.dma_start(env["kv_dram"][bass.ds(t, 1)].rearrange("t p c -> p (t c)"),
                             kv[i][:].rearrange("p h c -> p (h c)")).then_inc(kv_stored[i], 16)

            load(0, 0)
            for n, (f, rows, w) in enumerate(weight_parts):
                sp.dma_start(f, w.rearrange("(k p) n -> p k n", p=P)[:, rows, :]).then_inc(w_in[n], 16)
            load(1, 1)
            with sp.Fori(0, TT // 2 - 1) as tb:
                for i in range(2):
                    load(2 * tb + 2 + i, i)
                    store(2 * tb + i, i)
            load_wq(sp, env, 0, 0)
            load_wq(sp, env, 1, 1)
            for i in range(2):
                store(TT - 2 + i, i)
            load_wq(sp, env, 2, 0)
            load_wq(sp, env, 3, 1)

        @block.gpsimd
        def _(pool):
            pool.memset(ident[:], 0.0).then_inc(ident_ready, 1)
            pool.wait_ge(ident_ready, 1)
            pool.affine_select(out=ident[:], in_=ident[:], compare_op=ALU.not_equal, fill=1.0, base=0,
                               pattern=[[-1, P]], channel_multiplier=1).then_inc(ident_ready, 1)
            pool.memset(minus_half[:], -0.5).then_inc(ident_ready, 1)
            def inverse_deviation(t, i):
                wait_apart(pool, ln_steps, 2 * t + 2)
                pool.tensor_scalar(var[:, i, :], mv[:, i, 1:2], EPS, None, ALU.add).then_inc(var_ready, 1)
                pool.wait_ge(var_ready, t + 1)
                pool.tensor_tensor(rstd[:, i, :], var[:, i, :], minus_half[:], ALU.pow).then_inc(rstd_ready, 1)

            def keep_latents(t, i):
                pool.wait_ge(lat_low, t + 1)
                for n in range(2):
                    last = pool.tensor_copy(xnT[n][:, :, bass.ds(t * P, P)], latents(seq[i][n]).bitcast(F32))
                last.then_inc(lat_kept, 1)

            pool.wait_ge(ident_ready, 3)
            inverse_deviation(0, 0)
            inverse_deviation(1, 1)
            with pool.Fori(0, TT // 2 - 1) as tb:
                for i in range(2):
                    inverse_deviation(2 * tb + 2 + i, i)
                    keep_latents(2 * tb + i, i)
            keep_latents(TT - 2, 0)
            keep_latents(TT - 1, 1)

        @block.scalar
        def _(act):
            def split_ctx(tb, i):
                t = 2 * tb + i
                act.wait_ge(ctx_in[i], 16 * (tb + 1))
                wait_pos(act, v_ps, 3 * (t - 1))
                act.activation(contexts(seq[i][0]), ctx_f[i][:], ACT.Copy).then_inc(ctx_high, 1)

            def split_latents(tb, i):
                t = 2 * tb + i
                act.wait_ge(xnT_ps, t + 1)
                wait_pos(act, lat_kept, t - 1)
                act.activation(latents(seq[i][0]), ps_t[:].rearrange("p (k n) -> p k n", k=KT),
                               ACT.Copy).then_inc(lat_high, 1)

            def values_out(tb, i, cs):
                t = 2 * tb + i
                wait_pos(act, kv_stored[i], 16 * tb)
                for c in cs:
                    act.wait_ge(v_ps, 3 * t + c + 1)
                    act.activation(kv[i][:, :, 2 * NK + c * HD:2 * NK + (c + 1) * HD],
                                   ps_v[c][:].rearrange("p (h d) -> p h d", h=HK), ACT.Copy).then_inc(v_out, 1)

            split_ctx(0, 0)
            for n, (f, _, _) in enumerate(weight_parts):
                act.wait_ge(w_in[n], 16)
                act.activation(split_parts[n][0], f, ACT.Copy).then_inc(w_high, 1)
            split_latents(0, 0)
            split_ctx(0, 1)

            def two_tiles(tb):
                for i in range(2):
                    values_out(tb, i, (0,))
                    split_latents(tb + i, 1 - i)
                    values_out(tb, i, (1, 2))
                    split_ctx(tb + 1, i)

            two_tiles(0)
            with act.Fori(1, TT // 2 - 1) as tb:
                two_tiles(tb)
            values_out(TT // 2 - 1, 0, (0,))
            split_latents(TT // 2 - 1, 1)
            values_out(TT // 2 - 1, 0, (1, 2))
            for c in range(2):
                high_wq(act, env, c, c, 1)
            values_out(TT // 2 - 1, 1, (0, 1, 2))

        @block.vector
        def _(dve):
            def layernorm(tb, i):
                t = 2 * tb + i
                dve.wait_ge(x_in[i], 16 * (tb + 1))
                wait_pos(dve, xnT_ps, t - 1)
                xt = x1[:, bass.ds(t, 1), :].rearrange("p t d -> p (t d)")
                dve.bn_stats(stats[:, i, :], xt).then_inc(ln_steps, 1)
                wait_apart(dve, ln_steps, 2 * t + 1)
                dve.bn_aggr(mv[:, i, :], stats[:, i, :]).then_inc(ln_steps, 1)
                dve.wait_ge(rstd_ready, t + 1)
                dve.tensor_scalar(xn[:, i, :], xt, mv[:, i, 0:1], rstd[:, i, :], ALU.subtract, ALU.mult)\
                    .then_inc(xn_ready, 1)

            def split_ctx(tb, i):
                t = 2 * tb + i
                dve.wait_ge(ctx_high, t + 1)
                dve.tensor_tensor(contexts(seq[i][1]), ctx_f[i][:], contexts(seq[i][0]).bitcast(F32),
                                  ALU.subtract).then_inc(ctx_low, 1)

            def split_latents(tb, i):
                t = 2 * tb + i
                dve.wait_ge(lat_high, t + 1)
                dve.tensor_tensor(latents(seq[i][1]), ps_t[:].rearrange("p (k n) -> p k n", k=KT),
                                  latents(seq[i][0]).bitcast(F32), ALU.subtract).then_inc(lat_low, 1)

            def keys_out(tb, i):
                t = 2 * tb + i
                wait_pos(dve, kv_stored[i], 16 * tb)
                for h in range(HK):
                    dve.wait_ge(k_ps, HK * t + h + 1)
                    dve.tensor_copy(kv[i][:, h, 0:2 * NK], ps_k[h % 2][:, 0:2 * NK]).then_inc(k_out, 1)

            layernorm(0, 0)
            split_ctx(0, 0)
            for n, (f, _, _) in enumerate(weight_parts):
                high, low = split_parts[n]
                dve.wait_ge(w_high, n + 1)
                dve.tensor_tensor(low, f, high.bitcast(F32), ALU.subtract).then_inc(w_low, 1)
            split_latents(0, 0)
            layernorm(0, 1)
            split_ctx(0, 1)

            def two_tiles(tb):
                for i in range(2):
                    split_latents(tb + i, 1 - i)
                    keys_out(tb, i)
                    layernorm(tb + 1, i)
                    split_ctx(tb + 1, i)

            two_tiles(0)
            with dve.Fori(1, TT // 2 - 1) as tb:
                two_tiles(tb)
            split_latents(TT // 2 - 1, 1)
            keys_out(TT // 2 - 1, 0)
            for c in range(2):
                low_wq(dve, env, c, c)
            keys_out(TT // 2 - 1, 1)

        @block.tensor
        def _(pe):
            def transposes(t, i):
                pe.wait_ge(xn_ready, t + 1)
                wait_pos(pe, lat_low, t)
                for k in range(KT):
                    last = pe.transpose(ps_t[:, k * P:(k + 1) * P], xn[:, i, k * P:(k + 1) * P], ident[:])
                last.then_inc(xnT_ps, 1)

            def value(t, i, c, first=False):
                wait_pos(pe, v_out, 3 * (t - 1) + c + 1)
                n = 0
                for a, b in PASSES:
                    if first and b == 1:
                        pe.wait_ge(w_low, 2)
                    for k in range(KT):
                        last = pe.matmul(ps_v[c][:], seq[i][a][:, k, (0, 2 * P, P)[c]:][:, 0:P], wv[b][:, k, :], start=(n == 0), stop=(n == 3 * KT - 1))
                        n += 1
                last.then_inc(v_ps, 1)

            def keys(t, i, h):
                wait_pos(pe, k_out, HK * t + h - 1)
                n = 0
                for a, b in PASSES:
                    for k in range(KT):
                        last = pe.matmul(ps_k[h % 2][:, 0:2 * NK], wk[a][:, k, h * HD:(h + 1) * HD],
                                         seq[i][b][:, k, :], start=(n == 0), stop=(n == 3 * KT - 1))
                        n += 1
                last.then_inc(k_ps, 1)

            def step(t, i, first=False, last=False):
                pe.wait_ge(ctx_low, t + 1)
                if first:
                    pe.wait_ge(w_high, 2)
                value(t, i, 0, first)
                if not (first or last):
                    transposes(t + 1, 1 - i)
                value(t, i, 1)
                if first:
                    transposes(t + 1, 1 - i)
                if first:
                    pe.wait_ge(w_low, 3)
                pe.wait_ge(lat_low, t + 1)
                for h in range(HK):
                    keys(t, i, h)
                value(t, i, 2)

            pe.wait_ge(ident_ready, 2)
            transposes(0, 0)
            step(0, 0, first=True)
            step(1, 1)
            with pe.Fori(1, TT // 2 - 1) as tb:
                for i in range(2):
                    step(2 * tb + i, i)
            step(TT - 2, 0)
            step(TT - 1, 1, last=True)


def stage_cross_attention(nc, env):
    ctx = ExitStack()
    with ctx:
        def sb(name, shape, dt=F32):
            return ctx.enter_context(nc.sbuf_tensor(name, shape, dt))

        def ps(name):
            return ctx.enter_context(nc.psum_tensor(name, [P, 512], F32))

        def sem(name):
            return ctx.enter_context(nc.semaphore(name))

        HALF = TT // 2
        HT = HALF * P
        STEPS = HK * B
        BODIES = STEPS // 4
        VO = 2 * NK
        WO_RING = G + 4

        x1, xnT, ident = env["x1"], env["xnT"], env["ident"]
        wq = env["wq_split"]
        wo_f = sb("wo_f", [P, 2, D])
        wo = [sb(f"wo_{n}", [P, WO_RING, D], F32R) for n in "hl"]
        kv_f = sb("kv_f", [P, 2, KV])
        kv = [sb(f"kv_{n}", [P, 2, KV], F32R) for n in "hl"]
        q_all = env["q_all"]
        q = [sb(f"q_{n}", [P, 2, G, NL], F32R) for n in "hl"]
        probs = [sb(f"probs{i}", [P, NL + 4 * NK]) for i in range(2)]
        pT_ctx = [sb(f"pT_ctx_{n}", [P, 512], F32R) for n in "hl"]
        pT_lat = [sb(f"pT_lat_{n}", [P, 512], F32R) for n in "hl"]
        oT = [sb(f"oT_{n}", [P, 2, G, P], F32R) for n in "hl"]
        nmax = sb("nmax", [P, 2, 4])
        psum_p = sb("psum_p", [P, 2, 4])
        rsum = sb("rsum", [P, 2, 4])
        ps_q = [ps(f"ps_q{i}") for i in range(2)]
        ps_s = [ps(f"ps_s{i}") for i in range(2)]
        ps_tc, ps_tl, ps_o, ps_y = ps("ps_tc"), ps("ps_tl"), ps("ps_o"), ps("ps_y")

        wo_in = [sem(f"wo_in{i}") for i in range(2)]
        kv_in = [sem(f"kv_in{i}") for i in range(2)]
        wq_low, q_ps = env["wq_low"], env["q_ps"]
        wo_high, wo_low = sem("wo_high"), sem("wo_low")
        kv_high, kv_low = sem("kv_high"), sem("kv_low")
        q_high, q_low = sem("q_high"), sem("q_low")
        q_out = sem("q_out")
        s_ps = sem("s_ps")
        pad_ready = sem("pad_ready")
        max_ready = sem("max_ready")
        exp_done = sem("exp_done")
        rsum_ready = sem("rsum_ready")
        probs_ready = sem("probs_ready")
        pT_ps = sem("pT_ps")
        pT_high, pT_low = sem("pT_high"), sem("pT_low")
        o_ps = sem("o_ps")
        oT_high, oT_low = sem("oT_high"), sem("oT_low")
        y_head = sem("y_head")
        x_added = sem("x_added")
        block = ctx.enter_context(nc.Block())

        @block.sync
        def _(sp):
            def load_kv(pair, i):
                wait_pos(sp, kv_low, pair - 1)
                t, h = pair % TT, pair // TT
                sp.dma_start(kv_f[:, i, :], env["kv_dram"][bass.ds(t, 1), :, bass.ds(h * KV, KV)]
                             .rearrange("t p c -> p (t c)")).then_inc(kv_in[i], 16)

            for i in range(2):
                sp.wait_ge(env["kv_stored"][i], 16 * (TT // 2))
                load_kv(i, i)
            for c in range(4, G + 2):
                load_wq(sp, env, c, c % 2)

            def body(bi, more_wq=4, more_kv=2):
                for k in range(4):
                    if k < more_wq:
                        load_wq(sp, env, 4 * bi + k + G + 2, k % 2)
                    if k % 2 and k // 2 < more_kv:
                        load_kv(2 * bi + 2 + k // 2, k // 2)

            with sp.Fori(0, BODIES - 3) as bi:
                body(bi)
            body(BODIES - 3, more_wq=2)
            sp.wait_ge(q_ps, 2 * HK * G)
            for n in range(2):
                c_load_w(sp, env, n)
            body(BODIES - 2, more_wq=0)

        @block.gpsimd
        def _(pool):
            def load_wo(w, i):
                wait_pos(pool, wo_low, w - 1)
                pool.dma_start(wo_f[:, i, :], env["wo"][bass.ds(w * HD, HD), :]).then_inc(wo_in[i], 16)

            def split_wo(w, i):
                pool.wait_ge(wo_in[i], 16 * (w // 2 + 1))
                old = w - WO_RING
                wait_apart(pool, y_head, (old // G * TT + TT - 1) * G + old % G + 1)
                place = bass.ds(w % WO_RING, 1)
                pool.tensor_copy(wo[0][:, place, :], wo_f[:, i:i + 1, :]).then_inc(wo_high, 1)
                wait_apart(pool, wo_high, w + 1)
                pool.tensor_tensor(wo[1][:, place, :], wo_f[:, i:i + 1, :], wo[0][:, place, :].bitcast(F32),
                                   ALU.subtract).then_inc(wo_low, 1)

            load_wo(0, 0)
            load_wo(1, 1)
            for w in range(WO_RING):
                split_wo(w, w % 2)
                load_wo(w + 2, w % 2)
            with pool.Fori(WO_RING // 2, HK * G // 2 - 1) as half:
                for i in range(2):
                    split_wo(2 * half + i, i)
                    load_wo(2 * half + i + 2, i)
            for i in range(2):
                split_wo(HK * G - 2 + i, i)
            c_inverse_deviation(pool, env, 0)

        def step_queries(bi, k):
            return q_all[:, bass.ds((bi // 2) % 2, 1), :, bass.ds((bi % 2) * 4 * NL + k * NL, NL)]\
                .rearrange("p a g t -> p (a g) t")

        def before(bi, k):
            return (bi, k - 1) if k else (bi - 1, 3)

        def after(bi, k):
            return (bi, k + 1) if k < 3 else (bi + 1, 0)

        def tail_slice(bi, k):
            return 4 * bi + k - (STEPS - 2 * KT + 1) if isinstance(bi, int) else -1

        @block.scalar
        def _(act):
            def queries_out(c, i, parity, g):
                act.wait_ge(q_ps, c + 1)
                act.activation(q_all[:, bass.ds(parity, 1), bass.ds(g, 1), :].rearrange("p a g t -> p (a g t)"),
                               ps_q[i][:], ACT.Copy, scale=XS).then_inc(q_out, 1)

            def split_kv(pair, i, uses):
                act.wait_ge(kv_in[i], 16 * uses)
                wait_pos(act, o_ps, 2 * (pair - 1))
                act.activation(kv[0][:, i, :], kv_f[:, i, :], ACT.Copy).then_inc(kv_high, 1)

            def split_q(bi, k):
                n = 4 * bi + k
                wait_pos(act, s_ps, 2 * (n - 1))
                act.wait_ge(q_out, (bi // 2 + 1) * G)
                act.activation(q[0][:, k % 2], step_queries(bi, k), ACT.Copy).then_inc(q_high, 1)

            def softmax(bi, k):
                n, i = 4 * bi + k, k % 2
                wait_pos(act, pT_ps, 2 * (n - 1))
                for j in range(4):
                    if j % 2 == 0:
                        act.wait_ge(max_ready, 2 * n + j // 2 + 1)
                    act.activation(probs[i][:, NL + j * NK:NL + (j + 1) * NK],
                                   ps_s[j // 2][:, (j % 2) * NK:(j % 2 + 1) * NK], ACT.Exp,
                                   bias=nmax[:, i, j:j + 1], accum_out=psum_p[:, i, j:j + 1]).then_inc(exp_done, 1)

            def split_probs(bi, k):
                n, rows = 4 * bi + k, slice(k % 2 * NL, k % 2 * NL + NL)
                wait_pos(act, o_ps, n)
                act.wait_ge(pT_ps, 2 * n + 1)
                act.activation(pT_ctx[0][:], ps_tc[:], ACT.Copy).then_inc(pT_high, 1)
                act.wait_ge(pT_ps, 2 * n + 2)
                act.activation(pT_lat[0][rows, :], ps_tl[rows, :], ACT.Copy).then_inc(pT_high, 1)

            def split_out(bi, k):
                n, pair = 4 * bi + k, 2 * bi + k // 2
                act.wait_ge(o_ps, n + 1)
                wait_pos(act, y_head, (pair - 1) * G)
                act.activation(oT[0][:, k // 2, :, k % 2 * NL:(k % 2 + 1) * NL],
                               ps_o[:].rearrange("p (g t) -> p g t", g=G), ACT.Copy).then_inc(oT_high, 1)

            def body(bi, queries=4, wqs=4, first=False, last=False):
                for k in range(4):
                    n = 4 * bi + k
                    softmax(bi, k)
                    if not (first and k == 0):
                        split_out(*before(bi, k))
                    if k < wqs:
                        high_wq(act, env, n + G + 1, (k + 1) % 2, 2 * bi + (k + G + 1) // 2 + 1)
                    if k % 2 == 0 and not (last and k == 2):
                        split_kv(2 * bi + k // 2 + 1, (k // 2 + 1) % 2, bi + k // 2 + 1)
                    if k < queries:
                        queries_out(n + G, k % 2, (bi // 2 + 1) % 2, (bi % 2) * 4 + k)
                    if not (last and k == 3):
                        split_q(*after(bi, k))
                    split_probs(bi, k)
                    if tail_slice(bi, k) >= 0:
                        c_high_slice(act, env, *divmod(tail_slice(bi, k), KT))

            for c in range(G):
                if c >= 2:
                    high_wq(act, env, c, c % 2, c // 2 + 1)
                if c:
                    queries_out(c - 1, (c - 1) % 2, 0, c - 1)
                if c == 5:
                    split_kv(0, 0, 1)
            high_wq(act, env, G, 0, G // 2 + 1)
            queries_out(G - 1, 1, 0, G - 1)
            split_q(0, 0)
            body(0, first=True)
            with act.Fori(1, BODIES - 3) as bi:
                body(bi)
            body(BODIES - 3, wqs=3)
            body(BODIES - 2, queries=0, wqs=0)
            body(BODIES - 1, queries=0, wqs=0, last=True)
            split_out(BODIES - 1, 3)
            c_high_x(act, env, 0, ps_q[0])
            c_high_slice(act, env, 1, KT - 1)

        @block.vector
        def _(dve):
            def low_kv(pair, i):
                dve.wait_ge(kv_high, pair + 1)
                dve.tensor_tensor(kv[1][:, i, :], kv_f[:, i, :], kv[0][:, i, :].bitcast(F32), ALU.subtract)\
                    .then_inc(kv_low, 1)

            def low_q(bi, k):
                dve.wait_ge(q_high, 4 * bi + k + 1)
                dve.tensor_tensor(q[1][:, k % 2], step_queries(bi, k), q[0][:, k % 2].bitcast(F32), ALU.subtract)\
                    .then_inc(q_low, 1)

            def row_max(bi, k):
                n, i = 4 * bi + k, k % 2
                for j in range(2):
                    dve.wait_ge(s_ps, 2 * n + j + 1)
                    dve.tensor_reduce(nmax[:, i, 2 * j:2 * j + 2],
                                      ps_s[j][:, 0:2 * NK].rearrange("p (j n) -> p j n", j=2), AX.X, ALU.max,
                                      negate=True).then_inc(max_ready, 1)

            def normalise(bi, k):
                n, i = 4 * bi + k, k % 2
                dve.wait_ge(exp_done, 4 * (n + 1))
                dve.reciprocal(rsum[:, i, :], psum_p[:, i, :]).then_inc(rsum_ready, 1)
                dve.wait_ge(rsum_ready, n + 1)
                for j in range(4):
                    p = probs[i][:, NL + j * NK:NL + (j + 1) * NK]
                    last = dve.tensor_scalar(p, p, rsum[:, i, j:j + 1], None, ALU.mult)
                last.then_inc(probs_ready, 1)

            def low_probs(bi, k):
                n, rows = 4 * bi + k, slice(k % 2 * NL, k % 2 * NL + NL)
                dve.wait_ge(pT_high, 2 * n + 1)
                dve.tensor_tensor(pT_ctx[1][:], ps_tc[:], pT_ctx[0][:].bitcast(F32), ALU.subtract).then_inc(pT_low, 1)
                dve.wait_ge(pT_high, 2 * n + 2)
                dve.tensor_tensor(pT_lat[1][rows, :], ps_tl[rows, :], pT_lat[0][rows, :].bitcast(F32), ALU.subtract)\
                    .then_inc(pT_low, 1)

            def add_output(pair):
                dve.wait_ge(y_head, (pair + 1) * G)
                xt = x1[:, bass.ds(pair % TT, 1), :].rearrange("p t d -> p (t d)")
                dve.tensor_tensor(xt, ps_y[:], xt, ALU.add).then_inc(x_added, 1)

            def low_out(bi, k):
                dve.wait_ge(oT_high, 4 * bi + k + 1)
                cols = slice(k % 2 * NL, (k % 2 + 1) * NL)
                dve.tensor_tensor(oT[1][:, k // 2, :, cols], ps_o[:].rearrange("p (g t) -> p g t", g=G),
                                  oT[0][:, k // 2, :, cols].bitcast(F32), ALU.subtract).then_inc(oT_low, 1)

            def body(bi, wqs=4, first=False, last=False):
                for k in range(4):
                    row_max(bi, k)
                    if k % 2 and not first:
                        add_output(2 * bi + k // 2 - 2)
                    normalise(bi, k)
                    if not (first and k == 0):
                        low_out(*before(bi, k))
                    if k < wqs:
                        low_wq(dve, env, 4 * bi + k + G + 1, (k + 1) % 2)
                    if k % 2 == 0 and not (last and k == 2):
                        low_kv(2 * bi + k // 2 + 1, (k // 2 + 1) % 2)
                    if not (last and k == 3):
                        low_q(*after(bi, k))
                    low_probs(bi, k)
                    if tail_slice(bi, k) >= 0:
                        c_low_slice(dve, env, *divmod(tail_slice(bi, k), KT))
                    if last and k == 1:
                        c_statistics(dve, env, 0)
                    if last and k == 2:
                        c_normalised(dve, env, 0)

            dve.memset(probs[1][:, 0:NL], 0.0).then_inc(pad_ready, 1)
            for c in range(G):
                if c >= 2:
                    low_wq(dve, env, c, c % 2)
                if c == 5:
                    low_kv(0, 0)
            low_wq(dve, env, G, 0)
            low_q(0, 0)
            body(0, first=True)
            with dve.Fori(1, BODIES - 3) as bi:
                body(bi)
            body(BODIES - 3, wqs=3)
            body(BODIES - 2, wqs=0)
            body(BODIES - 1, wqs=0, last=True)
            low_out(BODIES - 1, 3)
            add_output(STEPS // 2 - 2)
            c_low_x(dve, env, 0, ps_q[0])
            c_low_slice(dve, env, 1, KT - 1)
            add_output(STEPS // 2 - 1)

        @block.tensor
        def _(pe):
            def product(out, pairs, **kw):
                for n, (lhsT, rhs) in enumerate(pairs):
                    last = pe.matmul(out, lhsT, rhs, start=(n == 0), stop=(n == len(pairs) - 1), **kw)
                return last

            def queries(c, i, half):
                pe.wait_ge(wq_low, c + 1)
                wait_pos(pe, q_out, c - 1)
                product(ps_q[i][:], [(wq[a][:, i, t, :], xnT[b][:, t, bass.ds(half * HT, HT)])
                                     for a, b in PASSES for t in range(KT)]).then_inc(q_ps, 1)

            def scores(bi, k):
                n, pair = 4 * bi + k, 2 * bi + k // 2
                keys = slice(k % 2 * NK, (k % 2 + 1) * NK)
                if k % 2 == 0:
                    pe.wait_ge(kv_low, pair + 1)
                pe.wait_ge(q_low, n + 1)
                for j in range(4):
                    if j % 2 == 0:
                        wait_pos(pe, exp_done, 4 * (n - 1) + j + 2)
                    last = product(ps_s[j // 2][:, (j % 2) * NK:(j % 2 + 1) * NK],
                                   [(q[a][:, k % 2, 2 * j:2 * j + 2, :].rearrange("p g t -> p (g t)"),
                                     kv[b][:, k // 2, keys]) for a, b in PASSES])
                    if j % 2:
                        last.then_inc(s_ps, 1)

            def transposes(bi, k):
                n, s = 4 * bi + k, k % 2
                pe.wait_ge(probs_ready, n + 1)
                wait_pos(pe, pT_low, 2 * n)
                for j in range(4):
                    start = NL + j * NK + (NL if s else 0)
                    last = pe.transpose(ps_tc[:, j * P:(j + 1) * P], probs[s][:, start:start + NC], ident[:])
                last.then_inc(pT_ps, 1)
                for j in range(4):
                    if s:
                        last = pe.transpose(ps_tl[:, j * P:(j + 1) * P], probs[s][:, j * NK:j * NK + P], ident[:])
                    else:
                        start = NL + j * NK + NC
                        last = pe.transpose(ps_tl[0:NL, j * P:(j + 1) * P], probs[s][:, start:start + NL], ident[:])
                last.then_inc(pT_ps, 1)

            def output_product(pair, i, heads):
                if 0 in heads:
                    pe.wait_ge(oT_low, 2 * (pair + 1))
                    wait_pos(pe, x_added, pair)
                for g in heads:
                    w = pair // TT * G + g
                    pe.wait_ge(wo_low, w + 1)
                    for n, (a, b) in enumerate(PASSES):
                        last = pe.matmul(ps_y[:], oT[a][:, i, g, :], wo[b][:, bass.ds(w % WO_RING, 1), :]
                                         .rearrange("p w d -> p (w d)"), start=(g == 0 and n == 0),
                                         stop=(g == G - 1 and n == 2))
                    last.then_inc(y_head, 1)

            def outputs(bi, k):
                n, i, s = 4 * bi + k, k // 2, k % 2
                lat = slice(s * NL, (s + 1) * NL)
                wait_pos(pe, oT_low, n)
                pe.wait_ge(pT_low, 2 * n + 1)
                for m, (a, b) in enumerate(PASSES):
                    pe.matmul(ps_o[:], kv[a][:, i, VO + s * HD:VO + (s + 1) * HD], pT_ctx[b][:], start=(m == 0),
                              stop=False)
                pe.wait_ge(pT_low, 2 * n + 2)
                for m, (a, b) in enumerate(PASSES):
                    last = pe.matmul(ps_o[:], kv[a][lat, i, VO + 2 * HD:VO + 3 * HD], pT_lat[b][lat, :], start=False,
                                     stop=(m == 2))
                last.then_inc(o_ps, 1)

            def body(bi, next_queries=True, first=False, last=False):
                for k in range(4):
                    pair, i, head = 2 * bi + (k - 3) // 2, (k + 1) // 2 % 2, (k + 1) % 2 * 4
                    if next_queries:
                        queries(4 * bi + k + G, k % 2, (bi // 2 + 1) % 2)
                    if not (first and k < 3):
                        output_product(pair, i, range(head, head + 3))
                    transposes(bi, k)
                    if not (first and k < 3):
                        output_product(pair, i, range(head + 3, head + 4))
                    if not (last and k == 3):
                        scores(*after(bi, k))
                    outputs(bi, k)

            for c in range(G):
                queries(c, c % 2, 0)
            pe.wait_ge(pad_ready, 1)
            scores(0, 0)
            body(0, first=True)
            with pe.Fori(1, BODIES - 2) as bi:
                body(bi)
            body(BODIES - 2, next_queries=False)
            body(BODIES - 1, next_queries=False, last=True)
            c_x_turned(pe, env, 0, ps_q[0])
            output_product(STEPS // 2 - 2, 0, range(G // 2, G))
            output_product(STEPS // 2 - 1, 1, range(G))


def stage_self_attention_and_experts(nc, env):
    ctx = ExitStack()
    with ctx:
        def sb(name, shape, dt=F32):
            return ctx.enter_context(nc.sbuf_tensor(name, shape, dt))

        def ps(name):
            return ctx.enter_context(nc.psum_tensor(name, [P, 512], F32))

        def sem(name):
            return ctx.enter_context(nc.semaphore(name))

        x1, ident, minus_half = env["x1"], env["ident"], env["minus_half"]
        names = ("k", "q", "v", "o")
        SCALE = float(SD) ** -0.5
        w_f = env["c_w_f"]
        w = dict(env["c_w"], **{n: [sb(f"c_w{n}_{p}", [P, KT, D], F32R) for p in "hl"] for n in "vo"})
        ident_r = sb("ident_r", [P, P], F32R)
        cmask_f, cmask = sb("c_mask_f", [P, D]), sb("c_mask", [P, D], F32R)
        bmask = sb("c_bmask", [P, 4])
        cos, sin = sb("c_cos", [P, SD]), sb("c_sin", [P, SD])
        xT = env["c_xT"]
        rows = iter(env["c_rows"])
        rot_a, rot_b = ({n: next(rows) for n in "kq"} for _ in range(2))
        kT = [sb(f"c_kT_{p}", [P, 4, P], F32R) for p in "hl"]
        qz = [[sb(f"qz{i}_{p}", [P, 4, 2, P], F32R) for p in "hl"] for i in range(2)]
        kblk = [[sb(f"kblk{s}_{p}", [P, 4, 4, NL], F32R) for p in "hl"] for s in range(2)]
        v_f, v_swap = next(rows), next(rows)
        vz = [[sb(f"vz{i}_{p}", [P, 2, D], F32R) for p in "hl"] for i in range(2)]
        probs = [next(rows) for _ in range(2)]
        nmax, psum_p, rsum = (sb(n, [P, 2, 8]) for n in ("c_nmax", "c_psum", "c_rsum"))
        pT = [sb(f"c_pT_{p}", [P, 4, P], F32R) for p in "hl"]
        oT = [sb(f"c_oT_{p}", [P, 2, 4, P], F32R) for p in "hl"]
        ps_t = ps("c_ps_t")
        ps_p = [ps(f"c_ps_p{i}") for i in range(2)]
        ps_s = [ps(f"c_ps_s{i}") for i in range(2)]
        ps_pt = ps("c_ps_pt")
        ps_o = ps("c_ps_o")

        rw = [sb(f"rw_{p}", [P, KT, E], F32R) for p in "hl"]
        eb = [sb(f"eb_{p}", [E, D], F32R) for p in "hl"]
        rbias = sb("rbias", [P, E])
        d_stats, d_mv = sb("d_stats", [P, 6]), sb("d_mv", [P, 2])
        d_var, d_rstd = sb("d_var", [P, 1]), sb("d_rstd", [P, 1])
        logits, d_probs, rest, chosen = (sb(n, [P, E]) for n in ("logits", "d_probs", "rest", "chosen"))
        d_nmax, d_psum, d_rsum, wsum = (sb(n, [P, 1]) for n in ("d_nmax", "d_psum", "d_rsum", "wsum"))
        top = sb("top", [P, 8])
        wT = [[sb(f"wT{i}_{p}", [E, P], F32R) for p in "hl"] for i in range(2)]
        d_own = dict(stored=sem("d_stored"), xn=env["d_xn"], xT=env["d_xT"], wT=wT[0], y=sb("y", [P, D])[:], bank=ps("ps_d"))
        d_spare = dict(stored=sem("d_spare_stored"), xn=env["c_xn"], xT=env["c_xT"], wT=wT[1], y=rot_a["k"], bank=ps_t)

        w_in = env["c_w_in"]
        table_in = [sem(f"c_table_in{i}") for i in range(5)]
        w_high, w_low = env["c_w_high"], env["c_w_low"]
        tables = sem("c_tables")
        qz_zeroed, vz_zeroed = sem("qz_zeroed"), [sem("vz_zeroed0"), sem("vz_zeroed1")]
        xT_low = env["c_xT_low"]
        kp_ps, qp_ps, vp_ps = sem("kp_ps"), sem("qp_ps"), env["vp_ps"]
        k_turned, q_turned = sem("k_turned"), sem("q_turned")
        k_rot, q_rot = sem("k_rot"), sem("q_rot")
        kT_ps, kT_high, kT_low = sem("c_kT_ps"), sem("c_kT_high"), sem("c_kT_low")
        qT_ps, qz_high, qz_low = sem("c_qT_ps"), sem("c_qz_high"), sem("c_qz_low")
        kblk_ready = sem("kblk_ready")
        v_out = sem("v_out_c")
        v_swapped = sem("v_swapped")
        vz_high, vz_low = sem("vz_high"), sem("vz_low")
        vz_even = sem("vz_even")
        s_ps, max_ready = sem("c_s_ps"), sem("c_max_ready")
        exp_done, rsum_ready = sem("c_exp_done"), sem("c_rsum_ready")
        probs_ready = sem("c_probs_ready")
        pT_ps, pT_high, pT_low = sem("c_pT_ps"), sem("c_pT_high"), sem("c_pT_low")
        o_ps, oT_high, oT_low = sem("c_o_ps"), sem("c_oT_high"), sem("c_oT_low")
        y_ps, x_added = sem("c_y_ps"), sem("c_x_added")
        d_stats_ready = sem("d_stats_ready")
        d_var_ready, d_rstd_ready = sem("d_var_ready"), sem("d_rstd_ready")
        d_xn_ready = sem("d_xn_ready")
        d_xT_ps, d_xT_high, d_xT_low = sem("d_xT_ps"), sem("d_xT_high"), sem("d_xT_low")
        l_ps = sem("l_ps")
        steps = sem("d_steps")
        d_exp_done = sem("d_exp_done")
        chosen_ready = sem("chosen_ready")
        wT_ps, wT_high, wT_low = sem("wT_ps"), sem("wT_high"), sem("wT_low")
        d_y_ps, y_part, y_ready = sem("d_y_ps"), sem("y_part"), sem("y_ready")
        block = ctx.enter_context(nc.Block())

        def tile(t):
            return x1[:, bass.ds(t, 1), :].rearrange("p t d -> p (t d)")

        def is_last(t):
            return isinstance(t, int) and t == TT - 1

        def has_two_after(t):
            return not isinstance(t, int) or t < TT - 2

        def run(eng, slot):
            def two_tiles(tb):
                for i in range(2):
                    for o in range(4):
                        slot(2 * tb + i, i, o)
            two_tiles(0)
            with eng.Fori(1, TT // 2 - 1) as tb:
                two_tiles(tb)
            two_tiles(TT // 2 - 1)

        def has_experts(t):
            return not isinstance(t, int) or t >= 2

        def experts_buffers(t):
            return d_spare if isinstance(t, int) and t == TT - 2 else d_own

        def used_before(t):
            if not isinstance(t, int) or t < TT - 2:
                return t
            return 0 if t == TT - 2 else TT - 2

        def before(t, i, o):
            return (t, i, o - 1) if o else (t - 1, 1 - i, 3)

        def value_block(i, j, h):
            rows = slice(h * NL, (h + 1) * NL)
            src = (v_f if j == h else v_swap)[rows, :]

            def heads(a):
                return a.rearrange("p (g h d) -> p g h d", h=2, d=SD)[:, :, h, :]
            return [heads(vz[i][p][rows, j, :]) for p in range(2)], heads(src)

        def own_columns(a):
            return a[:].rearrange("p o j (c n) -> p o (j c) n", c=2)[:, :, 0:4:3, :]

        def batches(a):
            return a[:].rearrange("p (o j n) -> p o j n", o=4, j=2)

        def output_block(o, q):
            rows = slice(32 * q, 32 * q + 32)
            return rows, ps_o[rows, :].rearrange("p (j q n) -> p j q n", j=2, q=4)[:, :, q, :]

        @block.sync
        def _(sp):
            for i, (dst, src) in enumerate(((cos, "cos"), (sin, "sin"), (bmask, "bmask"), (cmask_f, "cmask"))):
                if i == 3:
                    c_load_w(sp, env, 2)
                sp.dma_start(dst[:], env[src]).then_inc(table_in[i], 16)
            c_load_w(sp, env, 3)
            sp.dma_start(rbias[:], env["router_bias"].unsqueeze(0).broadcast_to([P, E])).then_inc(table_in[4], 16)

            def swap(t):
                sp.wait_ge(v_out, t + 1)
                wait_pos(sp, vz_low, t)
                for h in range(2):
                    sp.dma_start(v_swap[h * NL:(h + 1) * NL, :], v_f[(1 - h) * NL:(2 - h) * NL, :])\
                        .then_inc(v_swapped, 16)
            def store(t):
                sp.wait_ge(y_ready, t + 1)
                d = experts_buffers(t)
                sp.dma_start(env["out"][bass.ds(t, 1)].rearrange("t p d -> p (t d)"), d["y"])\
                    .then_inc(d["stored"], 16)

            swap(0)
            swap(1)
            sp.wait_ge(w_low, c_weights_split(2))
            sp.dma_start(w_f[0][:, :, 0:E], env["router_wT"].rearrange("(k p) e -> p k e", p=P)).then_inc(w_in[4], 16)
            sp.wait_ge(w_low, c_weights_split(3))
            sp.dma_start(w_f[1][0:E, 0, :], env["expert_bias"]).then_inc(w_in[5], 16)
            swap(2)
            with sp.Fori(3, TT) as t:
                swap(t)
                store(t - 3)
            for t in range(TT - 3, TT):
                store(t)
            sp.wait_ge(d_own["stored"], 16 * (TT - 1))
            sp.wait_ge(d_spare["stored"], 16)

        @block.gpsimd
        def _(pool):
            def d_inverse_deviation(t):
                wait_apart(pool, d_stats_ready, 2 * t + 2)
                pool.tensor_scalar(d_var[:], d_mv[:, 1:2], EPS, None, ALU.add).then_inc(d_var_ready, 1)
                pool.wait_ge(d_var_ready, t + 1)
                pool.tensor_tensor(d_rstd[:], d_var[:], minus_half[:], ALU.pow).then_inc(d_rstd_ready, 1)

            def rotate(t, n, turned, rot):
                pool.wait_ge(turned, t + 1)
                pool.tensor_tensor(rot_a[n][:], rot_a[n][:], rot_b[n][:], ALU.add).then_inc(rot, 1)

            def spread_keys(t, s):
                pool.wait_ge(kT_low, t + 1)
                wait_pos(pool, s_ps, 2 * (2 * t + s - 1))
                for p in range(2):
                    k = kT[p][:, 2 * s:2 * s + 2, :].rearrange("p a (j n) -> p (a j) n", j=2).bitcast(F32)
                    last = pool.tensor_tensor(kblk[s][p][:], k.unsqueeze(2).broadcast_to([P, 4, 4, NL]),
                                              bmask[:].unsqueeze(1).unsqueeze(3).broadcast_to([P, 4, 4, NL]), ALU.mult)
                last.then_inc(kblk_ready, 1)

            def low_values(t, i):
                pool.wait_ge(vz_high, t + 1)
                for h in range(2):
                    if h:
                        pool.wait_ge(kblk_ready, 2 * t + 2)
                        pool.wait_ge(vz_even, t + 1)
                    for j in range(2):
                        dst, src = value_block(i, j, h)
                        last = pool.tensor_tensor(dst[1], src, dst[0].bitcast(F32), ALU.subtract)
                    last.then_inc(vz_low if h else vz_even, 1)
                pool.wait_ge(vz_low, t + 1)

            c_inverse_deviation(pool, env, 1)
            for i in range(2):
                for p in range(2):
                    last = pool.memset(qz[i][p][:].bitcast(F32), 0.0)
            last.then_inc(qz_zeroed, 1)
            pool.wait_ge(table_in[2], 16)
            rotate(0, "k", k_turned, k_rot)
            rotate(0, "q", q_turned, q_rot)
            spread_keys(0, 0)
            spread_keys(0, 1)
            for p in range(2):
                last = pool.memset(vz[1][p][:].bitcast(F32), 0.0)
            last.then_inc(vz_zeroed[1], 1)
            low_values(0, 0)

            def slot(t, i, o):
                if o == 0 and has_experts(t):
                    d_inverse_deviation(t - 2)
                if is_last(t):
                    return
                if o == 0:
                    rotate(t + 1, "k", k_turned, k_rot)
                    if has_two_after(t):
                        c_inverse_deviation(pool, env, t + 2)
                if o == 1:
                    rotate(t + 1, "q", q_turned, q_rot)
                    spread_keys(t + 1, 0)
                if o == 2:
                    spread_keys(t + 1, 1)
                if o == 3:
                    low_values(t + 1, 1 - i)
            run(pool, slot)
            for t in range(TT - 2, TT):
                d_inverse_deviation(t)

        @block.scalar
        def _(act):
            def copy(out, in_):
                return act.activation(out, in_, ACT.Copy)

            def split_w(n):
                act.wait_ge(w_in[n], 16)
                copy(w[names[n]][0][:], w_f[n % 2]).then_inc(w_high, 1)

            def high_k(t):
                act.wait_ge(kT_ps, t + 1)
                wait_pos(act, kblk_ready, 2 * t)
                copy(kT[0][:].rearrange("p k n -> p (k n)"), ps_t[:]).then_inc(kT_high, 1)

            def high_q(t, i):
                act.wait_ge(qT_ps, t + 1)
                wait_pos(act, s_ps, 4 * (t - 1))
                act.activation(own_columns(qz[i][0]), batches(ps_t), ACT.Copy, scale=SCALE).then_inc(qz_high, 1)

            def values_out(t):
                act.wait_ge(vp_ps, t + 1)
                wait_pos(act, vz_low, t)
                copy(v_f[:], ps_p[0][:]).then_inc(v_out, 1)

            def high_values(t, i):
                act.wait_ge(v_swapped, 32 * (t + 1))
                if isinstance(t, int) and t < 2:
                    act.wait_ge(vz_zeroed[i], 1)
                wait_pos(act, o_ps, 4 * (t - 1))
                for j in range(2):
                    for h in range(2):
                        dst, src = value_block(i, j, h)
                        last = copy(dst[0], src)
                last.then_inc(vz_high, 1)

            def exponential(m, b):
                act.wait_ge(max_ready, m + 1)
                wait_pos(act, pT_ps, m - 1)
                for h in range(8):
                    head = slice(h * NL, (h + 1) * NL)
                    last = act.activation(probs[b][:, head], ps_s[b][:, head], ACT.Exp, bias=nmax[:, b, h:h + 1],
                                          accum_out=psum_p[:, b, h:h + 1])
                last.then_inc(exp_done, 1)

            def high_probs(m):
                act.wait_ge(pT_ps, m + 1)
                wait_pos(act, o_ps, m)
                copy(pT[0][:].rearrange("p k n -> p (k n)"), ps_pt[:]).then_inc(pT_high, 1)

            def high_out(t, i, o):
                m = 4 * t + o
                act.wait_ge(o_ps, m + 1)
                if o == 0:
                    wait_pos(act, y_ps, t - 1)
                for q in range(4):
                    rows, src = output_block(o, q)
                    last = copy(oT[0][rows, i, o, :].rearrange("p (j n) -> p j n", j=2), src)
                last.then_inc(oT_high, 1)

            def d_high_x(t):
                d = experts_buffers(t)
                act.wait_ge(d_xT_ps, t + 1)
                wait_pos(act, l_ps, used_before(t))
                copy(d["xT"][0].rearrange("p k n -> p (k n)"), d["bank"][:]).then_inc(d_xT_high, 1)

            def d_exponential(t):
                act.wait_ge(steps, 7 * t + 2)
                act.activation(d_probs[:], logits[:], ACT.Exp, bias=d_nmax[:], accum_out=d_psum[:])\
                    .then_inc(d_exp_done, 1)

            def d_high_w(t):
                d = experts_buffers(t)
                act.wait_ge(wT_ps, t + 1)
                wait_pos(act, d_y_ps, used_before(t))
                copy(d["wT"][0][:], d["bank"][0:E, 0:P]).then_inc(wT_high, 1)

            high_k(0)
            act.wait_ge(table_in[3], 16)
            copy(cmask[:], cmask_f[:])
            copy(ident_r[:], ident[:]).then_inc(tables, 1)
            split_w(2)
            act.wait_ge(qz_zeroed, 1)
            high_q(0, 0)
            c_high_x(act, env, 1, ps_t)
            values_out(0)
            exponential(0, 0)
            high_values(0, 0)
            exponential(1, 1)

            def slot(t, i, o):
                m = 4 * t + o
                more = not is_last(t)
                high_probs(m)
                if o == 1 and has_experts(t):
                    d_high_x(t - 2)
                if o == 3 and has_experts(t):
                    d_high_w(t - 2)
                if o == 3 and is_last(t):
                    d_high_x(t - 1)
                if o == 2 and more:
                    values_out(t + 1)
                if o == 3 and more:
                    high_values(t + 1, 1 - i)
                if not (isinstance(m, int) and m == 0):
                    high_out(*before(t, i, o))
                if o == 1 and more:
                    high_q(t + 1, 1 - i)
                if o == 2 and has_two_after(t):
                    c_high_x(act, env, t + 2, ps_t)
                if o == 2 and has_experts(t):
                    d_exponential(t - 2)
                if more or o < 2:
                    exponential(m + 2, o % 2)
                if o == 0 and more:
                    high_k(t + 1)
                if isinstance(m, int) and m == 2:
                    split_w(3)
                if isinstance(m, int) and m == 5:
                    act.wait_ge(w_in[4], 16)
                    copy(rw[0][:], w_f[0][:, :, 0:E]).then_inc(w_high, 1)
                    act.wait_ge(w_in[5], 16)
                    copy(eb[0][:], w_f[1][0:E, 0, :]).then_inc(w_high, 1)
            run(act, slot)
            high_out(TT - 1, 1, 3)
            d_exponential(TT - 2)
            d_high_w(TT - 2)
            d_high_x(TT - 1)
            d_exponential(TT - 1)
            d_high_w(TT - 1)

        @block.vector
        def _(dve):
            def sub(out, a, b):
                return dve.tensor_tensor(out, a, b.bitcast(F32), ALU.subtract)

            def low_w(n):
                dve.wait_ge(w_high, c_weights_split(n))
                sub(w[names[n]][1][:], w_f[n % 2], w[names[n]][0][:]).then_inc(w_low, 1)

            def flat(a):
                return a[:].rearrange("p k n -> p (k n)")

            def turn(t, n, proj, bank, turned, rot_T):
                dve.wait_ge(proj, t + 1)
                wait_pos(dve, rot_T, t)
                heads = "p (h d) -> p h d"
                dve.tensor_tensor(rot_a[n][:].rearrange(heads, d=SD), bank[:].rearrange(heads, d=SD),
                                  cos[:].unsqueeze(1).broadcast_to([P, D // SD, SD]), ALU.mult)
                pairs = "p (h c e) -> p h c e"
                for e in range(2):
                    last = dve.tensor_tensor(
                        rot_b[n][:].rearrange(pairs, c=SD // 2, e=2)[:, :, :, e],
                        bank[:].rearrange(pairs, c=SD // 2, e=2)[:, :, :, 1 - e],
                        sin[:].rearrange("p (c e) -> p c e", e=2)[:, :, e].unsqueeze(1)
                        .broadcast_to([P, D // SD, SD // 2]), ALU.mult)
                last.then_inc(turned, 1)

            def low_k(t):
                dve.wait_ge(kT_high, t + 1)
                sub(flat(kT[1]), ps_t[:], flat(kT[0])).then_inc(kT_low, 1)

            def low_q(t, i):
                dve.wait_ge(qz_high, t + 1)
                for o in range(4):
                    last = dve.scalar_tensor_tensor(own_columns(qz[i][1])[:, o], batches(ps_t)[:, o], SCALE,
                                                    own_columns(qz[i][0])[:, o].bitcast(F32), ALU.mult, ALU.subtract)
                last.then_inc(qz_low, 1)

            def per_head(a, b):
                return a[:, b, :].unsqueeze(2).broadcast_to([P, 8, NL])

            def heads(a):
                return a[:].rearrange("p (h n) -> p h n", h=8)

            def row_max(m, b):
                dve.wait_ge(s_ps, m + 1)
                dve.tensor_reduce(nmax[:, b, :], heads(ps_s[b]), AX.X, ALU.max, negate=True).then_inc(max_ready, 1)

            def divide_by_sum(m, b):
                dve.wait_ge(exp_done, m + 1)
                dve.reciprocal(rsum[:, b, :], psum_p[:, b, :]).then_inc(rsum_ready, 1)
                dve.wait_ge(rsum_ready, m + 1)
                dve.tensor_tensor(heads(probs[b]), heads(probs[b]), per_head(rsum, b), ALU.mult)\
                    .then_inc(probs_ready, 1)

            def low_probs(m):
                dve.wait_ge(pT_high, m + 1)
                sub(flat(pT[1]), ps_pt[:], flat(pT[0])).then_inc(pT_low, 1)

            def low_out(t, i, o):
                m = 4 * t + o
                dve.wait_ge(oT_high, m + 1)
                for q in range(4):
                    rows, src = output_block(o, q)
                    dst = [oT[p][rows, i, o, :].rearrange("p (j n) -> p j n", j=2) for p in range(2)]
                    last = sub(dst[1], src, dst[0])
                last.then_inc(oT_low, 1)

            def add_output(t):
                dve.wait_ge(y_ps, t + 1)
                dve.tensor_tensor(tile(t), ps_p[1][:], tile(t), ALU.add).then_inc(x_added, 1)

            def d_statistics(t):
                wait_apart(dve, x_added, t + 1)
                dve.bn_stats(d_stats[:], tile(t)).then_inc(d_stats_ready, 1)
                wait_apart(dve, d_stats_ready, 2 * t + 1)
                dve.bn_aggr(d_mv[:], d_stats[:]).then_inc(d_stats_ready, 1)

            def d_normalised(t):
                dve.wait_ge(d_rstd_ready, t + 1)
                dve.tensor_scalar(experts_buffers(t)["xn"], tile(t), d_mv[:, 0:1], d_rstd[:], ALU.subtract, ALU.mult)\
                    .then_inc(d_xn_ready, 1)

            def d_low_x(t):
                d = experts_buffers(t)
                dve.wait_ge(d_xT_high, t + 1)
                sub(d["xT"][1].rearrange("p k n -> p (k n)"), d["bank"][:], d["xT"][0].rearrange("p k n -> p (k n)"))\
                    .then_inc(d_xT_low, 1)

            def d_logits(t):
                dve.wait_ge(l_ps, t + 1)
                dve.tensor_tensor(logits[:], experts_buffers(t)["bank"][:, 0:E], rbias[:], ALU.add).then_inc(steps, 1)
                dve.wait_ge(steps, 7 * t + 1)
                dve.tensor_reduce(d_nmax[:], logits[:], AX.X, ALU.max, negate=True).then_inc(steps, 1)

            def d_choose(t):
                def step(n, instruction):
                    instruction.then_inc(steps, 1)
                    wait_apart(dve, steps, 7 * t + n)

                dve.wait_ge(d_exp_done, t + 1)
                step(3, dve.reciprocal(d_rsum[:], d_psum[:]))
                step(4, dve.tensor_scalar(d_probs[:], d_probs[:], d_rsum[:], None, ALU.mult))
                step(5, dve.max(top[:], d_probs[:]))
                step(6, dve.match_replace(rest[:], top[:], d_probs[:], 0.0))
                wait_pos(dve, wT_ps, t)
                dve.tensor_tensor(chosen[:], d_probs[:], rest[:], ALU.subtract).then_inc(chosen_ready, 1)
                step(7, dve.tensor_reduce(wsum[:], top[:], AX.X, ALU.add))
                d = experts_buffers(t)
                wait_pos(dve, d["stored"], 16 * used_before(t))
                dve.scalar_tensor_tensor(d["y"], d["xn"], wsum[:], tile(t), ALU.mult, ALU.add).then_inc(y_part, 1)

            def d_low_w(t):
                d = experts_buffers(t)
                dve.wait_ge(wT_high, t + 1)
                sub(d["wT"][1][:], d["bank"][0:E, 0:P], d["wT"][0][:]).then_inc(wT_low, 1)

            def d_add(t):
                d = experts_buffers(t)
                dve.wait_ge(d_y_ps, t + 1)
                dve.wait_ge(y_part, t + 1)
                dve.tensor_tensor(d["y"], d["y"], d["bank"][:], ALU.add).then_inc(y_ready, 1)

            c_statistics(dve, env, 1)
            c_normalised(dve, env, 1)
            for i in range(2):
                dve.wait_ge(table_in[i], 16)
            turn(0, "k", kp_ps, ps_p[0], k_turned, kT_ps)
            dve.memset(vz[0][0][:].bitcast(F32), 0.0)
            turn(0, "q", qp_ps, ps_p[1], q_turned, qT_ps)
            dve.memset(vz[0][1][:].bitcast(F32), 0.0).then_inc(vz_zeroed[0], 1)
            low_k(0)
            low_w(2)
            dve.wait_ge(qz_zeroed, 1)
            low_q(0, 0)
            c_low_x(dve, env, 1, ps_t)
            row_max(0, 0)
            row_max(1, 1)
            divide_by_sum(0, 0)
            turn(1, "k", kp_ps, ps_p[0], k_turned, kT_ps)

            def slot(t, i, o):
                m = 4 * t + o
                more = not is_last(t)
                if o == 1 and more:
                    low_k(t + 1)
                if more or o < 3:
                    divide_by_sum(m + 1, (o + 1) % 2)
                low_probs(m)
                if has_experts(t):
                    if o == 0:
                        d_normalised(t - 2)
                    if o == 1:
                        d_low_x(t - 2)
                    if o == 2:
                        d_logits(t - 2)
                    if o == 3:
                        d_low_w(t - 2)
                if not (isinstance(m, int) and m == 0):
                    low_out(*before(t, i, o))
                if o == (1 if is_last(t) else 3) and not (isinstance(t, int) and t == 0):
                    add_output(t - 1)
                if more or o < 2:
                    row_max(m + 2, o % 2)
                if o == 0 and has_two_after(t):
                    c_statistics(dve, env, t + 2)
                if o == 0 and more:
                    turn(t + 1, "q", qp_ps, ps_p[1], q_turned, qT_ps)
                if o == 1 and more:
                    low_q(t + 1, 1 - i)
                if o == 1 and has_two_after(t):
                    c_normalised(dve, env, t + 2)
                if o == 2 and has_two_after(t):
                    c_low_x(dve, env, t + 2, ps_t)
                if o == 2 and is_last(t):
                    d_normalised(t - 1)
                if o == 2 and has_experts(t):
                    d_choose(t - 2)
                if o == 3 and has_experts(t):
                    d_add(t - 2)
                if o == (1 if is_last(t) else 3) and not (isinstance(t, int) and t == 0):
                    d_statistics(t - 1)
                if o == 3 and is_last(t):
                    d_low_x(t - 1)
                if o == 3 and has_two_after(t):
                    turn(t + 2, "k", kp_ps, ps_p[0], k_turned, kT_ps)
                if isinstance(m, int) and m == 2:
                    low_w(3)
                if isinstance(m, int) and m == 5:
                    dve.wait_ge(w_high, c_weights_split(4))
                    sub(rw[1][:], w_f[0][:, :, 0:E], rw[0][:]).then_inc(w_low, 1)
                    dve.wait_ge(w_high, c_weights_split(5))
                    sub(eb[1][:], w_f[1][0:E, 0, :], eb[0][:]).then_inc(w_low, 1)
                    dve.wait_ge(table_in[4], 16)
            run(dve, slot)
            low_out(TT - 1, 1, 3)
            d_logits(TT - 2)
            d_choose(TT - 2)
            add_output(TT - 1)
            d_statistics(TT - 1)
            d_low_w(TT - 2)
            d_normalised(TT - 1)
            d_add(TT - 2)
            d_low_x(TT - 1)
            d_logits(TT - 1)
            d_choose(TT - 1)
            d_low_w(TT - 1)
            d_add(TT - 1)

        @block.tensor
        def _(pe):
            def turn_tile(src, done):
                for k in range(KT):
                    last = pe.transpose(ps_t[:, k * P:(k + 1) * P], src[:, k * P:(k + 1) * P], ident[:])
                last.then_inc(done, 1)

            def project(n, bank, done):
                ops = [(a, b, k) for a, b in PASSES for k in range(KT)]
                for c, (a, b, k) in enumerate(ops):
                    last = pe.matmul(bank[:], xT[a][:, k, :], w[n][b][:, k, :], start=(c == 0),
                                     stop=(c == len(ops) - 1))
                last.then_inc(done, 1)

            def x_turned(t):
                wait_pos(pe, qz_low, t)
                c_x_turned(pe, env, t, ps_t)

            def k_project(t):
                pe.wait_ge(xT_low, t + 1)
                wait_pos(pe, v_out, t)
                project("k", ps_p[0], kp_ps)

            def q_project(t):
                wait_pos(pe, x_added, t - 2)
                project("q", ps_p[1], qp_ps)

            def v_project(t):
                pe.wait_ge(k_turned, t + 1)
                project("v", ps_p[0], vp_ps)

            def k_turn(t):
                pe.wait_ge(k_rot, t + 1)
                pe.wait_ge(xT_low, t + 1)
                turn_tile(rot_a["k"], kT_ps)

            def q_turn(t):
                pe.wait_ge(q_rot, t + 1)
                pe.wait_ge(kT_low, t + 1)
                turn_tile(rot_a["q"], qT_ps)

            def scores(t, i, o):
                m, s, b = 4 * t + o, o // 2, o % 2
                rows = slice(b * NL, (b + 1) * NL)
                if o % 2 == 0:
                    pe.wait_ge(kblk_ready, 2 * t + s + 1)
                if o == 0:
                    pe.wait_ge(qz_low, t + 1)
                wait_pos(pe, exp_done, m - 1)
                pe.matmul(ps_s[b][:], ident_r[:], cmask[:], start=True, stop=False, skip_group_check=True)
                ops = [(x, j, p, r) for x in range(2) for j in range(2) for p, r in PASSES]
                for c, (x, j, p, r) in enumerate(ops):
                    last = pe.matmul(ps_s[b][:, x * 256:(x + 1) * 256], qz[i][p][rows, 2 * s + x, j, :],
                                     kblk[s][r][rows, 2 * x + j, :, :].rearrange("p h n -> p (h n)"), start=False,
                                     stop=(c == len(ops) - 1), skip_group_check=True)
                last.then_inc(s_ps, 1)

            def probs_turned(m, b):
                pe.wait_ge(probs_ready, m + 1)
                wait_pos(pe, pT_low, m)
                for q in range(4):
                    last = pe.transpose(ps_pt[:, q * P:(q + 1) * P], probs[b][:, q * P:(q + 1) * P], ident[:])
                last.then_inc(pT_ps, 1)

            def outputs(t, i, o):
                m = 4 * t + o
                pe.wait_ge(pT_low, m + 1)
                if o == 0:
                    pe.wait_ge(vz_low, t + 1)
                wait_pos(pe, oT_low, m)
                for j in range(2):
                    for c, (a, b) in enumerate(PASSES):
                        last = pe.matmul(ps_o[:, j * 256:(j + 1) * 256], vz[i][a][:, j, o * P:(o + 1) * P],
                                         pT[b][:, :, j * NL:(j + 1) * NL], start=(c == 0), stop=(c == 2))
                last.then_inc(o_ps, 1)

            def output_product(t, i):
                pe.wait_ge(oT_low, 4 * (t + 1))
                if isinstance(t, int) and t + 3 > TT:
                    pe.wait_ge(x_added, t)
                else:
                    pe.wait_ge(q_turned, t + 3)
                for c, (a, b, k) in enumerate([(a, b, k) for a, b in PASSES for k in range(4)]):
                    last = pe.matmul(ps_p[1][:], oT[a][:, i, k, :], w["o"][b][:, k, :], start=(c == 0), stop=(c == 11))
                last.then_inc(y_ps, 1)

            def d_x_turned(t):
                d = experts_buffers(t)
                pe.wait_ge(d_xn_ready, t + 1)
                wait_pos(pe, y_ready, used_before(t))
                for k in range(KT):
                    last = pe.transpose(d["bank"][:, k * P:(k + 1) * P], d["xn"][:, k * P:(k + 1) * P], ident[:])
                last.then_inc(d_xT_ps, 1)

            def router(t):
                d = experts_buffers(t)
                pe.wait_ge(d_xT_low, t + 1)
                for c, (a, b, k) in enumerate([(a, b, k) for a, b in PASSES for k in range(KT)]):
                    last = pe.matmul(d["bank"][:, 0:E], d["xT"][a][:, k, :], rw[b][:, k, :], start=(c == 0),
                                     stop=(c == 11))
                last.then_inc(l_ps, 1)

            def d_w_turned(t):
                wait_apart(pe, chosen_ready, t + 1)
                pe.transpose(experts_buffers(t)["bank"][0:E, 0:P], chosen[:], ident[:]).then_inc(wT_ps, 1)

            def d_output(t):
                d = experts_buffers(t)
                pe.wait_ge(wT_low, t + 1)
                for c, (a, b) in enumerate(PASSES):
                    last = pe.matmul(d["bank"][:], d["wT"][a][:], eb[b][:], start=(c == 0), stop=(c == 2))
                last.then_inc(d_y_ps, 1)

            pe.wait_ge(w_low, c_weights_split(1))
            k_project(0)
            q_project(0)
            k_turn(0)
            q_turn(0)
            x_turned(1)
            pe.wait_ge(w_low, c_weights_split(2))
            v_project(0)
            pe.wait_ge(tables, 1)
            scores(0, 0, 0)
            scores(0, 0, 1)
            k_project(1)

            def slot(t, i, o):
                more = not is_last(t)
                if o >= 2 and isinstance(t, int) and t == 1:
                    pe.wait_ge(w_low, c_weights_split(3 if o == 2 else 5))
                probs_turned(4 * t + o, o % 2)
                if o == 3 and has_experts(t):
                    d_w_turned(t - 2)
                if o < 2:
                    scores(t, i, o + 2)
                elif more:
                    scores(t + 1, 1 - i, o - 2)
                if o == 0 and more:
                    q_project(t + 1)
                    k_turn(t + 1)
                if o == 1 and more:
                    q_turn(t + 1)
                    v_project(t + 1)
                if o == 2:
                    if has_two_after(t):
                        x_turned(t + 2)
                    if not (isinstance(t, int) and t == 0 or is_last(t)):
                        output_product(t - 1, 1 - i)
                if o == 0 and is_last(t):
                    output_product(t - 1, 1 - i)
                if o == 3 and is_last(t):
                    d_x_turned(t - 1)
                if o == 3 and has_experts(t):
                    d_output(t - 2)
                if o == 3 and has_two_after(t):
                    k_project(t + 2)
                if o == 0 and has_experts(t):
                    d_x_turned(t - 2)
                if o == 1 and has_experts(t):
                    router(t - 2)
                outputs(t, i, o)
            run(pe, slot)
            router(TT - 2)
            output_product(TT - 1, 1)
            d_w_turned(TT - 2)
            d_x_turned(TT - 1)
            d_output(TT - 2)
            router(TT - 1)
            d_w_turned(TT - 1)
            d_output(TT - 1)


def build(nc, **env):
    with ExitStack() as ctx:
        def sb(name, shape, dt=F32):
            return ctx.enter_context(nc.sbuf_tensor(name, shape, dt))

        def sem(name):
            return ctx.enter_context(nc.semaphore(name))

        env["ident"] = sb("ident", [P, P])
        env["minus_half"] = sb("minus_half", [P, 1])
        env["x1"] = sb("x1", [P, TT, D])
        env["kv_stored"] = [sem(f"kv_stored{i}") for i in range(2)]
        env["wq_in"] = [sem(f"wq_in{i}") for i in range(2)]
        env["wq_high"], env["wq_low"] = sem("wq_high"), sem("wq_low")
        env["q_ps"] = sem("q_ps")
        env["xnT"] = [sb(f"xnT_{n}", [P, KT, TT * P], F32R) for n in "hl"]
        env["wq_f"] = sb("wq_f", [P, 2, KT, HD])
        env["wq_split"] = [sb(f"wq_{n}", [P, 2, KT, HD], F32R) for n in "hl"]
        stage_keys_values(nc, env)
        env["q_all"] = sb("q_all", [P, 2, G, TT // 2 * P])
        next_stage_views(env)
        env["c_stats"], env["c_mv"] = sb("c_stats", [P, 6]), sb("c_mv", [P, 2])
        env["c_var"], env["c_rstd"] = sb("c_var", [P, 1]), sb("c_rstd", [P, 1])
        env["c_w_in"] = [sem(f"c_w_in{i}") for i in range(6)]
        env["c_w_high"], env["c_w_low"] = sem("c_w_high"), sem("c_w_low")
        env["c_stats_ready"] = sem("c_stats_ready")
        env["c_var_ready"], env["c_rstd_ready"] = sem("c_var_ready"), sem("c_rstd_ready")
        env["c_xn_ready"] = sem("c_xn_ready")
        env["c_xT_ps"] = sem("c_xT_ps")
        env["c_xT_high"], env["c_xT_low"] = sem("c_xT_high"), sem("c_xT_low")
        env["vp_ps"] = sem("vp_ps")
        stage_cross_attention(nc, env)
        stage_self_attention_and_experts(nc, env)


def kernel(**inputs):
    import concourse.bacc as bacc
    from concourse.bass_utils import run_bass_kernel_spmd

    a = {n: np.asarray(v) for n, v in inputs.items()}
    order = np.arange(D).reshape(2, 2, 2, 4, SD).transpose(0, 2, 1, 3, 4).reshape(-1)
    half = np.arange(P) % NL
    angle = np.outer(half, 1.0 / 10000.0 ** (np.arange(0, SD, 2).astype(np.float32) / SD)).astype(np.float32)
    arrays = dict(
        x=a["x"].reshape(TT, P, D),
        ctxT=a["ctx_4096"].reshape(TT, 2, NC, KT, P).transpose(0, 4, 3, 1, 2).reshape(TT, P, KT * 2 * NC),
        wq=a["L0_xattn_Wq"].reshape(KT, P, HK * G, HD).transpose(2, 1, 0, 3).reshape(HK * G, P, KT * HD),
        wk=a["L0_xattn_Wk"], wv=a["L0_xattn_Wv"], wo=a["L0_xattn_Wo"],
        c_wq=a["L0_attn_wq"], c_wk=a["L0_attn_wk"], c_wv=a["L0_attn_wv"][:, order], c_wo=a["L0_attn_wo"][order],
        router_wT=a["L0_ffn_router_weight"].T, router_bias=a["L0_ffn_router_bias"],
        expert_bias=a["L0_ffn_expert_bias"],
        cos=np.repeat(np.cos(angle), 2, axis=1),
        sin=np.repeat(np.sin(angle), 2, axis=1) * np.tile(np.array([-1, 1], np.float32), SD // 2),
        bmask=(half[:, None] // SD == np.arange(4)).astype(np.float32),
        cmask=np.tile(np.where(half[:, None] >= np.arange(NL), 0, -1e30).astype(np.float32), (1, 8)),
    )
    arrays = {n: np.ascontiguousarray(v) for n, v in arrays.items()}
    nc = bacc.Bacc("TRN2", target_bir_lowering=False, num_devices=1)
    env = {n: nc.dram_tensor(f"in_{n}", v.shape, mybir.dt.from_np(v.dtype), kind="ExternalInput").ap()
           for n, v in arrays.items()}
    env["kv_dram"] = nc.dram_tensor("kv_dram", (TT, P, HK * KV), F32, kind="Internal").ap()
    env["out"] = nc.dram_tensor("out", (TT, P, D), F32, kind="ExternalOutput").ap()
    build(nc, **env)
    r = run_bass_kernel_spmd(nc, [{f"in_{n}": v for n, v in arrays.items()}], core_ids=[0])
    return r.results[0]["out"].reshape(B, NL, D)
```
